# Optimizing a Trainium2 kernel written in Bass

```python
import numpy as np
import jax
import jax.numpy as jnp

def _softmax(x, axis=-1):
    return jax.nn.softmax(x, axis=axis)

def _gelu(x):
    return jax.nn.gelu(x, approximate=True)

def _silu(x):
    return jax.nn.silu(x)

def _sigmoid(x):
    return jax.nn.sigmoid(x)

def _layernorm(x, axis=-1, eps=1e-05):
    m = jnp.mean(x, axis=axis, keepdims=True)
    v = jnp.var(x, axis=axis, keepdims=True)
    return (x - m) / jnp.sqrt(v + eps)

def _scatter_add(tgt, idx, src, axis=0):
    return tgt.at[idx].add(src)

def _segment_sum(src, seg, n):
    return jax.ops.segment_sum(src, seg, n)
kernel_name = 'mk_gnn_ffn_d4_gnn_r16_0d3869'

def setup_inputs(seed: int=0):
    np.random.seed(seed)
    _w = jnp.asarray

    def _rec_inputs():
        import jax
        import jax.numpy as jnp
        _gk = jax.random.key(seed)
        x = -0.000364 + 1 * jax.random.normal(jax.random.fold_in(_gk, 1), (625, 768), jnp.float32)
        _s = jax.random.randint(jax.random.fold_in(_gk, 2), (5000,), 0, 625, jnp.int32)
        _d = jax.random.randint(jax.random.fold_in(_gk, 3), (5000,), 0, 625, jnp.int32)
        _loop = jnp.arange(625, dtype=jnp.int32)
        src = jnp.concatenate([_s, _d, _loop])
        dst = jnp.concatenate([_d, _s, _loop])
        _o = jnp.argsort(dst, stable=True)
        src = src[_o]
        dst = dst[_o]
        return (x, src, dst)
    x, src, dst = _rec_inputs()

    def _L0_gnn_setup():
        import jax, jax.numpy as jnp
        import numpy as np
        N = 1250
        DEG = 16
        E = N * DEG
        H = 12
        DIN = 64
        DOUT = 64
        NEG_SLOPE = 0.2
        key = jax.random.key(seed)
        k_h, k_src, k_w, k_al, k_ar, k_wr = jax.random.split(key, 6)
        std = 1.414 * np.sqrt(2.0 / (DIN + DOUT))
        h = jax.random.normal(k_h, (N, H * DIN), dtype=jnp.float32)
        src = jax.random.randint(k_src, (E,), 0, N, dtype=jnp.int64)
        dst = jnp.repeat(jnp.arange(N, dtype=jnp.int64), DEG)
        W = jax.random.normal(k_w, (DOUT, DIN), dtype=jnp.float32) * std
        attn_l = jax.random.normal(k_al, (1, H, DOUT), dtype=jnp.float32) * std
        attn_r = jax.random.normal(k_ar, (1, H, DOUT), dtype=jnp.float32) * std
        W_res = jax.random.normal(k_wr, (DOUT, DIN), dtype=jnp.float32) * std
        return {'h': h, 'src': src, 'dst': dst, 'W': W, 'attn_l': attn_l, 'attn_r': attn_r, 'W_res': W_res}
    _L0_gnn_all = _L0_gnn_setup()
    _L0_gnn_in = {k: v for k, v in _L0_gnn_all.items() if k in ('W', 'attn_l', 'attn_r', 'W_res')}
    del _L0_gnn_all

    def _L0_ffn_setup():
        import jax, jax.numpy as jnp
        import numpy as np
        NUM_EXPERTS = 8
        TOP_K = 2
        CAP_FACTOR = 1.0
        D_MODEL = 768
        D_FF = 192
        key = jax.random.key(seed)
        k0, k1, k2, k3 = jax.random.split(key, 4)
        B, S, D = (1, 128, D_MODEL)
        inputs = jax.random.normal(k0, (B, S, D), dtype=jnp.float32)
        router_w = jax.random.normal(k1, (NUM_EXPERTS, D), dtype=jnp.float32) * D ** (-0.5)
        w1 = jax.random.normal(k2, (NUM_EXPERTS, D, D_FF), dtype=jnp.float32) * D ** (-0.5)
        w2 = jax.random.normal(k3, (NUM_EXPERTS, D_FF, D), dtype=jnp.float32) * D_FF ** (-0.5)
        return {'inputs': inputs, 'router_w': router_w, 'w1': w1, 'w2': w2}
    _L0_ffn_all = _L0_ffn_setup()
    _L0_ffn_in = {k: v for k, v in _L0_ffn_all.items() if k in ('router_w', 'w1', 'w2')}
    del _L0_ffn_all

    def _L1_gnn_setup():
        import jax, jax.numpy as jnp
        import numpy as np
        N_NODES = 625
        key = jax.random.key(seed)
        k1, k2, k3 = jax.random.split(key, 3)
        x = jax.random.normal(k1, (N_NODES, 768), dtype=jnp.float32)
        edge_index = jax.random.randint(k2, (2, 6250), 0, N_NODES, dtype=jnp.int32)
        W = jax.random.normal(k3, (768, 768), dtype=jnp.float32) * (1.0 / np.sqrt(768))
        b = jnp.zeros((768,), dtype=jnp.float32)
        return {'x': x, 'edge_index': edge_index, 'W': W, 'b': b}
    _L1_gnn_all = _L1_gnn_setup()
    _L1_gnn_in = {k: v for k, v in _L1_gnn_all.items() if k in ('W', 'b')}
    del _L1_gnn_all

    def _L1_ffn_setup():
        import jax, jax.numpy as jnp
        import numpy as np
        B, N, D, H, E, HID, TOPK = (8, 197, 768, 12, 8, 192, 2)

        def _layernorm(x, w, b, eps=1e-05):
            mu = jnp.mean(x, axis=-1, keepdims=True)
            var = jnp.mean((x - mu) ** 2, axis=-1, keepdims=True)
            return (x - mu) * jax.lax.rsqrt(var + eps) * w + b
        key = jax.random.key(seed)
        ks = jax.random.split(key, 8)
        s = 0.02
        return {'x': jax.random.normal(ks[0], (B, N, D), jnp.float32), 'norm1_w': jnp.ones((D,), jnp.float32), 'norm1_b': jnp.zeros((D,), jnp.float32), 'qkv_w': jax.random.normal(ks[1], (3 * D, D), jnp.float32) * s, 'qkv_b': jnp.zeros((3 * D,), jnp.float32), 'proj_w': jax.random.normal(ks[2], (D, D), jnp.float32) * s, 'proj_b': jnp.zeros((D,), jnp.float32), 'norm2_w': jnp.ones((D,), jnp.float32), 'norm2_b': jnp.zeros((D,), jnp.float32), 'w_gate': jax.random.normal(ks[3], (D, E), jnp.float32) * s, 'W1': jax.random.normal(ks[4], (E, D, HID), jnp.float32) * s, 'b1': jnp.zeros((E, HID), jnp.float32), 'W2': jax.random.normal(ks[5], (E, HID, D), jnp.float32) * s, 'b2': jnp.zeros((E, D), jnp.float32)}
    _L1_ffn_all = _L1_ffn_setup()
    _L1_ffn_in = {k: v for k, v in _L1_ffn_all.items() if k in ('norm1_w', 'norm1_b', 'qkv_w', 'qkv_b', 'proj_w', 'proj_b', 'norm2_w', 'norm2_b', 'w_gate', 'W1', 'b1', 'W2', 'b2')}
    del _L1_ffn_all

    def _L2_gnn_setup():
        import jax, jax.numpy as jnp
        import numpy as np
        N_NODES = 625
        D = 768
        N_EDGES = 10000

        def gcn_conv(x, W, b, src, dst, n_nodes):
            h = x @ W
            deg = jax.ops.segment_sum(jnp.ones_like(dst, dtype=h.dtype), dst, num_segments=n_nodes)
            dinv = jnp.where(deg > 0, jax.lax.rsqrt(deg), 0.0)
            norm = dinv[src] * dinv[dst]
            msgs = h[src] * norm[:, None]
            out = jax.ops.segment_sum(msgs, dst, num_segments=n_nodes)
            return out + b

        def add_self_loops(edge_index, n_nodes):
            loop = jnp.arange(n_nodes, dtype=edge_index.dtype)
            src = jnp.concatenate([edge_index[0], loop])
            dst = jnp.concatenate([edge_index[1], loop])
            return (src, dst)
        key = jax.random.key(seed)
        k1, k2, k3, k4 = jax.random.split(key, 4)
        x = jax.random.normal(k1, (N_NODES, D), dtype=jnp.float32)
        edge_index = jax.random.randint(k2, (2, N_EDGES), 0, N_NODES, dtype=jnp.int32)
        glorot = float(np.sqrt(6.0 / (D + D)))
        W1 = jax.random.uniform(k3, (D, D), jnp.float32, -glorot, glorot)
        W2 = jax.random.uniform(k4, (D, D), jnp.float32, -glorot, glorot)
        b1 = jnp.zeros((D,), jnp.float32)
        b2 = jnp.zeros((D,), jnp.float32)
        return {'x': x, 'W1': W1, 'b1': b1, 'W2': W2, 'b2': b2, 'edge_index': edge_index}
    _L2_gnn_all = _L2_gnn_setup()
    _L2_gnn_in = {k: v for k, v in _L2_gnn_all.items() if k in ('W1', 'b1', 'W2', 'b2')}
    del _L2_gnn_all

    def _L2_ffn_setup():
        import jax, jax.numpy as jnp
        import numpy as np
        key = jax.random.key(seed)
        ks = jax.random.split(key, 6)
        B, N, D, E, S, H = (4, 256, 768, 4, 1024, 192)
        sc = lambda d: 1.0 / np.sqrt(d)
        return {'x': jax.random.normal(ks[0], (B, N, D), dtype=jnp.float32), 'phi': jax.random.normal(ks[1], (E, S, D), dtype=jnp.float32) * sc(D), 'w1': jax.random.normal(ks[2], (E, D, H), dtype=jnp.float32) * sc(D), 'b1': jnp.zeros((E, H), dtype=jnp.float32), 'w2': jax.random.normal(ks[3], (E, H, D), dtype=jnp.float32) * sc(H), 'b2': jnp.zeros((E, D), dtype=jnp.float32)}
    _L2_ffn_all = _L2_ffn_setup()
    _L2_ffn_in = {k: v for k, v in _L2_ffn_all.items() if k in ('phi', 'w1', 'b1', 'w2', 'b2')}
    del _L2_ffn_all

    def _L3_gnn_setup():
        import jax, jax.numpy as jnp
        import numpy as np
        N_NODES = 625
        N_EDGES = 5000
        IN_DIM, HID, OUT_DIM, HEADS = (768, 512, 768, 4)
        NEG_SLOPE = 0.2

        def _gat_layer(x, src, dst, W, a_src, a_dst, b, heads, d_out, concat):
            N = x.shape[0]
            h = (x @ W).reshape(N, heads, d_out)
            as_n = jnp.einsum('nhd,hd->nh', h, a_src)
            ad_n = jnp.einsum('nhd,hd->nh', h, a_dst)
            e = jax.nn.leaky_relu(as_n[src] + ad_n[dst], NEG_SLOPE)
            e_max = jax.lax.stop_gradient(jax.ops.segment_max(e, dst, num_segments=N))
            ex = jnp.exp(e - e_max[dst])
            denom = jax.ops.segment_sum(ex, dst, num_segments=N)
            alpha = ex / (denom[dst] + 1e-16)
            msg = alpha[:, :, None] * h[src]
            out = jax.ops.segment_sum(msg, dst, num_segments=N)
            out = out.reshape(N, heads * d_out) if concat else out.mean(axis=1)
            return out + b
        key = jax.random.key(seed)
        ks = jax.random.split(key, 10)
        g = 0.05
        return {'x': jax.random.normal(ks[0], (N_NODES, IN_DIM), jnp.float32), 'edge_index': jax.random.randint(ks[1], (2, N_EDGES), 0, N_NODES, jnp.int64), 'W1': jax.random.normal(ks[2], (IN_DIM, HEADS * HID), jnp.float32) * g, 'a1_src': jax.random.normal(ks[3], (HEADS, HID), jnp.float32) * g, 'a1_dst': jax.random.normal(ks[4], (HEADS, HID), jnp.float32) * g, 'b1': jnp.zeros((HEADS * HID,), jnp.float32), 'W2': jax.random.normal(ks[5], (HEADS * HID, OUT_DIM), jnp.float32) * g, 'a2_src': jax.random.normal(ks[6], (1, OUT_DIM), jnp.float32) * g, 'a2_dst': jax.random.normal(ks[7], (1, OUT_DIM), jnp.float32) * g, 'b2': jnp.zeros((OUT_DIM,), jnp.float32)}
    _L3_gnn_all = _L3_gnn_setup()
    _L3_gnn_in = {k: v for k, v in _L3_gnn_all.items() if k in ('W1', 'a1_src', 'a1_dst', 'b1', 'W2', 'a2_src', 'a2_dst', 'b2')}
    del _L3_gnn_all

    def _L3_ffn_setup():
        import jax, jax.numpy as jnp
        import numpy as np
        TOP_K = 2
        key = jax.random.key(seed)
        k1, k2, k3, k4 = jax.random.split(key, 4)
        B, S, H, I, E = (8, 128, 768, 192, 8)
        x = jax.random.normal(k1, (B, S, H), dtype=jnp.float32)
        router_w = jax.random.uniform(k2, (E, H), dtype=jnp.float32, minval=-1.0, maxval=1.0) * (1.0 / np.sqrt(H))
        up_w = jax.random.uniform(k3, (E, H, I), dtype=jnp.float32, minval=-1.0, maxval=1.0) * (1.0 / np.sqrt(H))
        down_w = jax.random.uniform(k4, (E, I, H), dtype=jnp.float32, minval=-1.0, maxval=1.0) * (1.0 / np.sqrt(I))
        return {'x': x, 'router_w': router_w, 'up_w': up_w, 'down_w': down_w}
    _L3_ffn_all = _L3_ffn_setup()
    _L3_ffn_in = {k: v for k, v in _L3_ffn_all.items() if k in ('router_w', 'up_w', 'down_w')}
    del _L3_ffn_all
    return {'x': x, 'src': src, 'dst': dst, 'L0_gnn_W': _L0_gnn_in['W'], 'L0_gnn_attn_l': _L0_gnn_in['attn_l'], 'L0_gnn_attn_r': _L0_gnn_in['attn_r'], 'L0_gnn_W_res': _L0_gnn_in['W_res'], 'L0_ffn_router_w': _L0_ffn_in['router_w'], 'L0_ffn_w1': _L0_ffn_in['w1'], 'L0_ffn_w2': _L0_ffn_in['w2'], 'L1_gnn_W': _L1_gnn_in['W'], 'L1_gnn_b': _L1_gnn_in['b'], 'L1_ffn_norm1_w': _L1_ffn_in['norm1_w'], 'L1_ffn_norm1_b': _L1_ffn_in['norm1_b'], 'L1_ffn_qkv_w': _L1_ffn_in['qkv_w'], 'L1_ffn_qkv_b': _L1_ffn_in['qkv_b'], 'L1_ffn_proj_w': _L1_ffn_in['proj_w'], 'L1_ffn_proj_b': _L1_ffn_in['proj_b'], 'L1_ffn_norm2_w': _L1_ffn_in['norm2_w'], 'L1_ffn_norm2_b': _L1_ffn_in['norm2_b'], 'L1_ffn_w_gate': _L1_ffn_in['w_gate'], 'L1_ffn_W1': _L1_ffn_in['W1'], 'L1_ffn_b1': _L1_ffn_in['b1'], 'L1_ffn_W2': _L1_ffn_in['W2'], 'L1_ffn_b2': _L1_ffn_in['b2'], 'L2_gnn_W1': _L2_gnn_in['W1'], 'L2_gnn_b1': _L2_gnn_in['b1'], 'L2_gnn_W2': _L2_gnn_in['W2'], 'L2_gnn_b2': _L2_gnn_in['b2'], 'L2_ffn_phi': _L2_ffn_in['phi'], 'L2_ffn_w1': _L2_ffn_in['w1'], 'L2_ffn_b1': _L2_ffn_in['b1'], 'L2_ffn_w2': _L2_ffn_in['w2'], 'L2_ffn_b2': _L2_ffn_in['b2'], 'L3_gnn_W1': _L3_gnn_in['W1'], 'L3_gnn_a1_src': _L3_gnn_in['a1_src'], 'L3_gnn_a1_dst': _L3_gnn_in['a1_dst'], 'L3_gnn_b1': _L3_gnn_in['b1'], 'L3_gnn_W2': _L3_gnn_in['W2'], 'L3_gnn_a2_src': _L3_gnn_in['a2_src'], 'L3_gnn_a2_dst': _L3_gnn_in['a2_dst'], 'L3_gnn_b2': _L3_gnn_in['b2'], 'L3_ffn_router_w': _L3_ffn_in['router_w'], 'L3_ffn_up_w': _L3_ffn_in['up_w'], 'L3_ffn_down_w': _L3_ffn_in['down_w']}

def reference(x, src, dst, L0_gnn_W, L0_gnn_attn_l, L0_gnn_attn_r, L0_gnn_W_res, L0_ffn_router_w, L0_ffn_w1, L0_ffn_w2, L1_gnn_W, L1_gnn_b, L1_ffn_norm1_w, L1_ffn_norm1_b, L1_ffn_qkv_w, L1_ffn_qkv_b, L1_ffn_proj_w, L1_ffn_proj_b, L1_ffn_norm2_w, L1_ffn_norm2_b, L1_ffn_w_gate, L1_ffn_W1, L1_ffn_b1, L1_ffn_W2, L1_ffn_b2, L2_gnn_W1, L2_gnn_b1, L2_gnn_W2, L2_gnn_b2, L2_ffn_phi, L2_ffn_w1, L2_ffn_b1, L2_ffn_w2, L2_ffn_b2, L3_gnn_W1, L3_gnn_a1_src, L3_gnn_a1_dst, L3_gnn_b1, L3_gnn_W2, L3_gnn_a2_src, L3_gnn_a2_dst, L3_gnn_b2, L3_ffn_router_w, L3_ffn_up_w, L3_ffn_down_w):
    import jax
    import jax.numpy as jnp

    def _L0_gnn_ref(h, src, dst, W, attn_l, attn_r, W_res):
        import jax, jax.numpy as jnp
        import numpy as np
        N = 1250
        DEG = 16
        E = N * DEG
        H = 12
        DIN = 64
        DOUT = 64
        NEG_SLOPE = 0.2
        n = h.shape[0]
        hv = h.reshape(n, H, DIN)
        ft = jnp.einsum('nhd,od->nho', hv, W)
        a1 = jnp.sum(ft * attn_l, axis=-1)
        a2 = jnp.sum(ft * attn_r, axis=-1)
        e = jax.nn.leaky_relu(a1[src] + a2[dst], negative_slope=NEG_SLOPE)
        m = jax.ops.segment_max(e, dst, num_segments=n)
        m = jnp.where(jnp.isfinite(m), m, 0.0)
        w = jnp.exp(e - m[dst])
        denom = jax.ops.segment_sum(w, dst, num_segments=n)
        alpha = w / jnp.maximum(denom[dst], 1e-16)
        msg = alpha[:, :, None] * ft[src]
        agg = jax.ops.segment_sum(msg, dst, num_segments=n)
        res = jnp.einsum('nhd,od->nho', hv, W_res)
        out = jax.nn.relu((agg + res).reshape(n, H * DOUT))
        return out

    def _L0_ffn_ref(inputs, router_w, w1, w2):
        import jax, jax.numpy as jnp
        import numpy as np
        NUM_EXPERTS = 8
        TOP_K = 2
        CAP_FACTOR = 1.0
        D_MODEL = 768
        D_FF = 192
        B, S, D = inputs.shape
        x = inputs.reshape(-1, D)
        N = x.shape[0]
        logits = x @ router_w.T
        probs = jax.nn.softmax(logits.astype(jnp.float32), axis=-1)
        weights, sel = jax.lax.top_k(probs, TOP_K)
        cap = int(CAP_FACTOR * N * TOP_K) + 1
        n_real = N * TOP_K
        expert_flat = sel.reshape(-1)
        weight_flat = weights.reshape(-1)
        token_idx = jnp.repeat(jnp.arange(N), TOP_K)
        pad = cap - n_real
        expert_flat = jnp.pad(expert_flat, (0, pad))
        weight_flat = jnp.pad(weight_flat, (0, pad))
        token_idx = jnp.pad(token_idx, (0, pad))
        valid = jnp.arange(cap) < n_real
        toks = x[token_idx]

        def mlp(w1e, w2e):
            return jax.nn.gelu(toks @ w1e) @ w2e
        ys = jax.vmap(mlp)(w1, w2)
        gate = (weight_flat * valid.astype(weight_flat.dtype)).astype(toks.dtype)
        res = ys[expert_flat, jnp.arange(cap)] * gate[:, None]
        out = jnp.zeros((N, D), dtype=inputs.dtype).at[token_idx].add(res)
        return out.reshape(B, S, D)

    def _L1_gnn_ref(x, edge_index, W, b):
        import jax, jax.numpy as jnp
        import numpy as np
        N_NODES = 625
        n = x.shape[0]
        loops = jnp.arange(n, dtype=edge_index.dtype)
        row = jnp.concatenate([edge_index[0], loops])
        col = jnp.concatenate([edge_index[1], loops])
        ones = jnp.ones(row.shape[0], dtype=x.dtype)
        deg = jax.ops.segment_sum(ones, col, num_segments=n)
        dinv = jnp.where(deg > 0, jax.lax.rsqrt(deg), 0.0)
        norm = dinv[row] * dinv[col]
        h = x @ W
        msg = h[row] * norm[:, None]
        out = jax.ops.segment_sum(msg, col, num_segments=n) + b
        return out

    def _L1_ffn_ref(x, norm1_w, norm1_b, qkv_w, qkv_b, proj_w, proj_b, norm2_w, norm2_b, w_gate, W1, b1, W2, b2):
        import jax, jax.numpy as jnp
        import numpy as np
        B, N, D, H, E, HID, TOPK = (8, 197, 768, 12, 8, 192, 2)

        def _layernorm(x, w, b, eps=1e-05):
            mu = jnp.mean(x, axis=-1, keepdims=True)
            var = jnp.mean((x - mu) ** 2, axis=-1, keepdims=True)
            return (x - mu) * jax.lax.rsqrt(var + eps) * w + b
        Bx, Nx, C = x.shape
        hd = C // H
        scale = hd ** (-0.5)
        xn = _layernorm(x, norm1_w, norm1_b)
        qkv = (xn @ qkv_w.T + qkv_b).reshape(Bx, Nx, 3, H, hd).transpose(2, 0, 3, 1, 4)
        q, k, v = (qkv[0], qkv[1], qkv[2])
        attn = jax.nn.softmax(jnp.einsum('bhqd,bhkd->bhqk', q, k) * scale, axis=-1)
        o = jnp.einsum('bhqk,bhkd->bqhd', attn, v).reshape(Bx, Nx, C)
        x = x + (o @ proj_w.T + proj_b)
        xn2 = _layernorm(x, norm2_w, norm2_b).reshape(-1, C)
        T = xn2.shape[0]
        logits = xn2 @ w_gate
        top_vals, top_idx = jax.lax.top_k(logits, TOPK)
        gates = jax.nn.softmax(top_vals, axis=-1)
        gates_full = jnp.zeros((T, E), xn2.dtype).at[jnp.arange(T)[:, None], top_idx].add(gates)

        def body(acc, p):
            w1, bb1, w2, bb2, g = p
            h = jax.nn.gelu(xn2 @ w1 + bb1, approximate=False)
            return (acc + g[:, None] * (h @ w2 + bb2), None)
        moe_out, _ = jax.lax.scan(body, jnp.zeros_like(xn2), (W1, b1, W2, b2, gates_full.T))
        return x + moe_out.reshape(Bx, Nx, C)

    def _L2_gnn_ref(x, W1, b1, W2, b2, edge_index):
        import jax, jax.numpy as jnp
        import numpy as np
        N_NODES = 625
        D = 768
        N_EDGES = 10000

        def gcn_conv(x, W, b, src, dst, n_nodes):
            h = x @ W
            deg = jax.ops.segment_sum(jnp.ones_like(dst, dtype=h.dtype), dst, num_segments=n_nodes)
            dinv = jnp.where(deg > 0, jax.lax.rsqrt(deg), 0.0)
            norm = dinv[src] * dinv[dst]
            msgs = h[src] * norm[:, None]
            out = jax.ops.segment_sum(msgs, dst, num_segments=n_nodes)
            return out + b

        def add_self_loops(edge_index, n_nodes):
            loop = jnp.arange(n_nodes, dtype=edge_index.dtype)
            src = jnp.concatenate([edge_index[0], loop])
            dst = jnp.concatenate([edge_index[1], loop])
            return (src, dst)
        n = x.shape[0]
        src, dst = add_self_loops(edge_index, n)
        h = gcn_conv(x, W1, b1, src, dst, n)
        h = jax.nn.relu(h)
        out = gcn_conv(h, W2, b2, src, dst, n)
        return out

    def _L2_ffn_ref(x, phi, w1, b1, w2, b2):
        import jax, jax.numpy as jnp
        import numpy as np
        logits = jnp.einsum('bnd,esd->bnes', x, phi)
        B, N, E, S = logits.shape
        dispatch = jax.nn.softmax(logits, axis=1)
        combine = jax.nn.softmax(logits.reshape(B, N, E * S), axis=-1).reshape(B, N, E, S)
        slots = jnp.einsum('bnd,bnes->besd', x, dispatch)
        h = jax.nn.gelu(jnp.einsum('besd,edh->besh', slots, w1) + b1[None, :, None, :])
        y = jnp.einsum('besh,ehd->besd', h, w2) + b2[None, :, None, :]
        out = jnp.einsum('besd,bnes->bnd', y, combine)
        return out

    def _L3_gnn_ref(x, edge_index, W1, a1_src, a1_dst, b1, W2, a2_src, a2_dst, b2):
        import jax, jax.numpy as jnp
        import numpy as np
        N_NODES = 625
        N_EDGES = 5000
        IN_DIM, HID, OUT_DIM, HEADS = (768, 512, 768, 4)
        NEG_SLOPE = 0.2

        def _gat_layer(x, src, dst, W, a_src, a_dst, b, heads, d_out, concat):
            N = x.shape[0]
            h = (x @ W).reshape(N, heads, d_out)
            as_n = jnp.einsum('nhd,hd->nh', h, a_src)
            ad_n = jnp.einsum('nhd,hd->nh', h, a_dst)
            e = jax.nn.leaky_relu(as_n[src] + ad_n[dst], NEG_SLOPE)
            e_max = jax.lax.stop_gradient(jax.ops.segment_max(e, dst, num_segments=N))
            ex = jnp.exp(e - e_max[dst])
            denom = jax.ops.segment_sum(ex, dst, num_segments=N)
            alpha = ex / (denom[dst] + 1e-16)
            msg = alpha[:, :, None] * h[src]
            out = jax.ops.segment_sum(msg, dst, num_segments=N)
            out = out.reshape(N, heads * d_out) if concat else out.mean(axis=1)
            return out + b
        N = x.shape[0]
        loops = jnp.arange(N, dtype=edge_index.dtype)
        src = jnp.concatenate([edge_index[0], loops])
        dst = jnp.concatenate([edge_index[1], loops])
        h = _gat_layer(x, src, dst, W1, a1_src, a1_dst, b1, HEADS, HID, True)
        h = jax.nn.elu(h)
        out = _gat_layer(h, src, dst, W2, a2_src, a2_dst, b2, 1, OUT_DIM, False)
        return out

    def _L3_ffn_ref(x, router_w, up_w, down_w):
        import jax, jax.numpy as jnp
        import numpy as np
        TOP_K = 2
        B, S, H = x.shape
        E = up_w.shape[0]
        T = B * S
        xf = x.reshape(T, H)
        logits = xf @ router_w.T
        probs = jax.nn.softmax(logits, axis=-1)
        top_w, top_i = jax.lax.top_k(probs, TOP_K)
        top_w = top_w / jnp.sum(top_w, axis=-1, keepdims=True)
        gate = jnp.zeros((T, E), dtype=xf.dtype).at[jnp.arange(T)[:, None], top_i].add(top_w)
        out = jnp.zeros_like(xf)
        for e in range(E):
            h = jax.nn.gelu(xf @ up_w[e], approximate=False)
            out = out + gate[:, e:e + 1] * (h @ down_w[e])
        return out.reshape(B, S, H)
    edge_index = jnp.stack([src, dst])
    x = x + _L0_gnn_ref(_layernorm(x, axis=-1), src, dst, L0_gnn_W, L0_gnn_attn_l, L0_gnn_attn_r, L0_gnn_W_res)
    x = x + _L0_ffn_ref(_layernorm(x, axis=-1)[None], L0_ffn_router_w, L0_ffn_w1, L0_ffn_w2)[0]
    x = x + _L1_gnn_ref(_layernorm(x, axis=-1), edge_index, L1_gnn_W, L1_gnn_b)
    x = x + _L1_ffn_ref(_layernorm(x, axis=-1)[None], L1_ffn_norm1_w, L1_ffn_norm1_b, L1_ffn_qkv_w, L1_ffn_qkv_b, L1_ffn_proj_w, L1_ffn_proj_b, L1_ffn_norm2_w, L1_ffn_norm2_b, L1_ffn_w_gate, L1_ffn_W1, L1_ffn_b1, L1_ffn_W2, L1_ffn_b2)[0]
    x = x + _L2_gnn_ref(_layernorm(x, axis=-1), L2_gnn_W1, L2_gnn_b1, L2_gnn_W2, L2_gnn_b2, edge_index)
    x = x + _L2_ffn_ref(_layernorm(x, axis=-1)[None], L2_ffn_phi, L2_ffn_w1, L2_ffn_b1, L2_ffn_w2, L2_ffn_b2)[0]
    x = x + _L3_gnn_ref(_layernorm(x, axis=-1), edge_index, L3_gnn_W1, L3_gnn_a1_src, L3_gnn_a1_dst, L3_gnn_b1, L3_gnn_W2, L3_gnn_a2_src, L3_gnn_a2_dst, L3_gnn_b2)
    x = x + _L3_ffn_ref(_layernorm(x, axis=-1)[None], L3_ffn_router_w, L3_ffn_up_w, L3_ffn_down_w)[0]
    return x

_drawn_inputs = setup_inputs


def setup_inputs(seed=0):
    import zlib

    import numpy as np

    out = dict(_drawn_inputs(seed))
    spreads = {'L1_gnn_b': (0.0, 0.1),
     'L1_ffn_norm1_w': (1.0, 0.6),
     'L1_ffn_norm1_b': (0.0, 0.406),
     'L1_ffn_qkv_b': (0.0, 0.1),
     'L1_ffn_proj_b': (0.0, 0.1),
     'L1_ffn_norm2_w': (1.0, 0.6),
     'L1_ffn_norm2_b': (0.0, 0.742),
     'L1_ffn_b1': (0.0, 0.8),
     'L1_ffn_b2': (0.0, 0.1),
     'L2_gnn_b1': (0.0, 0.273),
     'L2_gnn_b2': (0.0, 0.1),
     'L2_ffn_b1': (0.0, 0.1),
     'L2_ffn_b2': (0.0, 0.1),
     'L3_gnn_b1': (0.0, 0.1),
     'L3_gnn_b2': (0.0, 0.1)}
    factors = {'L3_gnn_a2_dst': 4.937}
    for name, (base, spread) in spreads.items():
        noise = np.random.default_rng([zlib.crc32(name.encode()), seed]).standard_normal(out[name].shape)
        drawn = base * np.exp(spread * noise) if base else spread * noise
        out[name] = jnp.asarray(drawn.astype(out[name].dtype))
    for name, factor in factors.items():
        out[name] = (out[name] * factor).astype(out[name].dtype)
    return out
```

```python
from contextlib import ExitStack, contextmanager

import concourse.bass as bass
from concourse import mybir

F32 = mybir.dt.float32
F16 = mybir.dt.float16
BF16 = mybir.dt.bfloat16
I32 = mybir.dt.int32
U32 = mybir.dt.uint32
ALU = mybir.AluOpType
ACT = mybir.ActivationFunctionType
AX = mybir.AxisListType

P = 128
N = 625
T = 125
NT = N // T
D = 768
KD = D // P
NP = 626
HALVES = [(0, 312), (312, 313)]
SLOT = 1024
MM = 200
TR = 137
EPS = 1e-5
SLOPE = 0.2
LOW = -1e30


class Own:

    def __init__(self, eng, sem):
        self.eng, self.sem, self.n, self.base = eng, sem, 0, 0

    def sign(self, ins):
        ins.then_inc(self.sem, 1)
        self.n += 1

    def wait(self):
        self.eng.wait_ge(self.sem, self.base + self.n)

    def link(self, ins):
        self.sign(ins)
        self.wait()

    @contextmanager
    def loop(self, count, per):
        before = self.base + self.n
        with self.eng.Fori(0, count) as i:
            self.base, self.n = i * per + before, 0
            yield i
            assert self.n == per, (self.n, per)
        self.base, self.n = before + count * per, 0


class Kit:

    def __init__(self, nc, ctx):
        self.nc, self.ctx, self.stage_no = nc, ctx, 0

    def sb(self, mem, name, shape, dt=F32):
        self.stage_no += 1
        return mem.enter_context(self.nc.sbuf_tensor(f"{name}_{self.stage_no}", shape, dt))

    @contextmanager
    def sems(self, names):
        self.stage_no += 1
        got = [self.nc.alloc_semaphore(f"{n}_{self.stage_no}") for n in names.split()]
        yield got
        self.nc.clear_and_free_semaphores(got)
        self.nc.all_engine_barrier()

    def slot(self, i):
        return self.ps[:, i * SLOT:(i + 1) * SLOT]

    def bank(self, i):
        return self.ps[:, i * 512:(i + 1) * 512]


def cols(t):
    return slice(t * T, (t + 1) * T)


def row_of(vec, parts, n=None):
    return vec.rearrange("(a n) -> a n", a=1).to_broadcast([parts, vec.shape[0]])


def setup(k, x, src, dst):
    nc = k.nc
    E = src.shape[0]
    EC = E // T
    G = 5
    REST = N - 512
    with ExitStack() as mem, k.sems(
            "x_loaded edges_loaded iota_done ident_done const_done own_dve own_pool onehot_ready onehot_used cleared "
            "counted evacuated turned mask_done") as (
            x_loaded, edges_loaded, iota_done, ident_done, const_done, own_dve, own_pool, onehot_ready, onehot_used,
            cleared, counted, evacuated, turned, mask_done), nc.Block() as block:
        ei = k.sb(mem, "edges_int", [T, 2, EC], I32)
        ef = k.sb(mem, "edges_float", [T, 2, EC])
        ioi = k.sb(mem, "iota_int", [P, N], I32)
        ioh = k.sb(mem, "iota_half", [P, N], F16)
        oh = k.sb(mem, "onehots", [T, G, 2, N + 1], BF16)
        zero = k.sb(mem, "zeros", [T, 512], BF16)

        def main(s):
            return k.bank(s)[0:T, 0:512]

        def rest(s):
            return k.bank(5)[0:T, s * REST:(s + 1) * REST] if s < 4 else k.bank(6)[0:T, 0:REST]

        @block.sync
        def _(sp):
            sp.dma_start(ei[:, 0, :], src.rearrange("(p c) -> p c", p=T)).then_inc(edges_loaded, 16)
            sp.dma_start(ei[:, 1, :], dst.rearrange("(p c) -> p c", p=T)).then_inc(edges_loaded, 16)
            sp.dma_start(k.X[:], x.rearrange("(t p) d -> p t d", p=T)).then_inc(x_loaded, 16)
            sp.wait_ge(x_loaded, 16)

        @block.gpsimd
        def _(pool):
            own = Own(pool, own_pool)
            pool.iota(ioi[:], pattern=[[1, N]], base=0, channel_multiplier=0).then_inc(iota_done, 1)
            own.link(pool.memset(k.ident[:], 0.0))
            pool.affine_select(out=k.ident[:], in_=k.ident[:], compare_op=ALU.not_equal, fill=1.0, base=0,
                               pattern=[[-1, P]], channel_multiplier=1).then_inc(ident_done, 1)
            pool.memset(k.ones[:], 1.0).then_inc(const_done, 1)
            pool.memset(k.eps[:], EPS).then_inc(const_done, 1)
            pool.memset(k.XT[:, :, N:NP], 0.0).then_inc(const_done, 1)

        @block.vector
        def _(dve):
            own = Own(dve, own_dve)
            dve.memset(zero[:], 0.0).then_inc(cleared, 1)
            dve.wait_ge(iota_done, 1)
            own.sign(dve.tensor_copy(ioh[:], ioi[:]))
            own.sign(dve.tensor_copy(k.iota8[:], ioi[:, 0:8]))
            dve.wait_ge(edges_loaded, 32)
            own.link(dve.tensor_copy(ef[:], ei[:]))
            dve.sem_inc(onehot_used, 1)
            with dve.Fori(0, EC // G) as i:
                dve.wait_ge(onehot_used, i + 1)
                for g in range(G):
                    for side in range(2):
                        dve.tensor_scalar(oh[:, g, side, 0:N], ioh[0:T, :], ef[:, side, bass.ds(i * G + g, 1)],
                                          None, ALU.is_equal).then_inc(onehot_ready, 1)
            dve.wait_ge(counted, 1)
            for s in range(NT):
                dve.tensor_copy(k.C[:, s, 0:512], main(s)).then_inc(evacuated, 1)
                dve.tensor_copy(k.C[:, s, 512:N], rest(s)).then_inc(evacuated, 1)
            for d in range(NT):
                dve.wait_ge(turned, d + 1)
                dve.tensor_scalar(k.MASK[:, d, :], k.slot(d % 3)[0:T, TR:TR + N], 0.5, LOW, ALU.is_lt,
                                  ALU.mult).then_inc(mask_done, 1)

        @block.tensor
        def _(pe):
            pe.wait_ge(cleared, 1)
            for b in range(7):
                pe.matmul(k.bank(b)[0:T, :], zero[:, 0:T], zero[:], start=True, stop=False, skip_group_check=True)
            with pe.Fori(0, EC // G) as i:
                for g in range(G):
                    pe.wait_ge(onehot_ready, i * (2 * G) + (2 * g + 2))
                    for s in range(NT):
                        for out, a, b in ((main(s), 0, 512), (rest(s), 512, N)):
                            last = pe.matmul(out, oh[:, g, 0, cols(s)], oh[:, g, 1, a:b], start=False, stop=False,
                                             skip_group_check=True)
                last.then_inc(onehot_used, 1)
            pe.matmul(k.bank(6)[0:T, :], zero[:, 0:T], zero[:], start=False, stop=True,
                      skip_group_check=True).then_inc(counted, 1)
            pe.wait_ge(ident_done, 1)
            pe.wait_ge(const_done, 1)
            pe.wait_ge(evacuated, 2 * NT)
            for d in range(NT):
                if d >= 3:
                    pe.wait_ge(mask_done, d - 2)
                for s in range(NT):
                    last = pe.transpose(k.slot(d % 3)[0:T, TR + s * T:TR + (s + 1) * T], k.C[:, s, cols(d)],
                                        k.ident[0:T, 0:T])
                last.then_inc(turned, 1)


def layer_norm(k, src, dst, out=None, scale=None, shift=None, add_to=None):
    nc = k.nc
    with ExitStack() as mem, k.sems(
            "own_dve var_ready std_ready normed turned moved_dve moved_act weights_loaded added") as (
            own_dve, var_ready, std_ready, normed, turned, moved_dve, moved_act, weights_loaded, added), \
            nc.Block() as block:
        stats = k.sb(mem, "stats", [T, NT, 2, 6])
        mv = k.sb(mem, "mean_var", [T, NT, 2])
        std = k.sb(mem, "std", [T, NT])
        rstd = k.sb(mem, "rstd", [T, NT])
        wb = k.sb(mem, "scale_shift", [P, 2, KD])

        if add_to is not None:
            @block.gpsimd
            def _(pool):
                for t in range(NT):
                    pool.tensor_tensor(add_to[:, t, :], add_to[:, t, :], src[:, t, :], ALU.add).then_inc(added, 1)

        if scale is not None:
            @block.sync
            def _(sp):
                sp.dma_start(wb[:, 0, :], scale).then_inc(weights_loaded, 16)
                sp.dma_start(wb[:, 1, :], shift).then_inc(weights_loaded, 16)

        @block.vector
        def _(dve):
            own = Own(dve, own_dve)
            for t in range(NT):
                for h in range(2):
                    own.sign(dve.bn_stats(stats[:, t, h, :], src[:, t, h * 384:(h + 1) * 384]))
            own.wait()
            for t in range(NT):
                dve.bn_aggr(mv[:, t, :], stats[:, t, :, :].rearrange("p a b -> p (a b)")).then_inc(var_ready, 1)
            dve.wait_ge(std_ready, 1)
            own.link(dve.reciprocal(rstd[:], std[:]))
            for t in range(NT):
                dve.tensor_scalar(dst[:, t, :], src[:, t, :], mv[:, t, 0:1], rstd[:, t:t + 1], ALU.subtract,
                                  ALU.mult).then_inc(normed, 1)
            if out is not None:
                if scale is not None:
                    dve.wait_ge(weights_loaded, 32)
                for c in range(KD):
                    dve.wait_ge(turned, c + 1)
                    a = k.slot(c % 4)[:, TR:TR + 3 * T]
                    if scale is None:
                        dve.tensor_copy(out[:, c, 0:3 * T], a).then_inc(moved_dve, 1)
                    else:
                        dve.tensor_scalar(out[:, c, 0:3 * T], a, wb[:, 0, c:c + 1], wb[:, 1, c:c + 1], ALU.mult,
                                          ALU.add).then_inc(moved_dve, 1)

        @block.scalar
        def _(act):
            act.wait_ge(var_ready, NT)
            act.activation(std[:], mv[:, :, 1], ACT.Sqrt, bias=k.eps[0:T, 0:1]).then_inc(std_ready, 1)
            if out is not None:
                if scale is not None:
                    act.wait_ge(weights_loaded, 32)
                for c in range(KD):
                    act.wait_ge(turned, c + 1)
                    a = k.slot(c % 4)[:, TR + 3 * T:TR + N]
                    if scale is None:
                        act.activation(out[:, c, 3 * T:N], a, ACT.Copy).then_inc(moved_act, 1)
                    else:
                        act.activation(out[:, c, 3 * T:N], a, ACT.Identity, bias=wb[:, 1, c:c + 1],
                                       scale=wb[:, 0, c:c + 1]).then_inc(moved_act, 1)

        @block.tensor
        def _(pe):
            if out is None:
                return
            pe.wait_ge(normed, NT)
            for c in range(KD):
                if c >= 4:
                    pe.wait_ge(moved_dve, c - 3)
                    pe.wait_ge(moved_act, c - 3)
                for t in range(NT):
                    last = pe.transpose(k.slot(c % 4)[:, TR + t * T:TR + (t + 1) * T],
                                        dst[:, t, c * P:(c + 1) * P], k.ident[0:T, 0:T])
                last.then_inc(turned, 1)


def rows_out(k, block, vec, R, dram, ready, turned, moved, stored, need=1):
    rows = k.rows

    def pe_part(pe):
        pe.wait_ge(ready, need)
        for t in range(NT):
            last = pe.transpose(k.slot(3)[0:R, TR + t * T:TR + (t + 1) * T], vec[:, t, :], k.ident[0:T, 0:T])
        last.then_inc(turned, 1)

    def dve_part(dve):
        dve.wait_ge(turned, 1)
        dve.tensor_copy(rows[0:R, :], k.slot(3)[0:R, TR:TR + N]).then_inc(moved, 1)

    def sp_part(sp):
        sp.wait_ge(moved, 1)
        sp.dma_start(dram, rows[0:R, :]).then_inc(stored, 16)
        sp.wait_ge(stored, 16)

    return pe_part, dve_part, sp_part


def add_loops(k):
    nc = k.nc
    with ExitStack() as mem, k.sems("own_dve looped deg_ready inverted rooted") as (
            own_dve, looped, deg_ready, inverted, rooted), nc.Block() as block:
        inv = k.sb(mem, "inverse_degree", [T, NT])
        off = k.sb(mem, "off_diagonal", [T, T])

        @block.vector
        def _(dve):
            own = Own(dve, own_dve)
            own.link(dve.tensor_scalar(off[:], k.ident[0:T, 0:T], -1.0, 1.0, ALU.mult, ALU.add))
            for s in range(NT):
                dve.tensor_tensor(k.C[:, s, cols(s)], k.C[:, s, cols(s)], k.ident[0:T, 0:T], ALU.add
                                  ).then_inc(looped, 1)
                own.sign(dve.tensor_tensor(k.MASK[:, s, cols(s)], k.MASK[:, s, cols(s)], off[:], ALU.mult))
            dve.wait_ge(deg_ready, 1)
            dve.reciprocal(inv[:], k.bank(7)[0:T, 0:NT]).then_inc(inverted, 1)

        @block.scalar
        def _(act):
            act.wait_ge(inverted, 1)
            act.activation(k.dinv[:], inv[:], ACT.Sqrt).then_inc(rooted, 1)

        @block.tensor
        def _(pe):
            pe.wait_ge(looped, NT)
            for d in range(NT):
                for s in range(NT):
                    last = pe.matmul(k.bank(7)[0:T, d:d + 1], k.C[:, s, cols(d)], k.ones[0:T, 0:1],
                                     start=(s == 0), stop=(s == NT - 1))
            last.then_inc(deg_ready, 1)


def gat_max(k, H, A12, a1_dram, r_dram, B1):
    nc = k.nc
    with ExitStack() as mem, k.sems(
            "row_loaded0 row_loaded1 maxed own_dve rows_ready turned moved stored") as (
            row_loaded0, row_loaded1, maxed, own_dve, rows_ready, turned, moved, stored), nc.Block() as block:
        row_loaded = [row_loaded0, row_loaded1]
        row = [k.sb(mem, "a1_row", [T, N]) for _ in range(2)]
        junk = k.sb(mem, "masked", [T, 2, N])
        M = k.sb(mem, "max_a1", [T, NT, H])
        m = k.sb(mem, "leaky_max", [T, NT, H])
        R = k.sb(mem, "score_rows", [T, NT, 2 * H])
        a1, a2 = A12[:, :, 0:H], A12[:, :, H:2 * H]
        pe_part, dve_part, sp_part = rows_out(k, block, R, 2 * H, r_dram, rows_ready, turned, moved, stored, need=2)

        @block.sync
        def _(sp):
            for h in range(H):
                if h >= 2:
                    sp.wait_ge(maxed, NT * (h - 1))
                sp.dma_start(row[h % 2][:], a1_dram[h:h + 1, :].to_broadcast([T, N])).then_inc(row_loaded[h % 2], 16)
            sp_part(sp)

        @block.vector
        def _(dve):
            own = Own(dve, own_dve)
            for h in range(H):
                dve.wait_ge(row_loaded[h % 2], 16 * (h // 2 + 1))
                for d in range(NT):
                    n = NT * h + d
                    if n >= 2:
                        dve.wait_ge(maxed, n - 1)
                    dve.tensor_tensor_reduce(junk[:, n % 2, :], row[h % 2][:], k.MASK[:, d, :], 1.0, -3e38,
                                             ALU.add, ALU.max, M[:, d, h:h + 1]).then_inc(maxed, 1)
            dve.wait_ge(maxed, NT * H)
            own.link(dve.tensor_tensor(M[:], M[:], a2, ALU.add))
            own.link(dve.scalar_tensor_tensor(m[:], M[:], SLOPE, M[:], ALU.mult, ALU.max))
            dve.tensor_tensor(R[:, :, 0:H], a2, m[:], ALU.subtract).then_inc(rows_ready, 1)
            dve.scalar_tensor_tensor(R[:, :, H:2 * H], a2, SLOPE, m[:], ALU.mult, ALU.subtract).then_inc(rows_ready, 1)
            own.link(dve.tensor_scalar(B1[:], a1, SLOPE, None, ALU.mult))
            dve_part(dve)

        @block.tensor
        def _(pe):
            pe_part(pe)


def gat_weights_parts(k, E, rows, r_dram, H, A12, B1, rows_loaded, e_ready, e_free, p_ready, p_free, own_sem, PB):
    r_v = r_dram.rearrange("(two h) n -> h two n", two=2)

    def load_rows(sp, h, b):
        sp.dma_start(rows[b][:], r_v[h, :, :].partition_broadcast(T)).then_inc(rows_loaded[b], 16)

    def act_head(act, h, b, round_no, nth):
        act.wait_ge(rows_loaded[b], round_no)
        for s in range(NT):
            e = E[(b * NT + s) % 2]
            act.wait_ge(e_free, nth + (s + 1))
            act.activation(e[:, 0, :], rows[b][:, 0, :], ACT.Exp, bias=A12[:, s, bass.ds(h, 1)]).then_inc(e_ready, 1)
            act.activation(e[:, 1, :], rows[b][:, 1, :], ACT.Exp, bias=B1[:, s, bass.ds(h, 1)]).then_inc(e_ready, 1)

    def dve_head(dve, own, b, head_no, nth):
        dve.wait_ge(p_free, head_no)
        for s in range(NT):
            e = E[(b * NT + s) % 2]
            dve.wait_ge(e_ready, nth * 2 + 2 * (s + 1))
            own.link(dve.tensor_tensor(e[:, 0, :], e[:, 0, :], e[:, 1, :], ALU.max))
            own.link(dve.scalar_tensor_tensor(PB[b][:, s, :], e[:, 0, :], 1.0, k.C[:, s, :], ALU.min, ALU.mult))
            dve.sem_inc(e_free, 1)
            dve.sem_inc(p_ready, 1)

    return load_rows, act_head, dve_head


def l0_gnn(k, W, al, ar, Wr):
    nc, H, HD = k.nc, 12, 64
    a1_dram, r_dram = k.dram("l0_a", [2 * H, N]), k.dram("l0_r", [2 * H, N])
    with ExitStack() as mem:
        FTX = k.sb(mem, "ft", [T, NT, H, HD + 1])
        A12 = k.sb(mem, "a12", [T, NT, 2 * H])
        B1 = k.sb(mem, "b1", [T, NT, H])
        Wbd = k.sb(mem, "w_blocks", [P, 2, P])
        with ExitStack() as tmp, k.sems(
                "cleared loaded attn_loaded product_done ft_moved scored own_dve ready turned moved stored") as (
                cleared, loaded, attn_loaded, product_done, ft_moved, scored, own_dve, ready, turned, moved, stored), \
                nc.Block() as block:
            attn = k.sb(tmp, "attn", [T, 2, D])
            prod = k.sb(tmp, "prod", [T, 2, D])
            pe_part, dve_part, sp_part = rows_out(k, block, A12, 2 * H, a1_dram, scored, turned, moved, stored,
                                                  need=2 * NT)

            @block.gpsimd
            def _(pool):
                pool.memset(Wbd[:], 0.0).then_inc(cleared, 1)
                pool.memset(FTX[:, :, :, HD:HD + 1], 1.0).then_inc(cleared, 1)

            @block.sync
            def _(sp):
                sp.dma_start(attn[:, 0, :], row_of(al, T)).then_inc(attn_loaded, 16)
                sp.dma_start(attn[:, 1, :], row_of(ar, T)).then_inc(attn_loaded, 16)
                sp.wait_ge(cleared, 2)
                for n, w in enumerate((W, Wr)):
                    for b in range(2):
                        sp.dma_start(Wbd[b * HD:(b + 1) * HD, n, b * HD:(b + 1) * HD], w).then_inc(loaded, 16)
                sp_part(sp)

            @block.tensor
            def _(pe):
                pe.wait_ge(loaded, 64)
                for t in range(NT):
                    if t >= 3:
                        pe.wait_ge(ft_moved, t - 2)
                    for c in range(KD):
                        last = pe.matmul(k.bank(2 * (t % 3) + c // 3)[0:T, (c % 3) * P:(c % 3 + 1) * P],
                                         k.XT[:, c, cols(t)], Wbd[:, 0, :], start=True, stop=True)
                    last.then_inc(product_done, 1)
                pe_part(pe)

            @block.scalar
            def _(act):
                for t in range(NT):
                    act.wait_ge(product_done, t + 1)
                    out = FTX[:, t, :, 0:HD].rearrange("p (b h) e -> p b h e", b=2)
                    pv = k.slot(t % 3)[0:T].rearrange("p (b n) -> p b n", b=2)[:, :, 0:384]
                    for b in range(2):
                        ins = act.activation(out[:, b], pv[:, b].rearrange("p (h e) -> p h e", e=HD), ACT.Copy)
                    ins.then_inc(ft_moved, 1)

            @block.vector
            def _(dve):
                own = Own(dve, own_dve)
                dve.wait_ge(attn_loaded, 32)
                for t in range(NT):
                    dve.wait_ge(ft_moved, t + 1)
                    for n in range(2):
                        own.link(dve.tensor_tensor(prod[:, n, :].rearrange("p (h e) -> p h e", e=HD),
                                                   FTX[:, t, :, 0:HD],
                                                   attn[:, n, :].rearrange("p (h e) -> p h e", e=HD), ALU.mult))
                        dve.tensor_reduce(A12[:, t, n * H:(n + 1) * H],
                                          prod[:, n, :].rearrange("p (h e) -> p h e", e=HD), AX.X,
                                          ALU.add).then_inc(scored, 1)
                dve_part(dve)

        gat_max(k, H, A12, a1_dram, r_dram, B1)

        with ExitStack() as tmp, k.sems(
                "rows_loaded0 rows_loaded1 e_ready e_free p_ready p_free own_dve agg_done agg_free res_done res_used") as (
                rows_loaded0, rows_loaded1, e_ready, e_free, p_ready, p_free, own_dve, agg_done, agg_free, res_done,
                res_used), nc.Block() as block:
            rows_loaded = [rows_loaded0, rows_loaded1]
            rows = [k.sb(tmp, "rows", [T, 2, N]) for _ in range(2)]
            E = [k.sb(tmp, "exps", [T, 2, N]) for _ in range(2)]
            PB = [k.sb(tmp, "weights", [T, NT, N]) for _ in range(2)]
            den = k.sb(tmp, "den", [T, NT, 1])
            agg = k.XN
            load_rows, act_head, dve_head = gat_weights_parts(k, E, rows, r_dram, H, A12, B1, rows_loaded, e_ready,
                                                              e_free, p_ready, p_free, own_dve, PB)

            @block.sync
            def _(sp):
                for b in range(2):
                    load_rows(sp, b, b)
                with sp.Fori(1, H // 2) as i:
                    for b in range(2):
                        sp.wait_ge(e_ready, (i * 2 + (b - 1)) * (2 * NT))
                        load_rows(sp, i * 2 + b, b)

            @block.scalar
            def _(act):
                with act.Fori(0, H // 2) as i:
                    for b in range(2):
                        act_head(act, i * 2 + b, b, i * 16 + 16, i * (2 * NT) + b * NT)

            @block.vector
            def _(dve):
                own = Own(dve, own_dve)
                dve.sem_inc(e_free, 2)
                dve.sem_inc(agg_free, 2)

                def weights(h, b):
                    dve_head(dve, own, b, h + 1, h * NT)

                def normalise(h, b):
                    dve.wait_ge(agg_done, h + 1)
                    o = k.bank(b)[0:T, 0:NT * (HD + 1)].rearrange("p (t e) -> p t e", e=HD + 1)
                    own.link(dve.tensor_scalar(den[:], o[:, :, HD:HD + 1], 1e-16, None, ALU.max))
                    own.link(dve.reciprocal(den[:], den[:]))
                    own.link(dve.tensor_tensor(agg[:, :, bass.ds(h * HD, HD)], o[:, :, 0:HD],
                                               den[:].to_broadcast([T, NT, HD]), ALU.mult))
                    dve.sem_inc(agg_free, 1)

                weights(0, 0)
                with own.loop(H // 2 - 1, 2 * (2 * NT + 3)) as i:
                    weights(i * 2 + 1, 1)
                    normalise(i * 2, 0)
                    weights(i * 2 + 2, 0)
                    normalise(i * 2 + 1, 1)
                weights(H - 1, 1)
                normalise(H - 2, 0)
                normalise(H - 1, 1)
                for t in range(NT):
                    dve.wait_ge(res_done, t + 1)
                    r = k.slot(1 + t % 3)[0:T].rearrange("p (b n) -> p b n", b=2)[:, :, 0:384]
                    a = agg[:, t, :].rearrange("p (b n) -> p b n", b=2)
                    own.link(dve.tensor_tensor(a, a, r, ALU.add))
                    dve.sem_inc(res_used, 1)
                    own.sign(dve.scalar_tensor_tensor(k.X[:, t, :], agg[:, t, :], 0.0, k.X[:, t, :], ALU.max, ALU.add))
                own.wait()

            @block.tensor
            def _(pe):
                pe.sem_inc(p_free, 2)
                with pe.Fori(0, H // 2) as i:
                    for b in range(2):
                        pe.wait_ge(p_ready, i * (2 * NT) + (b + 1) * NT)
                        pe.wait_ge(agg_free, i * 2 + (b + 1))
                        for d in range(NT):
                            for s in range(NT):
                                last = pe.matmul(k.bank(b)[0:T, d * (HD + 1):(d + 1) * (HD + 1)],
                                                 PB[b][:, s, cols(d)], FTX[:, s, bass.ds(i * 2 + b, 1), :],
                                                 start=(s == 0), stop=(s == NT - 1))
                        last.then_inc(agg_done, 1)
                        pe.wait_ge(agg_done, i * 2 + (b + 1))
                        pe.sem_inc(p_free, 1)
                for t in range(NT):
                    if t >= 3:
                        pe.wait_ge(res_used, t - 2)
                    for c in range(KD):
                        last = pe.matmul(k.bank(2 + 2 * (t % 3) + c // 3)[0:T, (c % 3) * P:(c % 3 + 1) * P],
                                         k.XT[:, c, cols(t)], Wbd[:, 1, :], start=True, stop=True)
                    last.then_inc(res_done, 1)



def product(pe, out, pairs):
    for n, (lhsT, rhs) in enumerate(pairs):
        last = pe.matmul(out, lhsT, rhs, start=(n == 0), stop=(n == len(pairs) - 1), skip_group_check=True)
    return last


def wide(pe, slot, parts, pairs):
    for a, n in HALVES:
        last = product(pe, slot[0:parts, MM + a:MM + a + n], pairs(a, n))
    return last


def halves(ap):
    return ap.rearrange("p (b n) -> p b n", b=2)[:, :, 0:384]


def split(ap):
    return ap.rearrange("p (b n) -> p b n", b=2)


def gcn_aggregate(k, src, scale_out):

    def pe_tile(pe, slot, d):
        for b in range(2):
            last = product(pe, slot[0:T, b * 512:b * 512 + 384],
                           [(k.C[:, s, cols(d)], src[:, s, b * 384:(b + 1) * 384]) for s in range(NT)])
        return last

    return pe_tile


def load_weight(sp, buf, w, sem):
    sp.dma_start(buf, w.rearrange("(k p) n -> p k n", p=P)).then_inc(sem, 16)


def add_bias(k, dst, vec):
    nc = k.nc
    with ExitStack() as mem, k.sems("loaded added") as (loaded, added), nc.Block() as block:
        row = k.sb(mem, "bias_row", [T, D])

        @block.sync
        def _(sp):
            sp.dma_start(row[:], row_of(vec, T)).then_inc(loaded, 16)

        @block.gpsimd
        def _(pool):
            pool.wait_ge(loaded, 16)
            for t in range(NT):
                pool.tensor_tensor(dst[:, t, :], dst[:, t, :], row[:], ALU.add).then_inc(added, 1)


def l1_gnn(k, W, bias):
    nc = k.nc
    with ExitStack() as mem, k.sems(
            "w_loaded bias_loaded product_done h_ready agg_done used own_dve biased") as (
            w_loaded, bias_loaded, product_done, h_ready, agg_done, used, own_dve, biased), nc.Block() as block:
        w = k.sb(mem, "w", [P, KD, D])
        row = k.sb(mem, "bias_row", [T, D])
        h = k.sb(mem, "h", [T, NT, D])
        tile_sums = gcn_aggregate(k, h, None)

        @block.sync
        def _(sp):
            load_weight(sp, w[:], W, w_loaded)
            sp.dma_start(row[:], row_of(bias, T)).then_inc(bias_loaded, 16)

        @block.tensor
        def _(pe):
            pe.wait_ge(w_loaded, 16)
            for t in range(NT):
                if t >= 4:
                    pe.wait_ge(h_ready, t - 3)
                for b in range(2):
                    last = product(pe, k.slot(t % 4)[0:T, b * 512:b * 512 + 384],
                                   [(k.XT[:, c, cols(t)], w[:, c, b * 384:(b + 1) * 384]) for c in range(KD)])
                last.then_inc(product_done, 1)
            pe.wait_ge(h_ready, NT)
            for d in range(NT):
                if d >= 4:
                    pe.wait_ge(used, d - 3)
                tile_sums(pe, k.slot(d % 4), d).then_inc(agg_done, 1)

        @block.gpsimd
        def _(pool):
            pool.wait_ge(bias_loaded, 16)
            for t in range(NT):
                pool.tensor_tensor(k.X[:, t, :], k.X[:, t, :], row[:], ALU.add).then_inc(biased, 1)

        @block.scalar
        def _(act):
            for t in range(NT):
                act.wait_ge(product_done, t + 1)
                act.activation(split(h[:, t, :]), halves(k.slot(t % 4)[0:T]), ACT.Copy,
                               scale=k.dinv[:, t:t + 1]).then_inc(h_ready, 1)

        @block.vector
        def _(dve):
            for d in range(NT):
                dve.wait_ge(agg_done, d + 1)
                dve.wait_ge(biased, d + 1)
                x = split(k.X[:, d, :])
                dve.scalar_tensor_tensor(x, halves(k.slot(d % 4)[0:T]), k.dinv[:, d:d + 1], x, ALU.mult,
                                         ALU.add).then_inc(used, 1)


def l2_gnn(k, W1, b1, W2, b2):
    nc = k.nc
    dinv_dram = k.dram("dinv_row", [1, N])
    with ExitStack() as mem, k.sems(
            "w1_loaded w2_loaded bias_loaded product_done h_ready agg_done agg_used used own_dve biased turned moved "
            "stored row_loaded activated") as (
            w1_loaded, w2_loaded, bias_loaded, product_done, h_ready, agg_done, agg_used, used, own_dve, biased,
            turned, moved, stored, row_loaded, activated), nc.Block() as block:
        w1 = k.sb(mem, "w1", [P, KD, D])
        w2 = k.sb(mem, "w2", [P, KD, D])
        b1c = k.sb(mem, "b1_column", [P, KD])
        row = k.sb(mem, "bias_row", [T, D])
        h = k.sb(mem, "h", [T, NT, D])
        dr = k.sb(mem, "dinv_row", [P, N])
        zT = k.sb(mem, "z_features", [P, KD, N])
        tile_sums = gcn_aggregate(k, h, None)

        @block.sync
        def _(sp):
            load_weight(sp, w1[:], W1, w1_loaded)
            sp.dma_start(row[:], row_of(b2, T)).then_inc(bias_loaded, 16)
            sp.dma_start(b1c[:], b1).then_inc(bias_loaded, 16)
            load_weight(sp, w2[:], W2, w2_loaded)
            sp.wait_ge(moved, 1)
            sp.dma_start(dinv_dram, k.rows[0:1, :]).then_inc(stored, 16)
            sp.wait_ge(stored, 16)
            sp.dma_start(dr[:], dinv_dram.to_broadcast([P, N])).then_inc(row_loaded, 16)

        @block.gpsimd
        def _(pool):
            pool.wait_ge(bias_loaded, 32)
            for t in range(NT):
                pool.tensor_tensor(k.X[:, t, :], k.X[:, t, :], row[:], ALU.add).then_inc(biased, 1)

        @block.tensor
        def _(pe):
            for t in range(NT):
                last = pe.transpose(k.slot(3)[0:1, TR + t * T:TR + (t + 1) * T], k.dinv[:, t:t + 1],
                                    k.ident[0:T, 0:T])
            last.then_inc(turned, 1)
            for conv in range(2):
                src, w = ((k.XT, w1), (zT, w2))[conv]
                pe.wait_ge((w1_loaded, w2_loaded)[conv], 16)
                if conv:
                    pe.wait_ge(activated, KD)
                for t in range(NT):
                    if t >= 3:
                        pe.wait_ge(h_ready, conv * NT + t - 2)
                    for b in range(2):
                        last = product(pe, k.slot(t % 3)[0:T, b * 512:b * 512 + 384],
                                       [(src[:, c, cols(t)], w[:, c, b * 384:(b + 1) * 384]) for c in range(KD)])
                    last.then_inc(product_done, 1)
                pe.wait_ge(h_ready, conv * NT + NT)
                if conv == 0:
                    for c in range(KD):
                        if c >= 3:
                            pe.wait_ge(agg_used, c - 2)
                        wide(pe, k.slot(c % 3), P, lambda a, n: [
                            (h[:, s, c * P:(c + 1) * P], k.C[:, s, a:a + n]) for s in range(NT)]).then_inc(agg_done, 1)
                else:
                    for d in range(NT):
                        if d >= 3:
                            pe.wait_ge(used, d - 2)
                        tile_sums(pe, k.slot(d % 3), d).then_inc(agg_done, 1)

        @block.scalar
        def _(act):
            for conv in range(2):
                for t in range(NT):
                    act.wait_ge(product_done, conv * NT + t + 1)
                    if conv:
                        act.wait_ge(agg_done, KD)
                    act.activation(split(h[:, t, :]), halves(k.slot(t % 3)[0:T]), ACT.Copy,
                                   scale=k.dinv[:, t:t + 1]).then_inc(h_ready, 1)
                if conv == 0:
                    act.wait_ge(bias_loaded, 32)
                    for c in range(KD):
                        act.wait_ge(agg_used, c + 1)
                        act.activation(zT[:, c, :], zT[:, c, :], ACT.Relu, bias=b1c[:, c:c + 1]).then_inc(activated, 1)

        @block.vector
        def _(dve):
            dve.wait_ge(turned, 1)
            dve.tensor_copy(k.rows[0:1, :], k.slot(3)[0:1, TR:TR + N]).then_inc(moved, 1)
            dve.wait_ge(row_loaded, 16)
            for c in range(KD):
                dve.wait_ge(agg_done, c + 1)
                dve.tensor_tensor(zT[:, c, :], k.slot(c % 3)[:, MM:MM + N], dr[:], ALU.mult).then_inc(agg_used, 1)
            for d in range(NT):
                dve.wait_ge(agg_done, KD + d + 1)
                dve.wait_ge(biased, d + 1)
                x = split(k.X[:, d, :])
                dve.scalar_tensor_tensor(x, halves(k.slot(d % 3)[0:T]), k.dinv[:, d:d + 1], x, ALU.mult,
                                         ALU.add).then_inc(used, 1)


def moe(k, router, w1, w2, acted, gating, b1=None, b2=None):
    nc = k.nc
    NE, F = 8, 192
    NC = NE * F // P
    PAIRC = 2 * F // P
    gates_dram = k.dram("gates", [NE, NP])
    with ExitStack() as mem, k.sems(
            "r_loaded logits_done exps_in exps_out own_dve gates_ready turned moved stored w1_loaded0 w1_loaded1 "
            "g_loaded0 g_loaded1 b_loaded w2_loaded up_done up_moved gate_done h_ready down_done down_used "
            "sel_ready own_pool") as (
            r_loaded, logits_done, exps_in, exps_out, own_dve, gates_ready, turned, moved, stored, w1_loaded0,
            w1_loaded1, g_loaded0, g_loaded1, b_loaded, w2_loaded, up_done, up_moved, gate_done, h_ready, down_done,
            down_used, sel_ready, own_pool), nc.Block() as block:
        w1_loaded, g_loaded = [w1_loaded0, w1_loaded1], [g_loaded0, g_loaded1]
        rw = k.sb(mem, "router", [P, KD, NE])
        w1b = [k.sb(mem, "w1_pair", [P, KD, 2 * F]) for _ in range(2)]
        w2b = k.sb(mem, "w2", [P, NC, D])
        HT = k.sb(mem, "hidden", [P, NC, NP])
        gT = k.sb(mem, "gates_rows", [NE, NP])
        g2 = [k.sb(mem, "gates_pair", [2, NP]) for _ in range(2)]
        sel = k.sb(mem, "selector", [2, PAIRC, P])
        b1c = k.sb(mem, "b1_columns", [P, NC])
        b2s = k.sb(mem, "b2", [NE, D])
        lg = k.sb(mem, "logits", [T, NT, NE])
        pr = k.sb(mem, "probs", [T, NT, NE])
        top = k.sb(mem, "top", [T, NT, 8])
        idx = k.sb(mem, "index", [T, NT, 8], U32)
        idf = k.sb(mem, "index_float", [T, NT, 8])
        sm = k.sb(mem, "sums", [T, NT, 1])
        wt = k.sb(mem, "top_weights", [T, NT, 2])
        gs = k.sb(mem, "gates", [T, 2, NT, NE])
        w1v = w1.rearrange("e (k p) f -> e p k f", p=P)

        @block.gpsimd
        def _(pool):
            own = Own(pool, own_pool)
            flat = sel[:].rearrange("e c p -> e (c p)")
            own.link(pool.memset(sel[:], 1.0))
            own.link(pool.affine_select(out=flat, in_=flat, compare_op=ALU.is_ge, fill=0.0, base=0,
                                        pattern=[[1, 2 * F]], channel_multiplier=-F))
            pool.affine_select(out=flat, in_=flat, compare_op=ALU.is_ge, fill=0.0, base=F - 1,
                               pattern=[[-1, 2 * F]], channel_multiplier=F).then_inc(sel_ready, 1)

        @block.sync
        def _(sp):
            sp.dma_start(rw[:], router.rearrange("(k p) e -> p k e", p=P)).then_inc(r_loaded, 16)

            def load_pair(pair, b):
                for e in range(2):
                    sp.dma_start(w1b[b][:, :, e * F:(e + 1) * F], w1v[pair * 2 + e]).then_inc(w1_loaded[b], 16)

            def load_gates(pair, b):
                sp.dma_start(g2[b][:], gates_dram[bass.ds(pair * 2, 2), :]).then_inc(g_loaded[b], 16)

            load_pair(0, 0)
            load_pair(1, 1)
            if b1 is not None:
                sp.dma_start(b1c[:], b1).then_inc(b_loaded, 16)
                sp.dma_start(b2s[:], b2).then_inc(b_loaded, 16)
            sp.dma_start(w2b[:], w2.rearrange("e f d -> (e f) d").rearrange("(c p) d -> p c d", p=P)
                         ).then_inc(w2_loaded, 16)
            sp.wait_ge(moved, 1)
            sp.dma_start(gates_dram, gT[:]).then_inc(stored, 16)
            sp.wait_ge(stored, 16)
            load_gates(0, 0)
            load_gates(1, 1)
            for pair in range(2, 4):
                sp.wait_ge(up_done, (pair - 1) * PAIRC)
                sp.wait_ge(gate_done, (pair - 1) * PAIRC)
                load_pair(pair, pair % 2)
                load_gates(pair, pair % 2)

        @block.tensor
        def _(pe):
            pe.wait_ge(r_loaded, 16)
            for t in range(NT):
                last = product(pe, k.bank(7)[0:T, t * NE:(t + 1) * NE],
                               [(k.XT[:, c, cols(t)], rw[:, c, :]) for c in range(KD)])
            last.then_inc(logits_done, 1)
            pe.wait_ge(sel_ready, 1)

            def up(chunk):
                pair, b, c = chunk // PAIRC, (chunk // PAIRC) % 2, chunk % PAIRC
                if c == 0:
                    pe.wait_ge(w1_loaded[b], 32 * (pair // 2 + 1))
                if chunk >= PAIRC:
                    pe.wait_ge(up_moved, chunk - PAIRC + 1)
                wide(pe, k.slot(c), P, lambda a, n: [
                    (w1b[b][:, kk, c * P:(c + 1) * P], k.XT[:, kk, a:a + n]) for kk in range(KD)]).then_inc(up_done, 1)

            def spread(chunk):
                pair, b, c = chunk // PAIRC, (chunk // PAIRC) % 2, chunk % PAIRC
                if chunk == 0:
                    pe.wait_ge(gates_ready, 1)
                    for t in range(NT):
                        last = pe.transpose(k.slot(3)[0:NE, TR + t * T:TR + (t + 1) * T], gs[:, 0, t, :],
                                            k.ident[0:T, 0:T])
                    last.then_inc(turned, 1)
                    pe.wait_ge(moved, 1)
                if c == 0:
                    pe.wait_ge(g_loaded[b], 16 * (pair // 2 + 1))
                if chunk >= 1:
                    pe.wait_ge(h_ready, chunk)
                wide(pe, k.slot(3), P, lambda a, n: [(sel[:, c, :], g2[b][:, a:a + n])]).then_inc(gate_done, 1)

            LAG = 2
            for chunk in range(NC + LAG):
                if chunk < NC:
                    up(chunk)
                if chunk >= LAG:
                    spread(chunk - LAG)
            pe.wait_ge(w2_loaded, 16)
            pe.wait_ge(h_ready, NC)
            if b1 is not None:
                pe.wait_ge(b_loaded, 32)
            for t in range(NT):
                if t >= 3:
                    pe.wait_ge(down_used, t - 2)
                for b in range(2):
                    pairs = [(HT[:, c, cols(t)], w2b[:, c, b * 384:(b + 1) * 384]) for c in range(NC)]
                    if b1 is not None:
                        pairs.append((gT[:, cols(t)], b2s[:, b * 384:(b + 1) * 384]))
                    last = product(pe, k.slot(t % 3)[0:T, b * 512:b * 512 + 384], pairs)
                last.then_inc(down_done, 1)

        @block.scalar
        def _(act):
            act.wait_ge(exps_in, 1)
            if gating == "logits":
                act.activation(wt[:], wt[:], ACT.Exp).then_inc(exps_out, 1)
            else:
                act.activation(pr[:], lg[:], ACT.Exp).then_inc(exps_out, 1)
            if b1 is not None:
                act.wait_ge(b_loaded, 32)
            for chunk in range(NC):
                act.wait_ge(up_done, chunk + 1)
                bias = b1c[:, chunk:chunk + 1] if b1 is not None else 0.0
                act.activation(HT[:, chunk, 0:N], k.slot(chunk % PAIRC)[:, MM:MM + N], acted, bias=bias
                               ).then_inc(up_moved, 1)

        @block.vector
        def _(dve):
            own = Own(dve, own_dve)
            dve.memset(gT[:, N:NP], 0.0).then_inc(own_dve, 1)
            own.n += 1
            dve.wait_ge(logits_done, 1)
            own.link(dve.tensor_copy(lg[:], k.bank(7)[0:T, 0:NT * NE].rearrange("p (t e) -> p t e", e=NE)))
            from_, weights = lg, None
            if gating != "logits":
                own.link(dve.tensor_reduce(sm[:], lg[:], AX.X, ALU.max))
                own.link(dve.tensor_tensor(lg[:], lg[:], sm[:].to_broadcast([T, NT, NE]), ALU.subtract))
                dve.sem_inc(exps_in, 1)
                dve.wait_ge(exps_out, 1)
                own.link(dve.tensor_reduce(sm[:], pr[:], AX.X, ALU.add))
                own.link(dve.reciprocal(sm[:], sm[:]))
                own.link(dve.tensor_tensor(pr[:], pr[:], sm[:].to_broadcast([T, NT, NE]), ALU.mult))
                from_ = pr
            for t in range(NT):
                own.sign(dve.max(top[:, t, :], from_[:, t, :]))
            own.wait()
            for t in range(NT):
                own.sign(dve.max_index(idx[:, t, :], top[:, t, :], from_[:, t, :]))
            own.wait()
            own.sign(dve.tensor_copy(idf[:], idx[:]))
            if gating == "logits":
                own.link(dve.tensor_tensor(wt[:], top[:, :, 0:2], top[:, :, 0:1].to_broadcast([T, NT, 2]), ALU.subtract))
                dve.sem_inc(exps_in, 1)
                dve.wait_ge(exps_out, 1)
            else:
                own.link(dve.tensor_copy(wt[:], top[:, :, 0:2]))
            if gating != "probs":
                own.link(dve.tensor_reduce(sm[:], wt[:], AX.X, ALU.add))
                own.link(dve.reciprocal(sm[:], sm[:]))
                own.link(dve.tensor_tensor(wt[:], wt[:], sm[:].to_broadcast([T, NT, 2]), ALU.mult))
            for n in range(2):
                own.sign(dve.tensor_tensor(gs[:, n, :, :], k.iota8[0:T, :].rearrange("p (a e) -> p a e", a=1)
                                           .to_broadcast([T, NT, NE]), idf[:, :, n:n + 1].to_broadcast([T, NT, NE]),
                                           ALU.is_equal))
            own.wait()
            for n in range(2):
                own.sign(dve.tensor_tensor(gs[:, n, :, :], gs[:, n, :, :], wt[:, :, n:n + 1].to_broadcast([T, NT, NE]),
                                           ALU.mult))
            own.wait()
            dve.tensor_tensor(gs[:, 0, :, :], gs[:, 0, :, :], gs[:, 1, :, :], ALU.add).then_inc(gates_ready, 1)
            dve.wait_ge(turned, 1)
            dve.tensor_copy(gT[:, 0:N], k.slot(3)[0:NE, TR:TR + N]).then_inc(moved, 1)
            for chunk in range(NC):
                dve.wait_ge(up_moved, chunk + 1)
                dve.wait_ge(gate_done, chunk + 1)
                dve.tensor_tensor(HT[:, chunk, 0:N], HT[:, chunk, 0:N], k.slot(3)[:, MM:MM + N], ALU.mult
                                  ).then_inc(h_ready, 1)
            for t in range(NT):
                dve.wait_ge(down_done, t + 1)
                x = split(k.X[:, t, :])
                dve.tensor_tensor(x, x, halves(k.slot(t % 3)[0:T]), ALU.add).then_inc(down_used, 1)


def at(sem_wait, sem, base, const):
    if isinstance(base, int):
        if base + const > 0:
            sem_wait(sem, base + const)
    else:
        assert const > 0
        sem_wait(sem, base + const)


def turn_parts(k, src, out, turned, moved_dve, moved_act, ready=None, need=0):

    def pe_part(pe):
        if ready is not None:
            pe.wait_ge(ready, need)
        for c in range(KD):
            if c >= 4:
                pe.wait_ge(moved_dve, c - 3)
                pe.wait_ge(moved_act, c - 3)
            for t in range(NT):
                last = pe.transpose(k.slot(c % 4)[:, TR + t * T:TR + (t + 1) * T], src[:, t, c * P:(c + 1) * P],
                                    k.ident[0:T, 0:T])
            last.then_inc(turned, 1)

    def dve_part(dve):
        for c in range(KD):
            dve.wait_ge(turned, c + 1)
            dve.tensor_copy(out[:, c, 0:3 * T], k.slot(c % 4)[:, TR:TR + 3 * T]).then_inc(moved_dve, 1)

    def act_part(act):
        for c in range(KD):
            act.wait_ge(turned, c + 1)
            act.activation(out[:, c, 3 * T:N], k.slot(c % 4)[:, TR + 3 * T:TR + N], ACT.Copy).then_inc(moved_act, 1)

    return pe_part, dve_part, act_part


def attention(k, x, qkv_w, qkv_b, qkv_columns, proj_w, proj_b):
    nc, H, HD = k.nc, 12, 64
    SCALE = HD ** -0.5
    GC = 3
    NG = 2 * KD // GC
    with ExitStack() as mem:
        QK = k.sb(mem, "qk", [P, 2 * KD, N])
        V = k.sb(mem, "v", [T, NT, D])
        O = k.sb(mem, "o", [T, NT, D])
        with ExitStack() as tmp, k.sems(
                "w_loaded0 w_loaded1 v_loaded b_loaded qk_done qk_moved v_done v_moved") as (
                w_loaded0, w_loaded1, v_loaded, b_loaded, qk_done, qk_moved, v_done, v_moved), nc.Block() as block:
            w_loaded = [w_loaded0, w_loaded1]
            wg = [k.sb(tmp, "qk_weights", [P, KD, GC * P]) for _ in range(2)]
            wv = k.sb(tmp, "v_weights", [P, KD, D])
            bc = k.sb(tmp, "qkv_bias", [P, 3 * KD])
            vrow = k.sb(tmp, "v_bias", [T, D])
            wsrc = qkv_w.rearrange("(k p) n -> p k n", p=P)

            @block.sync
            def _(sp):
                sp.dma_start(wg[0][:], wsrc[:, :, 0:GC * P]).then_inc(w_loaded[0], 16)
                sp.dma_start(bc[:], qkv_columns).then_inc(b_loaded, 16)
                sp.dma_start(wg[1][:], wsrc[:, :, GC * P:2 * GC * P]).then_inc(w_loaded[1], 16)
                sp.dma_start(wv[:], wsrc[:, :, 2 * D:3 * D]).then_inc(v_loaded, 16)
                sp.dma_start(vrow[:], row_of(qkv_b[2 * D:3 * D], T)).then_inc(b_loaded, 16)
                for g in range(2, NG):
                    sp.wait_ge(qk_done, (g - 1) * GC)
                    sp.dma_start(wg[g % 2][:], wsrc[:, :, g * GC * P:(g + 1) * GC * P]).then_inc(w_loaded[g % 2], 16)

            @block.tensor
            def _(pe):
                pe.sem_inc(qk_moved, GC)
                with pe.Fori(0, NG // 2) as i:
                    for b in range(2):
                        pe.wait_ge(w_loaded[b], i * 16 + 16)
                        for c in range(GC):
                            pe.wait_ge(qk_moved, i * (2 * GC) + (b * GC + c + 1))
                            wide(pe, k.slot(c), P, lambda a, n: [
                                (wg[b][:, kk, c * P:(c + 1) * P], k.XT[:, kk, a:a + n]) for kk in range(KD)]
                                ).then_inc(qk_done, 1)
                pe.wait_ge(v_loaded, 16)
                for t in range(NT):
                    if t >= 1:
                        pe.wait_ge(qk_moved, 2 * KD + min(t, 3))
                    if t >= 4:
                        pe.wait_ge(v_moved, t - 3)
                    for b in range(2):
                        last = product(pe, k.slot((3 + t) % 4)[0:T, b * 512:b * 512 + 384],
                                       [(k.XT[:, c, cols(t)], wv[:, c, b * 384:(b + 1) * 384]) for c in range(KD)])
                    last.then_inc(v_done, 1)

            @block.scalar
            def _(act):
                act.wait_ge(b_loaded, 32)
                with act.Fori(0, NG // 2) as i:
                    for c in range(2 * GC):
                        act.wait_ge(qk_done, i * (2 * GC) + (c + 1))
                        chunk = i * (2 * GC) + c
                        act.activation(QK[:, bass.ds(chunk, 1), :].rearrange("p a n -> p (a n)"),
                                       k.slot(c % GC)[:, MM:MM + N], ACT.Identity, bias=bc[:, bass.ds(chunk, 1)]
                                       ).then_inc(qk_moved, 1)

            @block.vector
            def _(dve):
                dve.wait_ge(b_loaded, 32)
                for t in range(NT):
                    dve.wait_ge(v_done, t + 1)
                    dve.tensor_tensor(split(V[:, t, :]), halves(k.slot((3 + t) % 4)[0:T]), split(vrow[:]), ALU.add
                                      ).then_inc(v_moved, 1)

        with ExitStack() as tmp, k.sems(
                "pair_ready s_done maxed e_done t_done moved_dve moved_act av_done normed own_dve") as (
                pair_ready, s_done, maxed, e_done, t_done, moved_dve, moved_act, av_done, normed, own_dve), \
                nc.Block() as block:
            QS = [k.sb(tmp, "pair", [P, 3, N]) for _ in range(2)]
            PR = [k.sb(tmp, "probs", [T, N]) for _ in range(2)]
            PT = [k.sb(tmp, "probs_turned", [T, NT, T]) for _ in range(2)]
            mx = k.sb(tmp, "max", [T, 2])
            nb = k.sb(tmp, "minus_max", [T, 2])
            sums = k.sb(tmp, "sums", [T, 4])
            inv = k.sb(tmp, "inverse", [T, 2])
            PU = 2 * NT
            BODY, U = 2 * PU, H * NT
            PEEL, LOOPS = 3, 2

            def s_ap(u):
                return k.slot(u % 2)[0:T, MM:MM + N]

            def t_ap():
                return k.slot(2)[0:T, TR:TR + N].rearrange("p (t n) -> p t n", n=T)

            def av_ap(u):
                return k.bank(6 + u % 2)[0:T, 0:2 * HD]

            def steps(eng, before, step, after):
                before()
                for u in range(PEEL):
                    step(0, u)
                with eng.Fori(0, LOOPS) as i:
                    for j in range(PEEL, PEEL + BODY):
                        step(i * BODY, j)
                for u in range(PEEL + LOOPS * BODY, U):
                    step(0, u)
                after()

            def head(base, j):
                return base // NT + j // NT

            def own_after_max(base, j):
                return base * 2, j + 1 + max(j - 3, 0) if isinstance(base, int) else 2 * j - 2

            def own_after_norm(base, j):
                return base * 2, min(j + 4, U) + j + 1 if isinstance(base, int) else 2 * j + 5

            @block.gpsimd
            def _(pool):
                for buf in QS:
                    for b in range(2):
                        other = slice((1 - b) * HD, (2 - b) * HD)
                        pool.memset(buf[other, b, :], 0.0).then_inc(pair_ready, 1)
                for pair in range(KD):
                    if pair >= 2:
                        pool.wait_ge(s_done, (pair - 1) * PU)
                    for b in range(2):
                        own = slice(b * HD, (b + 1) * HD)
                        pool.tensor_copy(QS[pair % 2][own, b, :], QK[own, pair, :]).then_inc(pair_ready, 1)
                        pool.wait_ge(pair_ready, 3 * pair + b + 5)
                    pool.tensor_copy(QS[pair % 2][:, 2, :], QK[:, KD + pair, :]).then_inc(pair_ready, 1)
                    pool.wait_ge(pair_ready, 3 * pair + 7)

            @block.tensor
            def _(pe):
                def scores(base, j):
                    if isinstance(base, int) and base + j >= U:
                        return
                    pair, b, t = j // PU, (j // NT) % 2, j % NT
                    if j % PU == 0:
                        at(pe.wait_ge, pair_ready, base // PU * 3, 3 * pair + 7)
                    at(pe.wait_ge, e_done, base, j - 1)
                    q = QS[pair % 2][:, b, cols(t)]
                    for a, n in HALVES:
                        last = pe.matmul(s_ap(j)[:, a:a + n], q, QS[pair % 2][:, 2, a:a + n],
                                         start=True, stop=True)
                    last.then_inc(s_done, 1)

                def turn(base, j):
                    at(pe.wait_ge, e_done, base, j + 1)
                    at(pe.wait_ge, moved_dve, base, j)
                    at(pe.wait_ge, moved_act, base, j)
                    for c in range(NT):
                        last = pe.transpose(t_ap()[:, c, :], PR[j % 2][:, cols(c)], k.ident[0:T, 0:T])
                    last.then_inc(t_done, 1)

                def mix(base, j):
                    at(pe.wait_ge, moved_dve, base, j + 1)
                    at(pe.wait_ge, moved_act, base, j + 1)
                    at(pe.wait_ge, normed, base, j - 1)
                    pair = base // PU + j // PU
                    product(pe, av_ap(j), [(PT[j % 2][:, c, :], V[:, c, bass.ds(pair * 2 * HD, 2 * HD)]) for c in range(NT)]
                            ).then_inc(av_done, 1)

                def step(base, j):
                    turn(base, j)
                    scores(base, j + 2)
                    if not (isinstance(base, int) and base + j == 0):
                        mix(base, j - 1)

                def before():
                    scores(0, 0)
                    scores(0, 1)

                steps(pe, before, step, lambda: mix(0, U - 1))

            @block.scalar
            def _(act):
                def exps(base, j):
                    if isinstance(base, int) and base + j >= U:
                        return
                    at(act.wait_ge, maxed, base, j + 1)
                    at(act.wait_ge, t_done, base, j - 1)
                    act.activation(PR[j % 2][:], s_ap(j), ACT.Exp, bias=nb[:, j % 2:j % 2 + 1], scale=SCALE,
                                   accum_out=sums[:, j % 4:j % 4 + 1]).then_inc(e_done, 1)

                def move(base, j):
                    at(act.wait_ge, t_done, base, j + 1)
                    at(act.wait_ge, av_done, base, j - 1)
                    act.activation(PT[j % 2][:, 3:NT, :], t_ap()[:, 3:NT, :], ACT.Copy).then_inc(moved_act, 1)

                def step(base, j):
                    exps(base, j + 1)
                    move(base, j)

                steps(act, lambda: exps(0, 0), step, lambda: None)

            @block.vector
            def _(dve):
                def maxima(base, j):
                    if isinstance(base, int) and base + j >= U:
                        return
                    at(dve.wait_ge, s_done, base, j + 1)
                    at(dve.wait_ge, e_done, base, j - 1)
                    dve.tensor_reduce(mx[:, j % 2:j % 2 + 1], s_ap(j), AX.X, ALU.max).then_inc(own_dve, 1)
                    at(dve.wait_ge, own_dve, *own_after_max(base, j))
                    dve.tensor_scalar(nb[:, j % 2:j % 2 + 1], mx[:, j % 2:j % 2 + 1], -SCALE, None, ALU.mult
                                      ).then_inc(maxed, 1)

                def move(base, j):
                    at(dve.wait_ge, t_done, base, j + 1)
                    at(dve.wait_ge, av_done, base, j - 1)
                    dve.tensor_copy(PT[j % 2][:, 0:3, :], t_ap()[:, 0:3, :]).then_inc(moved_dve, 1)

                def norm(base, j):
                    at(dve.wait_ge, av_done, base, j + 1)
                    dve.reciprocal(inv[:, j % 2:j % 2 + 1], sums[:, j % 4:j % 4 + 1]).then_inc(own_dve, 1)
                    at(dve.wait_ge, own_dve, *own_after_norm(base, j))
                    h, b = head(base, j), (j // NT) % 2
                    dve.tensor_scalar(O[:, j % NT, bass.ds(h * HD, HD)], av_ap(j)[:, b * HD:(b + 1) * HD], inv[:, j % 2:j % 2 + 1], None,
                                      ALU.mult).then_inc(normed, 1)

                def step(base, j):
                    move(base, j)
                    maxima(base, j + 2)
                    if not (isinstance(base, int) and base + j == 0):
                        norm(base, j - 1)

                def before():
                    maxima(0, 0)
                    maxima(0, 1)

                steps(dve, before, step, lambda: norm(0, U - 1))

        with ExitStack() as tmp, k.sems(
                "w_loaded b_loaded turned moved_dve moved_act biased done used") as (
                w_loaded, b_loaded, turned, moved_dve, moved_act, biased, done, used), nc.Block() as block:
            wp = k.sb(tmp, "proj_weights", [P, KD, D])
            OT = k.sb(tmp, "o_features", [P, KD, N])
            row = k.sb(tmp, "proj_bias", [T, D])
            pe_part, dve_part, act_part = turn_parts(k, O, OT, turned, moved_dve, moved_act)

            @block.sync
            def _(sp):
                sp.dma_start(row[:], row_of(proj_b, T)).then_inc(b_loaded, 16)
                load_weight(sp, wp[:], proj_w, w_loaded)

            @block.gpsimd
            def _(pool):
                pool.wait_ge(b_loaded, 16)
                for t in range(NT):
                    pool.tensor_tensor(x[:, t, :], x[:, t, :], row[:], ALU.add).then_inc(biased, 1)

            @block.scalar
            def _(act):
                act_part(act)

            @block.tensor
            def _(pe):
                pe_part(pe)
                pe.wait_ge(w_loaded, 16)
                pe.wait_ge(moved_dve, KD)
                pe.wait_ge(moved_act, KD)
                for t in range(NT):
                    if t >= 4:
                        pe.wait_ge(used, t - 3)
                    for b in range(2):
                        last = product(pe, k.slot(t % 4)[0:T, b * 512:b * 512 + 384],
                                       [(OT[:, c, cols(t)], wp[:, c, b * 384:(b + 1) * 384]) for c in range(KD)])
                    last.then_inc(done, 1)

            @block.vector
            def _(dve):
                dve_part(dve)
                for t in range(NT):
                    dve.wait_ge(done, t + 1)
                    dve.wait_ge(biased, t + 1)
                    xs = split(x[:, t, :])
                    dve.tensor_tensor(xs, xs, halves(k.slot(t % 4)[0:T]), ALU.add).then_inc(used, 1)


def l1_ffn(k, a):
    nc = k.nc
    w = {n[7:]: v for n, v in a.items() if n.startswith("L1_ffn_")}
    with ExitStack() as mem:
        Y = k.sb(mem, "y_normed", [T, NT, D])
        layer_norm(k, k.XN, Y, k.XT, w["norm1_w_columns"], w["norm1_b_columns"])
    attention(k, k.XN, w["qkv_w"], w["qkv_b"], w["qkv_b_columns"], w["proj_w"], w["proj_b"])
    with ExitStack() as mem:
        Y = k.sb(mem, "y_normed", [T, NT, D])
        layer_norm(k, k.XN, Y, k.XT, w["norm2_w_columns"], w["norm2_b_columns"], add_to=k.X)
    moe(k, w["w_gate"], w["W1"], w["W2"], ACT.Gelu, "logits", w["b1_columns"], w["b2"])


def l2_ffn(k, phi, w1, b1, w2, b2):
    nc = k.nc
    NE, S, F = 4, 1024, 192
    NS = NE * S // P
    ES = S // P
    F2 = F - P
    G = 2
    top_dram = k.dram("top_row", [1, N])
    with ExitStack() as mem:
        XW = k.XN
        GT = [ap[:].rearrange("p k n -> p (k n)")[:, 0:NE * N].rearrange("p (e n) -> p e n", n=N)
              for ap in (k.XT, k.XN)]
        HS = k.sb(mem, "hidden", [P, NS, F + 1])
        with ExitStack() as lmem:
            L = k.sb(lmem, "logits", [P, NS, N])
            M = k.sb(lmem, "running_max", [P, N])
            with ExitStack() as tmp, k.sems("w_loaded done moved") as (w_loaded, done, moved), nc.Block() as block:
                w = k.sb(tmp, "w1", [P, KD, NE * F])

                @block.sync
                def _(sp):
                    for e in range(NE):
                        sp.dma_start(w[:, :, e * F:(e + 1) * F], w1[e].rearrange("(k p) f -> p k f", p=P)
                                     ).then_inc(w_loaded, 16)

                @block.tensor
                def _(pe):
                    pe.wait_ge(w_loaded, 16 * NE)
                    for t in range(NT):
                        if t >= 4:
                            pe.wait_ge(moved, t - 3)
                        for b in range(2):
                            last = product(pe, k.slot(t % 4)[0:T, b * 512:b * 512 + 384],
                                           [(k.XT[:, c, cols(t)], w[:, c, b * 384:(b + 1) * 384]) for c in range(KD)])
                        last.then_inc(done, 1)

                @block.scalar
                def _(act):
                    for t in range(NT):
                        act.wait_ge(done, t + 1)
                        act.activation(split(XW[:, t, :]), halves(k.slot(t % 4)[0:T]), ACT.Copy).then_inc(moved, 1)

                @block.vector
                def _(dve):
                    dve.memset(M[:], -3e38)

                @block.gpsimd
                def _(pool):
                    pool.memset(HS[:, :, F:F + 1], 1.0)

            with ExitStack() as tmp, k.sems(
                    "phi_loaded0 phi_loaded1 phi_used b_loaded l_done maxed copied e_done t_done t_moved "
                    "d_ready h_done h_moved own_dve") as (
                    phi_loaded0, phi_loaded1, phi_used, b_loaded, l_done, maxed, copied, e_done, t_done, t_moved,
                    d_ready, h_done, h_moved, own_dve), nc.Block() as block:
                phi_loaded = [phi_loaded0, phi_loaded1]
                ph = [k.sb(tmp, "phi", [P, KD, P]) for _ in range(2)]
                row = k.sb(tmp, "b1_rows", [P, NE, F])
                DT = [k.sb(tmp, "dispatch_turned", [P, N]) for _ in range(2)]
                DN = [k.sb(tmp, "dispatch", [T, NT, P]) for _ in range(2)]
                nm = k.sb(tmp, "minus_max", [P, 2])
                cs = k.sb(tmp, "sums", [P, 2])
                rc = k.sb(tmp, "inverse", [P, 2])
                phv = phi.rearrange("(k p) s -> p k s", p=P)

                def l_ap(j):
                    return k.slot(j % 2)[:, MM:MM + N]

                def t_ap():
                    return k.slot(2)[0:T, 0:NT * P].rearrange("p (t n) -> p t n", n=P)

                def h_ap(j):
                    return k.bank(6 + j % 2)[:, 0:F]

                @block.sync
                def _(sp):
                    def load(chunk, b):
                        sp.dma_start(ph[b][:], phv[:, :, bass.ts(chunk, P)]).then_inc(phi_loaded[b], 16)

                    load(0, 0)
                    load(1, 1)
                    sp.dma_start(row[:].rearrange("p e f -> p (e f)"), row_of(b1.rearrange("e f -> (e f)"), P)
                                 ).then_inc(b_loaded, 16)
                    with sp.Fori(1, NS // G) as i:
                        for b in range(G):
                            sp.wait_ge(l_done, i * G + (b - 1))
                            load(i * G + b, b)

                @block.tensor
                def _(pe):
                    def logits(base, b):
                        at(pe.wait_ge, phi_loaded[b], (base // G) * 16, 16)
                        at(pe.wait_ge, copied, base, b - 1)
                        at(pe.wait_ge, e_done, base, b - 1)
                        wide(pe, k.slot(b), P, lambda a, n: [
                            (ph[b][:, c, :], k.XT[:, c, a:a + n]) for c in range(KD)]).then_inc(l_done, 1)

                    def turn(base, b):
                        at(pe.wait_ge, e_done, base, b + 1)
                        at(pe.wait_ge, t_moved, base, b)
                        for t in range(NT):
                            last = pe.transpose(t_ap()[:, t, :], DT[b][:, cols(t)], k.ident[:])
                        last.then_inc(t_done, 1)

                    def hidden(base, b):
                        at(pe.wait_ge, t_moved, base, b + 1)
                        at(pe.wait_ge, h_moved, base, b - 1)
                        e = base // ES
                        product(pe, h_ap(b), [(DN[b][:, t, :], XW[:, t, bass.ds(e * F, F)]) for t in range(NT)]
                                ).then_inc(h_done, 1)

                    def pair(base, next_):
                        turn(base, 0)
                        logits_at(next_, 0)
                        hidden(base, 0)
                        turn(base, 1)
                        logits_at(next_, 1)
                        hidden(base, 1)

                    def logits_at(base, b):
                        if base is not None:
                            if isinstance(base, int):
                                logits(base, b)
                            else:
                                pe.wait_ge(phi_loaded[b], (base // G) * 16 + 16)
                                pe.wait_ge(copied, base + (b - 1))
                                pe.wait_ge(e_done, base + (b - 1))
                                wide(pe, k.slot(b), P, lambda a, n: [
                                    (ph[b][:, c, :], k.XT[:, c, a:a + n]) for c in range(KD)]).then_inc(l_done, 1)

                    logits(0, 0)
                    logits(0, 1)
                    pair(0, G)
                    with pe.Fori(1, NS // G - 1) as i:
                        for b in range(G):
                            pe.wait_ge(e_done, i * G + (b + 1))
                            pe.wait_ge(t_moved, i * G + b)
                            for t in range(NT):
                                last = pe.transpose(t_ap()[:, t, :], DT[b][:, cols(t)], k.ident[:])
                            last.then_inc(t_done, 1)
                            logits_at(i * G + G, b)
                            pe.wait_ge(t_moved, i * G + (b + 1))
                            pe.wait_ge(h_moved, i * G + (b - 1))
                            product(pe, h_ap(b), [(DN[b][:, t, :], XW[:, t, bass.ds(((i * G) // ES) * F, F)])
                                                  for t in range(NT)]).then_inc(h_done, 1)
                    pair(NS - G, None)

                @block.vector
                def _(dve):
                    own = Own(dve, own_dve)

                    def chunk_max(base, b):
                        at(dve.wait_ge, l_done, base, b + 1)
                        own.link(dve.tensor_reduce(nm[:, b:b + 1], l_ap(b), AX.X, ALU.max, negate=True))
                        own.link(dve.tensor_tensor(M[:], M[:], l_ap(b), ALU.max))
                        dve.sem_inc(maxed, 1)

                    def finish(base, b):
                        at(dve.wait_ge, t_done, base, b + 1)
                        at(dve.wait_ge, h_done, base, b - 1)
                        own.link(dve.tensor_copy(DN[b][:], t_ap()))
                        dve.sem_inc(t_moved, 1)
                        own.link(dve.reciprocal(rc[:, b:b + 1], cs[:, b:b + 1]))
                        at(dve.wait_ge, h_done, base, b + 1)
                        own.link(dve.scalar_tensor_tensor(
                            HS[:, bass.ds(base + b, 1), 0:F].rearrange("p a n -> p (a n)"), h_ap(b), rc[:, b:b + 1],
                            row[:, base // ES, :], ALU.mult, ALU.add))
                        dve.sem_inc(h_moved, 1)

                    dve.wait_ge(b_loaded, 16)
                    chunk_max(0, 0)
                    chunk_max(0, 1)
                    finish(0, 0)
                    chunk_max(G, 0)
                    finish(0, 1)
                    chunk_max(G, 1)
                    with own.loop(NS // G - 2, 2 * 5) as i0:
                        i = i0 + 1
                        for b in range(G):
                            dve.wait_ge(t_done, i * G + (b + 1))
                            dve.wait_ge(h_done, i * G + (b - 1))
                            own.link(dve.tensor_copy(DN[b][:], t_ap()))
                            dve.sem_inc(t_moved, 1)
                            own.link(dve.reciprocal(rc[:, b:b + 1], cs[:, b:b + 1]))
                            dve.wait_ge(l_done, i * G + (G + b + 1))
                            dve.wait_ge(e_done, i * G + (b + 1))
                            own.link(dve.tensor_reduce(nm[:, b:b + 1], l_ap(b), AX.X, ALU.max, negate=True))
                            own.link(dve.tensor_tensor(M[:], M[:], l_ap(b), ALU.max))
                            dve.sem_inc(maxed, 1)
                            dve.wait_ge(h_done, i * G + (b + 1))
                            own.link(dve.scalar_tensor_tensor(
                                HS[:, bass.ds(i * G + b, 1), 0:F].rearrange("p a n -> p (a n)"), h_ap(b),
                                rc[:, b:b + 1], row[:, bass.ds((i * G) // ES, 1), :].rearrange("p a n -> p (a n)"),
                                ALU.mult, ALU.add))
                            dve.sem_inc(h_moved, 1)
                    finish(NS - G, 0)
                    finish(NS - G, 1)

                @block.scalar
                def _(act):
                    def exps(base, b):
                        at(act.wait_ge, maxed, base, b + 1)
                        at(act.wait_ge, t_done, base, b - 1)
                        at(act.wait_ge, h_moved, base, b - 1)
                        act.activation(DT[b][:], l_ap(b), ACT.Exp, bias=nm[:, b:b + 1], accum_out=cs[:, b:b + 1]
                                       ).then_inc(e_done, 1)
                        act.activation(L[:, bass.ds(base + b, 1), :].rearrange("p a n -> p (a n)"), l_ap(b), ACT.Copy
                                       ).then_inc(copied, 1)

                    exps(0, 0)
                    exps(0, 1)
                    with act.Fori(1, NS // G) as i:
                        for b in range(G):
                            act.wait_ge(maxed, i * G + (b + 1))
                            act.wait_ge(t_done, i * G + (b - 1))
                            act.wait_ge(h_moved, i * G + (b - 1))
                            act.activation(DT[b][:], l_ap(b), ACT.Exp, bias=nm[:, b:b + 1], accum_out=cs[:, b:b + 1]
                                           ).then_inc(e_done, 1)
                            act.activation(L[:, bass.ds(i * G + b, 1), :].rearrange("p a n -> p (a n)"), l_ap(b),
                                           ACT.Copy).then_inc(copied, 1)

            with ExitStack() as tmp, k.sems(
                    "turned reduced turned_back moved stored row_loaded gelu_done diff_done e_done staged g_done g_moved "
                    "g_used") as (turned, reduced, turned_back, moved, stored, row_loaded, gelu_done, diff_done, e_done, staged,
                          g_done, g_moved, g_used), nc.Block() as block:
                top = k.sb(tmp, "top", [T, NT])
                trow = k.sb(tmp, "top_row", [P, N])
                CT = [k.sb(tmp, "combine", [P, N]) for _ in range(2)]
                HB = [k.sb(tmp, "hidden_chunk", [P, F + 1]) for _ in range(2)]

                def chunk_of(ap, n):
                    return ap[:, bass.ds(n, 1), :].rearrange("p a n -> p (a n)")

                @block.scalar
                def _(act):
                    for q in range(4):
                        n = NS // 4
                        act.activation(HS[:, q * n:(q + 1) * n, 0:F], HS[:, q * n:(q + 1) * n, 0:F],
                                       ACT.Gelu_apprx_tanh).then_inc(gelu_done, 1)
                    with act.Fori(0, NE) as e:
                        for j in range(ES):
                            act.wait_ge(diff_done, e * ES + (j + 1))
                            act.activation(CT[j % 2][:], CT[j % 2][:], ACT.Exp).then_inc(e_done, 1)
                        act.wait_ge(g_done, e * 2 + 2)
                        act.activation(GT[1][0:F2 + 1, bass.ds(e, 1), :].rearrange("p a n -> p (a n)"),
                                       k.slot(1)[0:F2 + 1, MM:MM + N], ACT.Copy).then_inc(g_moved, 1)

                @block.gpsimd
                def _(pool):
                    pool.wait_ge(gelu_done, 4)
                    pool.wait_ge(turned_back, 1)
                    pool.tensor_copy(HB[0][:], HS[:, 0, :]).then_inc(staged, 1)
                    pool.tensor_copy(HB[1][:], HS[:, 1, :]).then_inc(staged, 1)
                    with pool.Fori(1, NS // G) as i:
                        for b in range(G):
                            pool.wait_ge(g_used, i * G + (b + 1))
                            pool.tensor_copy(HB[b][:], chunk_of(HS, i * G + b)).then_inc(staged, 1)

                @block.sync
                def _(sp):
                    sp.wait_ge(moved, 1)
                    sp.dma_start(top_dram, k.rows[0:1, :]).then_inc(stored, 16)
                    sp.wait_ge(stored, 16)
                    sp.dma_start(trow[:], top_dram.to_broadcast([P, N])).then_inc(row_loaded, 16)

                @block.tensor
                def _(pe):
                    for t in range(NT):
                        last = pe.transpose(k.slot(2)[0:T, t * P:(t + 1) * P], M[:, cols(t)], k.ident[:])
                    last.then_inc(turned, 1)
                    pe.wait_ge(reduced, 1)
                    for t in range(NT):
                        last = pe.transpose(k.slot(3)[0:1, TR + t * T:TR + (t + 1) * T], top[:, t:t + 1],
                                            k.ident[0:T, 0:T])
                    last.then_inc(turned_back, 1)
                    pe.sem_inc(g_moved, 2)
                    pe.sem_inc(g_used, 2)
                    with pe.Fori(0, NE) as e:
                        pe.wait_ge(g_moved, e * 2 + 2)
                        for j in range(ES):
                            pe.wait_ge(staged, e * ES + (j + 1))
                            pe.wait_ge(e_done, e * ES + (j + 1))
                            for c, (f0, fn) in enumerate(((0, P), (P, F2 + 1))):
                                for a, n in HALVES:
                                    last = pe.matmul(k.slot(c)[0:fn, MM + a:MM + a + n], HB[j % 2][:, f0:f0 + fn],
                                                     CT[j % 2][:, a:a + n], start=(j == 0), stop=(j == ES - 1))
                            last.then_inc(g_used, 1)
                        pe.wait_ge(g_used, e * ES + (ES + 2))
                        pe.sem_inc(g_done, 2)

                @block.vector
                def _(dve):
                    dve.wait_ge(turned, 1)
                    dve.tensor_reduce(top[:], k.slot(2)[0:T, 0:NT * P].rearrange("p (t n) -> p t n", n=P), AX.X,
                                      ALU.max).then_inc(reduced, 1)
                    dve.wait_ge(turned_back, 1)
                    dve.tensor_copy(k.rows[0:1, :], k.slot(3)[0:1, TR:TR + N]).then_inc(moved, 1)
                    dve.wait_ge(row_loaded, 16)
                    with dve.Fori(0, NE) as e:
                        for j in range(ES):
                            dve.wait_ge(g_used, e * ES + (j + 1))
                            dve.tensor_tensor(CT[j % 2][:], chunk_of(L, e * ES + j), trow[:], ALU.subtract
                                              ).then_inc(diff_done, 1)
                        dve.wait_ge(g_done, e * 2 + 2)
                        dve.tensor_copy(GT[0][:, bass.ds(e, 1), :].rearrange("p a n -> p (a n)"),
                                        k.slot(0)[:, MM:MM + N]).then_inc(g_moved, 1)

        with ExitStack() as tmp, k.sems("w_loaded ones_done done inverted used own_dve") as (
                w_loaded, ones_done, done, inverted, used, own_dve), nc.Block() as block:
            w2b = k.sb(tmp, "w2", [P, NE, 2, D + 1])
            inv = k.sb(tmp, "inverse", [T, NT])

            @block.gpsimd
            def _(pool):
                pool.memset(w2b[:, :, :, D:D + 1], 0.0).then_inc(ones_done, 1)
                pool.wait_ge(ones_done, 1)
                pool.memset(w2b[F2:F2 + 1, :, 1, D:D + 1], 1.0).then_inc(ones_done, 1)

            @block.sync
            def _(sp):
                for e in range(NE):
                    sp.dma_start(w2b[:, e, 0, 0:D], w2[e, 0:P, :]).then_inc(w_loaded, 16)
                    sp.dma_start(w2b[0:F2, e, 1, 0:D], w2[e, P:F, :]).then_inc(w_loaded, 16)
                    sp.dma_start(w2b[F2:F2 + 1, e, 1, 0:D], b2[e:e + 1, :]).then_inc(w_loaded, 16)

            @block.tensor
            def _(pe):
                pe.wait_ge(w_loaded, 48 * NE)
                pe.wait_ge(ones_done, 2)
                for t in range(NT):
                    if t >= 4:
                        pe.wait_ge(used, t - 3)
                    for b in range(2):
                        n = 384 + b
                        last = product(pe, k.slot(t % 4)[0:T, b * 512:b * 512 + n],
                                       [(GT[c][0:p, e, cols(t)], w2b[0:p, e, c, b * 384:b * 384 + n])
                                        for e in range(NE) for c, p in ((0, P), (1, F2 + 1))])
                    last.then_inc(done, 1)

            @block.vector
            def _(dve):
                for t in range(NT):
                    dve.wait_ge(done, t + 1)
                    dve.reciprocal(inv[:, t:t + 1], k.slot(t % 4)[0:T, 512 + 384:512 + 385]).then_inc(inverted, 1)
                    dve.wait_ge(inverted, t + 1)
                    x = split(k.X[:, t, :])
                    dve.scalar_tensor_tensor(x, halves(k.slot(t % 4)[0:T]), inv[:, t:t + 1], x, ALU.mult, ALU.add
                                             ).then_inc(used, 1)


def l3_gnn(k, W1, s1, d1, b1, W2, s2, d2, b2):
    nc, H, HD = k.nc, 4, 512
    K2 = H * HD // P
    a_dram, r_dram = k.dram("l3_a", [2 * H, N]), k.dram("l3_r", [2 * H, N])
    a_dram2, r_dram2 = k.dram("l3_a2", [2, N]), k.dram("l3_r2", [2, N])
    with ExitStack() as mem:
        ZT = k.sb(mem, "z_features", [P, K2, N])
        with ExitStack() as hmem:
            H1 = k.sb(hmem, "h1", [T, NT, H * HD])
            A12 = k.sb(hmem, "a12", [T, NT, 2 * H])
            B1 = k.sb(hmem, "b1", [T, NT, H])
            with ExitStack() as tmp, k.sems(
                    "w_loaded0 w_loaded1 a_loaded done moved scored own_dve turned moved_rows stored") as (
                    w_loaded0, w_loaded1, a_loaded, done, moved, scored, own_dve, turned, moved_rows, stored), \
                    nc.Block() as block:
                w_loaded = [w_loaded0, w_loaded1]
                wb = [k.sb(tmp, "w1_head", [P, KD, HD]) for _ in range(2)]
                ar = k.sb(tmp, "attn", [T, 2, H * HD])
                junk = k.sb(tmp, "junk", [T, 2, HD])
                pe_part, dve_part, sp_part = rows_out(k, block, A12, 2 * H, a_dram, scored, turned, moved_rows, stored,
                                                      need=2 * NT * H)
                wv = W1.rearrange("(k p) n -> p k n", p=P)

                @block.sync
                def _(sp):
                    for h in range(H):
                        if h >= 2:
                            sp.wait_ge(done, (h - 1) * NT)
                        sp.dma_start(wb[h % 2][:], wv[:, :, h * HD:(h + 1) * HD]).then_inc(w_loaded[h % 2], 16)
                        if h == 0:
                            sp.dma_start(ar[:, 0, :], row_of(s1, T)).then_inc(a_loaded, 16)
                            sp.dma_start(ar[:, 1, :], row_of(d1, T)).then_inc(a_loaded, 16)
                    sp_part(sp)

                @block.tensor
                def _(pe):
                    for h in range(H):
                        pe.wait_ge(w_loaded[h % 2], 16 * (h // 2 + 1))
                        for t in range(NT):
                            n = h * NT + t
                            if n >= 6:
                                pe.wait_ge(moved, n - 5)
                            product(pe, k.bank(n % 6)[0:T, :], [(k.XT[:, c, cols(t)], wb[h % 2][:, c, :])
                                                                for c in range(KD)]).then_inc(done, 1)
                    pe_part(pe)

                @block.scalar
                def _(act):
                    for h in range(H):
                        for t in range(NT):
                            n = h * NT + t
                            act.wait_ge(done, n + 1)
                            act.activation(H1[:, t, h * HD:(h + 1) * HD], k.bank(n % 6)[0:T, :], ACT.Copy
                                           ).then_inc(moved, 1)

                @block.vector
                def _(dve):
                    dve.wait_ge(a_loaded, 32)
                    for h in range(H):
                        for t in range(NT):
                            n = h * NT + t
                            dve.wait_ge(moved, n + 1)
                            for side in range(2):
                                if n >= 1:
                                    dve.wait_ge(scored, 2 * n - 1 + side)
                                dve.tensor_tensor_reduce(
                                    junk[:, side, :], H1[:, t, h * HD:(h + 1) * HD], ar[:, side, h * HD:(h + 1) * HD],
                                    1.0, 0.0, ALU.mult, ALU.add, A12[:, t, side * H + h:side * H + h + 1]
                                    ).then_inc(scored, 1)
                    dve_part(dve)

            gat_max(k, H, A12, a_dram, r_dram, B1)

            with ExitStack() as tmp, k.sems(
                    "rows_loaded0 rows_loaded1 b_loaded e_ready e_free p_ready p_free own_dve den_done inverted "
                    "agg_done clipped elu_used exp_done own_low") as (
                    rows_loaded0, rows_loaded1, b_loaded, e_ready, e_free, p_ready, p_free, own_dve, den_done,
                    inverted, agg_done, clipped, elu_used, exp_done, own_low), nc.Block() as block:
                rows_loaded = [rows_loaded0, rows_loaded1]
                rows = [k.sb(tmp, "rows", [T, 2, N]) for _ in range(1)] * 2
                E = [k.sb(tmp, "exps", [T, 2, N]) for _ in range(2)]
                PB = [k.sb(tmp, "weights", [T, NT, N])] * 2
                rec = k.sb(tmp, "inverse", [P, N])
                low = [k.sb(tmp, "low", [P, N]) for _ in range(2)]
                bc = k.sb(tmp, "b1_columns", [P, K2])
                FC = HD // P
                load_rows, act_head, dve_head = gat_weights_parts(
                    k, E, rows, r_dram, H, A12, B1, rows_loaded, e_ready, e_free, p_ready, p_free, own_dve, PB)

                @block.sync
                def _(sp):
                    sp.dma_start(bc[:], b1).then_inc(b_loaded, 16)
                    for h in range(H):
                        if h >= 1:
                            sp.wait_ge(e_ready, h * 2 * NT)
                        load_rows(sp, h, h % 2)

                def elu_exps(act, h):
                    for f in range(h * FC, (h + 1) * FC):
                        act.wait_ge(clipped, f + 1)
                        act.activation(low[f % 2][:], low[f % 2][:], ACT.Exp).then_inc(exp_done, 1)

                @block.scalar
                def _(act):
                    act.wait_ge(b_loaded, 16)
                    for h in range(H):
                        act_head(act, h, h % 2, 16 * (h // 2 + 1), h * NT)
                        elu_exps(act, h)

                @block.vector
                def _(dve):
                    own = Own(dve, own_dve)
                    dve.sem_inc(e_free, 2)
                    dve.wait_ge(b_loaded, 16)

                    def elu(h):
                        dve.wait_ge(den_done, h + 1)
                        own.link(dve.tensor_scalar(rec[:], k.slot(3)[:, MM:MM + N], 1e-16, None, ALU.add))
                        own.link(dve.reciprocal(rec[:], rec[:]))
                        dve.sem_inc(inverted, 1)

                        def last_part(f):
                            z = ZT[:, f, :]
                            dve.wait_ge(exp_done, f + 1)
                            own.link(dve.tensor_scalar(z, z, bc[:, f:f + 1], 0.0, ALU.add, ALU.max))
                            own.link(dve.scalar_tensor_tensor(z, low[f % 2][:], -1.0, z, ALU.add, ALU.add))

                        for f in range(h * FC, (h + 1) * FC):
                            z = ZT[:, f, :]
                            dve.wait_ge(agg_done, f + 1)
                            own.link(dve.tensor_tensor(z, k.slot(f % 3)[:, MM:MM + N], rec[:], ALU.mult))
                            dve.sem_inc(elu_used, 1)
                            own.link(dve.tensor_scalar(low[f % 2][:], z, bc[:, f:f + 1], 0.0, ALU.add, ALU.min))
                            dve.sem_inc(clipped, 1)
                            if f > h * FC:
                                last_part(f - 1)
                        last_part((h + 1) * FC - 1)

                    for h in range(H):
                        dve_head(dve, own, h % 2, h + 1, h * NT)
                        elu(h)

                @block.tensor
                def _(pe):
                    pe.sem_inc(p_free, 1)
                    for h in range(H):
                        pe.wait_ge(p_ready, NT * (h + 1))
                        if h >= 1:
                            pe.wait_ge(inverted, h)
                        wide(pe, k.slot(3), P, lambda a, n: [
                            (k.ones[0:T, :], PB[h % 2][:, s, a:a + n]) for s in range(NT)]).then_inc(den_done, 1)
                        for f in range(h * FC, (h + 1) * FC):
                            if f >= 3:
                                pe.wait_ge(elu_used, f - 2)
                            wide(pe, k.slot(f % 3), P, lambda a, n: [
                                (H1[:, s, f * P:(f + 1) * P], PB[h % 2][:, s, a:a + n]) for s in range(NT)]
                                ).then_inc(agg_done, 1)
                        pe.wait_ge(agg_done, (h + 1) * FC)
                        pe.sem_inc(p_free, 1)

        H2 = k.sb(mem, "h2", [T, NT, D + 1])
        A12 = k.sb(mem, "a12", [T, NT, 2])
        B1 = k.sb(mem, "b1", [T, NT, 1])
        with ExitStack() as tmp, k.sems(
                "w_loaded0 w_loaded1 a_loaded done moved scored own_dve ready turned moved_rows stored") as (
                w_loaded0, w_loaded1, a_loaded, done, moved, scored, own_dve, ready, turned, moved_rows, stored), \
                nc.Block() as block:
            w_loaded = [w_loaded0, w_loaded1]
            wb = [k.sb(tmp, "w2_block", [P, K2, 384]) for _ in range(2)]
            ar = k.sb(tmp, "attn", [T, 2, D])
            junk = k.sb(tmp, "junk", [T, 2, D])
            pe_part, dve_part, sp_part = rows_out(k, block, A12, 2, a_dram2, scored, turned, moved_rows, stored,
                                                  need=2 * NT)
            wv = W2.rearrange("(k p) n -> p k n", p=P)

            @block.gpsimd
            def _(pool):
                pool.memset(H2[:, :, D:D + 1], 1.0)

            @block.sync
            def _(sp):
                for b in range(2):
                    sp.dma_start(wb[b][:], wv[:, :, b * 384:(b + 1) * 384]).then_inc(w_loaded[b], 16)
                sp.dma_start(ar[:, 0, :], row_of(s2, T)).then_inc(a_loaded, 16)
                sp.dma_start(ar[:, 1, :], row_of(d2, T)).then_inc(a_loaded, 16)
                sp_part(sp)

            @block.tensor
            def _(pe):
                for b in range(2):
                    pe.wait_ge(w_loaded[b], 16)
                    for t in range(NT):
                        n = b * NT + t
                        if n >= 6:
                            pe.wait_ge(moved, n - 5)
                        product(pe, k.bank(n % 6)[0:T, 0:384], [(ZT[:, c, cols(t)], wb[b][:, c, :])
                                                               for c in range(K2)]).then_inc(done, 1)
                pe_part(pe)

            @block.scalar
            def _(act):
                for b in range(2):
                    for t in range(NT):
                        n = b * NT + t
                        act.wait_ge(done, n + 1)
                        act.activation(H2[:, t, b * 384:(b + 1) * 384], k.bank(n % 6)[0:T, 0:384], ACT.Copy
                                       ).then_inc(moved, 1)

            @block.vector
            def _(dve):
                dve.wait_ge(a_loaded, 32)
                for t in range(NT):
                    dve.wait_ge(moved, NT + t + 1)
                    for side in range(2):
                        if t >= 1:
                            dve.wait_ge(scored, 2 * t - 1 + side)
                        dve.tensor_tensor_reduce(junk[:, side, :], H2[:, t, 0:D], ar[:, side, :], 1.0, 0.0, ALU.mult,
                                                 ALU.add, A12[:, t, side:side + 1]).then_inc(scored, 1)
                dve_part(dve)

        gat_max(k, 1, A12, a_dram2, r_dram2, B1)

        with ExitStack() as tmp, k.sems(
                "rows_loaded0 b_loaded e_ready e_free p_ready p_free own_dve agg_done inverted used biased") as (
                rows_loaded0, b_loaded, e_ready, e_free, p_ready, p_free, own_dve, agg_done, inverted, used, biased), \
                nc.Block() as block:
            rows = [k.sb(tmp, "rows", [T, 2, N])]
            E = [k.sb(tmp, "exps", [T, 2, N]) for _ in range(2)]
            PB = [k.sb(tmp, "weights", [T, NT, N])]
            den = k.sb(tmp, "den", [T, NT])
            row = k.sb(tmp, "bias_row", [T, D])
            load_rows, act_head, dve_head = gat_weights_parts(
                k, E, rows, r_dram2, 1, A12, B1, [rows_loaded0], e_ready, e_free, p_ready, p_free, own_dve, PB)

            @block.sync
            def _(sp):
                load_rows(sp, 0, 0)
                sp.dma_start(row[:], row_of(b2, T)).then_inc(b_loaded, 16)

            @block.gpsimd
            def _(pool):
                pool.wait_ge(b_loaded, 16)
                for t in range(NT):
                    pool.tensor_tensor(k.X[:, t, :], k.X[:, t, :], row[:], ALU.add).then_inc(biased, 1)

            @block.scalar
            def _(act):
                act_head(act, 0, 0, 16, 0)

            @block.tensor
            def _(pe):
                pe.sem_inc(p_free, 1)
                pe.wait_ge(p_ready, NT)
                for d in range(NT):
                    if d >= 4:
                        pe.wait_ge(used, d - 3)
                    for b in range(2):
                        n = 384 + b
                        last = product(pe, k.slot(d % 4)[0:T, b * 512:b * 512 + n],
                                       [(PB[0][:, s, cols(d)], H2[:, s, b * 384:b * 384 + n]) for s in range(NT)])
                    last.then_inc(agg_done, 1)

            @block.vector
            def _(dve):
                own = Own(dve, own_dve)
                dve.sem_inc(e_free, 2)
                dve_head(dve, own, 0, 1, 0)
                for d in range(NT):
                    dve.wait_ge(agg_done, d + 1)
                    own.link(dve.tensor_scalar(den[:, d:d + 1], k.slot(d % 4)[0:T, 512 + 384:512 + 385], 1e-16, None,
                                               ALU.add))
                    own.link(dve.reciprocal(den[:, d:d + 1], den[:, d:d + 1]))
                    dve.wait_ge(biased, d + 1)
                    x = split(k.X[:, d, :])
                    dve.scalar_tensor_tensor(x, halves(k.slot(d % 4)[0:T]), den[:, d:d + 1], x, ALU.mult, ALU.add
                                             ).then_inc(used, 1)


def build(nc, a, out):
    ctx = ExitStack()
    with ctx:
        k = Kit(nc, ctx)
        

        def dram(name, shape):
            k.stage_no += 1
            return nc.dram_tensor(f"{name}_{k.stage_no}", shape, F32).ap()

        k.dram = dram
        k.X = k.sb(ctx, "X", [T, NT, D])
        k.XN = k.sb(ctx, "XN", [T, NT, D])
        k.XT = k.sb(ctx, "XT", [P, KD, NP])
        k.C = k.sb(ctx, "counts", [T, NT, N])
        k.MASK = k.sb(ctx, "mask", [T, NT, N])
        k.dinv = k.sb(ctx, "dinv", [T, NT])
        k.ident = k.sb(ctx, "ident", [P, P])
        k.ones = k.sb(ctx, "ones", [P, P])
        k.eps = k.sb(ctx, "eps", [P, 1])
        k.iota8 = k.sb(ctx, "iota8", [P, 8])
        k.rows = k.sb(ctx, "rows", [24, N])
        k.ps = ctx.enter_context(nc.psum_tensor("ps", [P, 4 * SLOT], F32))
        setup(k, a["x"], a["src"], a["dst"])
        layer_norm(k, k.X, k.XN, k.XT)
        l0_gnn(k, a["L0_gnn_W"], a["L0_gnn_attn_l"], a["L0_gnn_attn_r"], a["L0_gnn_W_res"])
        add_loops(k)
        layer_norm(k, k.X, k.XN, k.XT)
        moe(k, a["L0_ffn_router_w"], a["L0_ffn_w1"], a["L0_ffn_w2"], ACT.Gelu_apprx_tanh, "probs")
        layer_norm(k, k.X, k.XN, k.XT)
        l1_gnn(k, a["L1_gnn_W"], a["L1_gnn_b"])
        layer_norm(k, k.X, k.XN)
        l1_ffn(k, a)
        layer_norm(k, k.X, k.XN, k.XT)
        l2_gnn(k, a["L2_gnn_W1"], a["L2_gnn_b1_columns"], a["L2_gnn_W2"], a["L2_gnn_b2"])
        layer_norm(k, k.X, k.XN, k.XT)
        l2_ffn(k, a["L2_ffn_phi"], a["L2_ffn_w1"], a["L2_ffn_b1"], a["L2_ffn_w2"], a["L2_ffn_b2"])
        layer_norm(k, k.X, k.XN, k.XT)
        l3_gnn(k, a["L3_gnn_W1"], a["L3_gnn_a1_src"], a["L3_gnn_a1_dst"], a["L3_gnn_b1_columns"], a["L3_gnn_W2"],
               a["L3_gnn_a2_src"], a["L3_gnn_a2_dst"], a["L3_gnn_b2"])
        layer_norm(k, k.X, k.XN, k.XT)
        moe(k, a["L3_ffn_router_w"], a["L3_ffn_up_w"], a["L3_ffn_down_w"], ACT.Gelu, "renormalised")
        with k.sems("stored") as (stored,), nc.Block() as block:
            @block.sync
            def _(sp):
                sp.dma_start(out.rearrange("(t p) d -> p t d", p=T), k.X[:]).then_inc(stored, 16)
                sp.wait_ge(stored, 16)


def layout(inputs):
    import numpy as np
    turned = {"L0_gnn_W", "L0_gnn_W_res", "L0_ffn_router_w", "L1_ffn_qkv_w", "L1_ffn_proj_w", "L3_ffn_router_w"}
    flat = {"L0_gnn_attn_l", "L0_gnn_attn_r", "L3_gnn_a1_src", "L3_gnn_a1_dst", "L3_gnn_a2_src", "L3_gnn_a2_dst"}
    columns = {"L1_ffn_norm1_w", "L1_ffn_norm1_b", "L1_ffn_norm2_w", "L1_ffn_norm2_b", "L1_ffn_qkv_b", "L1_ffn_b1",
               "L2_gnn_b1", "L3_gnn_b1"}
    arrays = {}
    for name, v in inputs.items():
        v = np.asarray(v)
        if name in turned:
            v = v.T
        if name in flat:
            v = v.reshape(-1)
        if name in columns:
            arrays[name + "_columns"] = np.ascontiguousarray(v.reshape(-1, P).T)
        if name == "L2_ffn_phi":
            v = v.reshape(-1, v.shape[-1]).T
        arrays[name] = np.ascontiguousarray(v)
    return arrays


def kernel(**inputs):
    import concourse.bacc as bacc
    from concourse.bass_utils import run_bass_kernel_spmd
    nc = bacc.Bacc("TRN2", target_bir_lowering=False, num_devices=1)
    arrays = layout(inputs)
    aps = {n: nc.dram_tensor("in_" + n, v.shape, mybir.dt.from_np(v.dtype), kind="ExternalInput").ap()
           for n, v in arrays.items()}
    out = nc.dram_tensor("out", (N, D), F32, kind="ExternalOutput").ap()
    build(nc, aps, out)
    r = run_bass_kernel_spmd(nc, [{"in_" + n: v for n, v in arrays.items()}], core_ids=[0])
    return r.results[0]["out"]
```

```python
from contextlib import ExitStack, contextmanager

import concourse.bass as bass
from concourse import mybir

F32 = mybir.dt.float32
F32R = mybir.dt.float32r
F16 = mybir.dt.float16
BF16 = mybir.dt.bfloat16
I32 = mybir.dt.int32
U32 = mybir.dt.uint32
ALU = mybir.AluOpType
ACT = mybir.ActivationFunctionType
AX = mybir.AxisListType

P = 128
N = 625
T = 125
NT = N // T
D = 768
KD = D // P
NP = 626
HALVES = [(0, 312), (312, 313)]
SLOT = 1024
MM = 200
TR = 137
RHALVES = [(0, 312), (312, 314)]
TC = 12
UNIT = 768
RING = 4
EPS = 1e-5
SLOPE = 0.2
LOW = -1e30


class Own:

    def __init__(self, eng, sem):
        self.eng, self.sem, self.n, self.base = eng, sem, 0, 0

    def sign(self, ins):
        ins.then_inc(self.sem, 1)
        self.n += 1

    def wait(self):
        self.eng.wait_ge(self.sem, self.base + self.n)

    def link(self, ins):
        self.sign(ins)
        self.wait()

    @contextmanager
    def loop(self, count, per):
        before = self.base + self.n
        with self.eng.Fori(0, count) as i:
            self.base, self.n = i * per + before, 0
            yield i
            assert self.n == per, (self.n, per)
        self.base, self.n = before + count * per, 0


class Kit:

    def __init__(self, nc, ctx):
        self.nc, self.ctx, self.stage_no = nc, ctx, 0

    def sb(self, mem, name, shape, dt=F32):
        self.stage_no += 1
        return mem.enter_context(self.nc.sbuf_tensor(f"{name}_{self.stage_no}", shape, dt))

    @contextmanager
    def sems(self, names):
        self.stage_no += 1
        got = [self.nc.alloc_semaphore(f"{n}_{self.stage_no}") for n in names.split()]
        yield got
        self.nc.clear_and_free_semaphores(got)
        self.nc.all_engine_barrier()

    @contextmanager
    def stage(self, names):
        with self.sems(names) as got:
            yield dict(zip(names.split(), got))

    def slot(self, i):
        return self.ps[:, i * SLOT:(i + 1) * SLOT]

    def bank(self, i):
        return self.ps[:, i * 512:(i + 1) * 512]


def cols(t):
    return slice(t * T, (t + 1) * T)


def row_of(vec, parts, n=None):
    return vec.rearrange("(a n) -> a n", a=1).to_broadcast([parts, vec.shape[0]])


def setup(k, x, src, dst, norm_args):
    nc = k.nc
    E = src.shape[0]
    EC = E // T
    G = 5
    REST = N - 512
    with ExitStack() as mem, k.stage(
            "x_loaded edges_loaded iota_done ident_done const_done own_dve own_pool onehot_ready onehot_used cleared "
            "counted evacuated turned mask_done" + Norm.SEMS) as s, nc.Block() as block:
        norm = Norm(k, mem, s, **norm_args)
        ei = k.sb(mem, "edges_int", [T, 2, EC], I32)
        ef = k.sb(mem, "edges_float", [T, 2, EC])
        ioi = k.sb(mem, "iota_int", [P, N], I32)
        ioh = k.sb(mem, "iota_half", [P, N], F16)
        oh = k.sb(mem, "onehots", [T, G, 2, N + 1], BF16)
        zero = k.sb(mem, "zeros", [T, 512], BF16)

        def main(c):
            return k.bank(c)[0:T, 0:512]

        def rest(c):
            return k.bank(5)[0:T, c * REST:(c + 1) * REST] if c < 4 else k.bank(6)[0:T, 0:REST]

        @block.sync
        def _(sp):
            sp.dma_start(ei[:, 0, :], src.rearrange("(p c) -> p c", p=T)).then_inc(s["edges_loaded"], 16)
            sp.dma_start(ei[:, 1, :], dst.rearrange("(p c) -> p c", p=T)).then_inc(s["edges_loaded"], 16)
            sp.dma_start(k.X[:], x.rearrange("(t p) d -> p t d", p=T)).then_inc(s["x_loaded"], 16)
            sp.wait_ge(s["x_loaded"], 16)

        @block.gpsimd
        def _(pool):
            own = Own(pool, s["own_pool"])
            pool.iota(ioi[:], pattern=[[1, N]], base=0, channel_multiplier=0).then_inc(s["iota_done"], 1)
            own.link(pool.memset(k.ident[:], 0.0))
            pool.affine_select(out=k.ident[:], in_=k.ident[:], compare_op=ALU.not_equal, fill=1.0, base=0,
                               pattern=[[-1, P]], channel_multiplier=1).then_inc(s["ident_done"], 1)
            pool.memset(k.ones[:], 1.0).then_inc(s["const_done"], 1)
            pool.memset(k.eps[:], EPS).then_inc(s["const_done"], 1)
            own.link(pool.memset(k.zero[:], 0.0))
            for part in (k.XT.hi, k.XT.lo):
                own.link(pool.tensor_copy(part[:, :, N:NP], k.zero[:]))

        @block.vector
        def _(dve):
            own = Own(dve, s["own_dve"])
            dve.memset(zero[:], 0.0).then_inc(s["cleared"], 1)
            dve.wait_ge(s["iota_done"], 1)
            own.sign(dve.tensor_copy(ioh[:], ioi[:]))
            own.sign(dve.tensor_copy(k.iota8[:], ioi[:, 0:8]))
            dve.wait_ge(s["edges_loaded"], 32)
            own.link(dve.tensor_copy(ef[:], ei[:]))
            dve.sem_inc(s["onehot_used"], G)

            def onehots(i):
                for g in range(G):
                    dve.wait_ge(s["onehot_used"], i * G + (g + 1))
                    for side in range(2):
                        dve.tensor_scalar(oh[:, g, side, 0:N], ioh[0:T, :], ef[:, side, bass.ds(i * G + g, 1)],
                                          None, ALU.is_equal).then_inc(s["onehot_ready"], 1)

            with dve.Fori(0, EC // G - NT) as i:
                onehots(i)
            dve.wait_ge(s["x_loaded"], 16)
            for t in range(NT):
                onehots(EC // G - NT + t)
                norm.variance(dve, t, 0, own)
                norm.apply(dve, t, 0, own)
            dve.wait_ge(s["counted"], 1)
            for c in range(NT):
                dve.tensor_copy(k.C[:, c, 0:512], main(c)).then_inc(s["evacuated"], 1)
                dve.tensor_copy(k.C[:, c, 512:N], rest(c)).then_inc(s["evacuated"], 1)
            for d in range(NT):
                dve.wait_ge(s["turned"], d + 1)
                dve.tensor_scalar(k.MASK[:, d, :], k.slot(d % 3)[0:T, TR:TR + N], 0.5, LOW, ALU.is_lt,
                                  ALU.mult).then_inc(s["mask_done"], 1)

        @block.scalar
        def _(act):
            act.wait_ge(s["const_done"], 2)
            for t in range(NT):
                norm.act_std(act, t)
            for t in range(NT):
                norm.act_hi(act, t)

        @block.tensor
        def _(pe):
            pe.wait_ge(s["cleared"], 1)
            for b in range(7):
                pe.matmul(k.bank(b)[0:T, :], zero[:, 0:T], zero[:], start=True, stop=False, skip_group_check=True)
            with pe.Fori(0, EC // G) as i:
                for g in range(G):
                    pe.wait_ge(s["onehot_ready"], i * (2 * G) + (2 * g + 2))
                    for c in range(NT):
                        for out, a, b in ((main(c), 0, 512), (rest(c), 512, N)):
                            last = pe.matmul(out, oh[:, g, 0, cols(c)], oh[:, g, 1, a:b], start=False, stop=False,
                                             skip_group_check=True)
                    last.then_inc(s["onehot_used"], 1)
            pe.matmul(k.bank(6)[0:T, :], zero[:, 0:T], zero[:], start=False, stop=True,
                      skip_group_check=True).then_inc(s["counted"], 1)
            pe.wait_ge(s["ident_done"], 1)
            pe.wait_ge(s["const_done"], 1)
            pe.wait_ge(s["evacuated"], 2 * NT)
            for d in range(NT):
                if d >= 3:
                    pe.wait_ge(s["mask_done"], d - 2)
                for c in range(NT):
                    last = pe.transpose(k.slot(d % 3)[0:T, TR + c * T:TR + (c + 1) * T], k.C[:, c, cols(d)],
                                        k.ident[0:T, 0:T])
                last.then_inc(s["turned"], 1)
            for t in range(NT):
                norm.pe(pe, t)


class Split:

    def __init__(self, k, mem, name, shape):
        self.hi, self.lo = k.sb(mem, name + "_hi", shape, F32R), k.sb(mem, name + "_lo", shape, F32R)

    def at(self, *index):
        return self.hi[index], self.lo[index]


def passes(lhsT, rhs):
    return [(lhsT[0], rhs[0]), (lhsT[0], rhs[1]), (lhsT[1], rhs[0])]


def low_part(dve, out, x, hi):
    return dve.tensor_tensor(out, x, hi.bitcast(F32), ALU.subtract)


def unit_pieces(unit):
    return len(unit[0]) if isinstance(unit[0], list) else 1


def load_unit(sp, buf, unit, sem):
    src, (blocks, width) = unit
    out = buf[:, 0:blocks * width].rearrange("p (a b) -> p a b", b=width)
    for a, b, piece in src if isinstance(src, list) else [(0, width, src)]:
        sp.dma_start(out[:, :, a:b], piece).then_inc(sem, 16)


class Ring:

    def __init__(self, k, mem, loaded, plan):
        self.whole = [k.sb(mem, "unit", [P, UNIT]) for _ in range(RING)]
        self.loaded, self.plan, self.number, self.ahead = loaded, plan, 0, 0
        self.counts = [0] * RING

    def enter(self, units):
        before, here = list(self.counts), self.ahead
        for r in range(RING):
            self.counts[r] += sum(unit_pieces(u) for u in units[r::RING])
        self.number, self.ahead = self.number + 1, 0
        return before, here

    def coming(self):
        return self.number < len(self.plan)

    def load_first(self, sp):
        for n in range(RING):
            load_unit(sp, self.whole[n], self.plan[self.number][n], self.loaded[n])
        self.ahead = RING


class Stream:

    SEMS = " unit_loaded0 unit_loaded1 unit_loaded2 unit_loaded3 unit_hi_made unit_lo_made unit_used"

    def __init__(self, k, mem, s, units, width=UNIT):
        self.k, self.units, self.ring = k, units, k.ring
        self.hi_made, self.lo_made, self.used = s["unit_hi_made"], s["unit_lo_made"], s["unit_used"]
        if k.ring is None:
            self.whole = [k.sb(mem, "unit", [P, width]) for _ in range(RING)]
            self.loaded = [s["unit_loaded0"], s["unit_loaded1"], s["unit_loaded2"], s["unit_loaded3"]]
            self.before, self.here = [0] * RING, 0
        else:
            self.whole, self.loaded = k.ring.whole, k.ring.loaded
            self.before, self.here = k.ring.enter(units)
        self.split = [Split(k, mem, "unit", [P, width]) for _ in range(RING)]

    def view(self, buf, n):
        dims = self.units[n][1]
        flat = buf[:, 0:dims[0] * dims[1]]
        return flat.rearrange("p (a b) -> p a b", b=dims[1])

    def load(self, sp, first=0, end=None):
        for n in range(max(first, self.here), len(self.units) if end is None else end):
            if n >= RING:
                sp.wait_ge(self.hi_made, n - RING + 1)
                sp.wait_ge(self.lo_made, n - RING + 1)
            load_unit(sp, self.whole[n % RING], self.units[n], self.loaded[n % RING])
        if end is None and self.ring is not None and self.ring.coming():
            sp.wait_ge(self.hi_made, len(self.units))
            sp.wait_ge(self.lo_made, len(self.units))
            self.ring.load_first(sp)

    def pieces(self, n):
        return self.before[n % RING] + sum(unit_pieces(u) for u in self.units[n % RING:n + 1:RING])

    def width(self, n):
        return self.units[n][1][0] * self.units[n][1][1]

    def hi(self, act, n):
        act.wait_ge(self.loaded[n % RING], 16 * self.pieces(n))
        if n >= RING:
            act.wait_ge(self.used, n - RING + 1)
        w = self.width(n)
        act.activation(self.split[n % RING].hi[:, 0:w], self.whole[n % RING][:, 0:w], ACT.Copy).then_inc(self.hi_made, 1)

    def lo(self, dve, n):
        dve.wait_ge(self.hi_made, n + 1)
        w, r = self.width(n), n % RING
        low_part(dve, self.split[r].lo[:, 0:w], self.whole[r][:, 0:w], self.split[r].hi[:, 0:w]).then_inc(self.lo_made, 1)

    def ready(self, pe, n):
        pe.wait_ge(self.lo_made, n + 1)

    def part(self, n, a, cols_):
        r = n % RING
        return tuple(self.view(x, n)[:, a, cols_] for x in (self.split[r].hi, self.split[r].lo))


def feature_units(w, c0, c1):
    v = w.rearrange("(k p) n -> p k n", p=P)
    return [(v[:, :, c * P:(c + 1) * P], (v.shape[1], P)) for c in range(c0, c1)]


def node_units(w, width, per):
    v = w.rearrange("(k p) n -> p k n", p=P)
    return [(v[:, c:c + per, b:b + width], (per, width))
            for b in range(0, w.shape[1], width) for c in range(0, v.shape[1], per)]


def wide3(pe, slot, parts, operands):
    for a, n in RHALVES:
        last = product(pe, slot[0:parts, MM + a:MM + a + n],
                       [p for lhsT, rhs in operands(slice(a, a + n)) for p in passes(lhsT, rhs)])
    return last


class Norm:

    SEMS = " n_own n_var n_std n_normed n_turned n_affine n_hi n_lo n_loaded"

    def __init__(self, k, mem, s, src, out, slot, scale=None, shift=None, again=False, split=False):
        self.k, self.s, self.src, self.slot, self.split = k, s, src, slot, split
        self.out = k.sb(mem, "normed", [T, NT, D]) if out is None else out
        self.again = k.sb(mem, "normed_again", [T, NT, D]) if again else None
        self.stats = k.sb(mem, "stats", [T, NT, 2, 2, 6])
        self.mv = k.sb(mem, "mean_var", [T, NT, 2, 2])
        self.std = k.sb(mem, "std", [T, NT, 2, 2])
        self.affine = scale is not None
        self.rounds = 2 if again else 1
        if self.affine:
            self.scale, self.shift = scale, shift
            self.wb = k.sb(mem, "scale_shift", [P, 2, KD])
            self.tmp = [k.sb(mem, "affine", [P, KD, T]) for _ in range(2)]
        self.order = [(step - n, n) for step in range(NT + 1) for n in range(self.rounds) if 0 <= step - n < NT]

    def sp(self, sp):
        if self.affine:
            sp.dma_start(self.wb[:, 0, :], self.scale).then_inc(self.s["n_loaded"], 16)
            sp.dma_start(self.wb[:, 1, :], self.shift).then_inc(self.s["n_loaded"], 16)

    def psum(self):
        return self.k.slot(self.slot)[:, TC:TC + KD * T].rearrange("p (c n) -> p c n", n=T)

    def sources(self, n):
        return (self.src, self.out) if n == 0 else (self.out, self.again)

    def variance(self, dve, t, n, own):
        src = self.sources(n)[0]
        for h in range(2):
            own.sign(dve.bn_stats(self.stats[:, t, n, h, :], src[:, t, h * 384:(h + 1) * 384]))
        own.wait()
        dve.bn_aggr(self.mv[:, t, n, :], self.stats[:, t, n, :, :].rearrange("p a b -> p (a b)")
                    ).then_inc(self.s["n_var"], 1)

    def apply(self, dve, t, n, own):
        src, out = self.sources(n)
        dve.wait_ge(self.s["n_std"], self.order.index((t, n)) + 1)
        own.link(dve.reciprocal(self.std[:, t, n, 1:2], self.std[:, t, n, 0:1]))
        own.link(dve.tensor_scalar(out[:, t, :], src[:, t, :], self.mv[:, t, n, 0:1], self.std[:, t, n, 1:2],
                                   ALU.subtract, ALU.mult))
        if n == self.rounds - 1:
            dve.sem_inc(self.s["n_normed"], 1)

    def act_std(self, act, number):
        t, n = self.order[number]
        act.wait_ge(self.s["n_var"], number + 1)
        act.activation(self.std[:, t, n, 0:1], self.mv[:, t, n, 1:2], ACT.Sqrt, bias=self.k.eps[0:T, 0:1]
                       ).then_inc(self.s["n_std"], 1)

    def pe(self, pe, t):
        pe.wait_ge(self.s["n_normed"], t + 1)
        if t >= 1:
            pe.wait_ge(self.s["n_hi"], t)
            if self.split and not self.affine:
                pe.wait_ge(self.s["n_lo"], t)
        src = self.out if self.again is None else self.again
        for c in range(KD):
            last = pe.transpose(self.psum()[:, c, :], src[:, t, c * P:(c + 1) * P], self.k.ident[0:T, 0:T])
        last.then_inc(self.s["n_turned"], 1)

    def act_hi(self, act, t):
        act.wait_ge(self.s["n_turned"], t + 1)
        x = self.psum()
        if not self.split:
            act.activation(self.k.XTF[:, :, cols(t)], x, ACT.Copy).then_inc(self.s["n_hi"], 1)
            return
        if self.affine:
            if t == 0:
                act.wait_ge(self.s["n_loaded"], 32)
            if t >= 2:
                act.wait_ge(self.s["n_lo"], t - 1)
            for c in range(KD):
                act.activation(self.tmp[t % 2][:, c, :], x[:, c, :], ACT.Identity, bias=self.wb[:, 1, c:c + 1],
                               scale=self.wb[:, 0, c:c + 1]).then_inc(self.s["n_affine"], 1)
            act.wait_ge(self.s["n_affine"], KD * (t + 1))
            x = self.tmp[t % 2][:]
        act.activation(self.k.XT.hi[:, :, cols(t)], x, ACT.Copy).then_inc(self.s["n_hi"], 1)

    def dve_lo(self, dve, t):
        if self.split and not self.affine:
            self.lo(dve, t, self.psum())

    def pool_lo(self, pool, t):
        if self.affine:
            self.lo(pool, t, self.tmp[t % 2][:])

    def lo(self, eng, t, x):
        eng.wait_ge(self.s["n_hi"], t + 1)
        low_part(eng, self.k.XT.lo[:, :, cols(t)], x, self.k.XT.hi[:, :, cols(t)]).then_inc(self.s["n_lo"], 1)

    def tail_dve(self, dve, own, tile):
        for step in range(NT + self.rounds + 1):
            if step < NT:
                tile(step)
                self.variance(dve, step, 0, own)
            for n in range(self.rounds):
                t = step - 1 - n
                if 0 <= t < NT:
                    self.apply(dve, t, n, own)
                    if n + 1 < self.rounds:
                        self.variance(dve, t, n + 1, own)
            if step > self.rounds:
                self.dve_lo(dve, step - 1 - self.rounds)

    def tail_act(self, act):
        number = 0
        for step in range(NT + self.rounds):
            for t, n in self.order:
                if t + n == step:
                    self.act_std(act, number)
                    number += 1
            if step >= self.rounds:
                self.act_hi(act, step - self.rounds)

    def tail_pe(self, pe, tile):
        for step in range(NT + self.rounds + 1):
            if step < NT:
                tile(step)
            if step > self.rounds:
                self.pe(pe, step - 1 - self.rounds)


class NoNorm:

    SEMS = ""

    def sp(self, sp):
        pass

    def tail_dve(self, dve, own, tile):
        for t in range(NT):
            tile(t)

    def tail_act(self, act):
        pass

    def tail_pe(self, pe, tile):
        for t in range(NT):
            tile(t)


def layer_norm(k, norm_args):
    nc = k.nc
    with ExitStack() as mem, k.stage(Norm.SEMS) as s, nc.Block() as block:
        norm = Norm(k, mem, s, **norm_args)

        @block.sync
        def _(sp):
            norm.sp(sp)

        @block.vector
        def _(dve):
            norm.tail_dve(dve, Own(dve, s["n_own"]), lambda t: None)

        @block.gpsimd
        def _(pool):
            for t in range(NT):
                norm.pool_lo(pool, t)

        @block.scalar
        def _(act):
            norm.tail_act(act)

        @block.tensor
        def _(pe):
            norm.tail_pe(pe, lambda t: None)


def rows_out(k, block, vec, R, dram, ready, turned, moved, stored, need=1):
    rows = k.rows

    def pe_part(pe):
        pe.wait_ge(ready, need)
        for t in range(NT):
            last = pe.transpose(k.slot(3)[0:R, TR + t * T:TR + (t + 1) * T], vec[:, t, :], k.ident[0:T, 0:T])
        last.then_inc(turned, 1)

    def dve_part(dve):
        dve.wait_ge(turned, 1)
        dve.tensor_copy(rows[0:R, :], k.slot(3)[0:R, TR:TR + N]).then_inc(moved, 1)

    def sp_part(sp):
        sp.wait_ge(moved, 1)
        sp.dma_start(dram, rows[0:R, :]).then_inc(stored, 16)
        sp.wait_ge(stored, 16)

    return pe_part, dve_part, sp_part


def add_loops(k):
    nc = k.nc
    with ExitStack() as mem, k.sems("own_dve looped deg_ready inverted rooted") as (
            own_dve, looped, deg_ready, inverted, rooted), nc.Block() as block:
        inv = k.sb(mem, "inverse_degree", [T, NT])
        off = k.sb(mem, "off_diagonal", [T, T])

        @block.sync
        def _(sp):
            if k.ring.coming():
                k.ring.load_first(sp)

        @block.vector
        def _(dve):
            own = Own(dve, own_dve)
            own.link(dve.tensor_scalar(off[:], k.ident[0:T, 0:T], -1.0, 1.0, ALU.mult, ALU.add))
            for s in range(NT):
                dve.tensor_tensor(k.C[:, s, cols(s)], k.C[:, s, cols(s)], k.ident[0:T, 0:T], ALU.add
                                  ).then_inc(looped, 1)
                own.sign(dve.tensor_tensor(k.MASK[:, s, cols(s)], k.MASK[:, s, cols(s)], off[:], ALU.mult))
            dve.wait_ge(deg_ready, 1)
            dve.reciprocal(inv[:], k.bank(7)[0:T, 0:NT]).then_inc(inverted, 1)

        @block.scalar
        def _(act):
            act.wait_ge(inverted, 1)
            act.activation(k.dinv[:], inv[:], ACT.Sqrt).then_inc(rooted, 1)

        @block.tensor
        def _(pe):
            pe.wait_ge(looped, NT)
            for d in range(NT):
                for s in range(NT):
                    last = pe.matmul(k.bank(7)[0:T, d:d + 1], k.C[:, s, cols(d)], k.ones[0:T, 0:1],
                                     start=(s == 0), stop=(s == NT - 1))
            last.then_inc(deg_ready, 1)


def gat_max(k, H, A12, a1_dram, r_dram, B1, B8):
    nc = k.nc
    with ExitStack() as mem, k.sems(
            "row_loaded0 row_loaded1 maxed own_dve rows_ready turned moved stored") as (
            row_loaded0, row_loaded1, maxed, own_dve, rows_ready, turned, moved, stored), nc.Block() as block:
        row_loaded = [row_loaded0, row_loaded1]
        row = [k.sb(mem, "a1_row", [T, N]) for _ in range(2)]
        junk = k.sb(mem, "masked", [T, 2, N])
        M = k.sb(mem, "max_a1", [T, NT, H])
        m = k.sb(mem, "leaky_max", [T, NT, H])
        R = k.sb(mem, "score_rows", [T, NT, 2 * H])
        a1, a2 = A12[:, :, 0:H], A12[:, :, H:2 * H]
        pe_part, dve_part, sp_part = rows_out(k, block, R, 2 * H, r_dram, rows_ready, turned, moved, stored, need=2)

        @block.sync
        def _(sp):
            for h in range(H):
                if h >= 2:
                    sp.wait_ge(maxed, NT * (h - 1))
                sp.dma_start(row[h % 2][:], a1_dram[h:h + 1, :].to_broadcast([T, N])).then_inc(row_loaded[h % 2], 16)
            sp_part(sp)

        @block.vector
        def _(dve):
            own = Own(dve, own_dve)
            for h in range(H):
                dve.wait_ge(row_loaded[h % 2], 16 * (h // 2 + 1))
                for d in range(NT):
                    n = NT * h + d
                    if n >= 2:
                        dve.wait_ge(maxed, n - 1)
                    dve.tensor_tensor_reduce(junk[:, n % 2, :], row[h % 2][:], k.MASK[:, d, :], 1.0, -3e38,
                                             ALU.add, ALU.max, M[:, d, h:h + 1]).then_inc(maxed, 1)
            dve.wait_ge(maxed, NT * H)
            own.link(dve.tensor_tensor(M[:], M[:], a2, ALU.add))
            own.link(dve.scalar_tensor_tensor(m[:], M[:], SLOPE, M[:], ALU.mult, ALU.max))
            dve.tensor_tensor(R[:, :, 0:H], a2, m[:], ALU.subtract).then_inc(rows_ready, 1)
            dve.scalar_tensor_tensor(R[:, :, H:2 * H], a2, SLOPE, m[:], ALU.mult, ALU.subtract).then_inc(rows_ready, 1)
            own.sign(dve.tensor_scalar(B1[:], a1, SLOPE, None, ALU.mult))
            own.link(dve.tensor_scalar(B8[:], a1, 1 - SLOPE, None, ALU.mult))
            dve_part(dve)

        @block.tensor
        def _(pe):
            pe_part(pe)


class GatWeights:

    SEMS = " rows_loaded0 rows_loaded1 rows_loaded2 z_ready e_ready p_dve p_pool"

    def __init__(self, k, mem, s, r_dram, H, B1, B8, ring, rows_ring=None, on_dve=1):
        self.k, self.s, self.B1, self.B8, self.ring = k, s, B1, B8, ring
        self.rows_ring = rows_ring or ring
        self.on_dve = on_dve
        self.r_v = r_dram.rearrange("(two h) n -> h two n", two=2)
        self.rows = [k.sb(mem, "rows", [T, 2, N]) for _ in range(self.rows_ring)]
        self.PB = [k.sb(mem, "weights", [T, NT, N]) for _ in range(ring)]
        self.rows_loaded = [s["rows_loaded0"], s["rows_loaded1"], s["rows_loaded2"]]

    def load(self, sp, h, b, wait=True):
        if wait:
            sp.wait_ge(self.s["z_ready"], (h - (self.rows_ring - 1)) * NT)
        sp.dma_start(self.rows[b][:], self.r_v[h, :, :].partition_broadcast(T)).then_inc(self.rows_loaded[b], 16)

    def maxima(self, dve, h, b, round_no, rb=None):
        rb = b if rb is None else rb
        dve.wait_ge(self.rows_loaded[rb], round_no * 16)
        rows = self.rows[rb]
        for c in range(NT):
            dve.scalar_tensor_tensor(self.PB[b][:, c, :], rows[:, 0, :], self.B8[:, c, bass.ds(h, 1)], rows[:, 1, :],
                                     ALU.add, ALU.max).then_inc(self.s["z_ready"], 1)

    def exps(self, act, h, b):
        for c in range(NT):
            act.wait_ge(self.s["z_ready"], h * NT + (c + 1))
            act.activation(self.PB[b][:, c, :], self.PB[b][:, c, :], ACT.Exp, bias=self.B1[:, c, bass.ds(h, 1)]
                           ).then_inc(self.s["e_ready"], 1)

    def counts(self, eng, h, b, tiles, sem):
        for c in tiles:
            eng.wait_ge(self.s["e_ready"], h * NT + (c + 1))
            eng.tensor_tensor(self.PB[b][:, c, :], self.PB[b][:, c, :], self.k.C[:, c, :], ALU.mult).then_inc(sem, 1)

    def counts_dve(self, dve, h, b):
        self.counts(dve, h, b, range(self.on_dve), self.s["p_dve"])

    def counts_pool(self, pool, h, b):
        self.counts(pool, h, b, range(self.on_dve, NT), self.s["p_pool"])

    def ready_tile(self, pe, c):
        if c < self.on_dve:
            pe.wait_ge(self.s["p_dve"], c + 1)
        else:
            pe.wait_ge(self.s["p_pool"], c - self.on_dve + 1)

    def ready(self, pe, h):
        pe.wait_ge(self.s["p_dve"], h * self.on_dve + self.on_dve)
        pe.wait_ge(self.s["p_pool"], h * (NT - self.on_dve) + (NT - self.on_dve))


def l0_gnn(k, W, al, ar, Wr, norm_args):
    nc, H, HD = k.nc, 12, 64
    a1_dram, r_dram = k.dram("l0_a", [2 * H, N]), k.dram("l0_r", [2 * H, N])
    with ExitStack() as mem:
        FTX = k.sb(mem, "ft", [T, NT, H + 1, HD + 1])
        A12 = k.sb(mem, "a12", [T, NT, 2 * H])
        B1 = k.sb(mem, "a1_times_slope", [T, NT, H])
        B8 = k.sb(mem, "a1_rest", [T, NT, H])
        Wbd = k.sb(mem, "w_blocks", [P, 2, P])
        with ExitStack() as tmp, k.sems(
                "cleared loaded attn_loaded product_done ft_moved scored own_dve weighed turned moved stored") as (
                cleared, loaded, attn_loaded, product_done, ft_moved, scored, own_dve, weighed, turned, moved, stored), \
                nc.Block() as block:
            attn = k.sb(tmp, "attn", [T, 2, D])
            prod = [k.sb(tmp, "prod", [T, 2, D]) for _ in range(2)]

            def weigh(eng, t, n):
                return eng.tensor_tensor(prod[t % 2][:, n, :].rearrange("p (h e) -> p h e", e=HD), FTX[:, t, 0:H, 0:HD],
                                         attn[:, n, :].rearrange("p (h e) -> p h e", e=HD), ALU.mult)

            pe_part, dve_part, sp_part = rows_out(k, block, A12, 2 * H, a1_dram, scored, turned, moved, stored,
                                                  need=2 * NT)

            @block.gpsimd
            def _(pool):
                pool.memset(Wbd[:], 0.0).then_inc(cleared, 1)
                pool.memset(FTX[:, :, 0:H, HD:HD + 1], 1.0).then_inc(cleared, 1)
                pool.memset(FTX[:, :, H, :], 0.0).then_inc(cleared, 1)
                pool.wait_ge(attn_loaded, 32)
                for t in range(NT):
                    pool.wait_ge(ft_moved, t + 1)
                    if t >= 2:
                        pool.wait_ge(scored, 2 * t - 2)
                    weigh(pool, t, 1).then_inc(weighed, 1)

            @block.sync
            def _(sp):
                sp.dma_start(attn[:, 0, :], row_of(al, T)).then_inc(attn_loaded, 16)
                sp.dma_start(attn[:, 1, :], row_of(ar, T)).then_inc(attn_loaded, 16)
                sp.wait_ge(cleared, 3)
                for n, w in enumerate((W, Wr)):
                    for b in range(2):
                        sp.dma_start(Wbd[b * HD:(b + 1) * HD, n, b * HD:(b + 1) * HD], w).then_inc(loaded, 16)
                sp_part(sp)

            @block.tensor
            def _(pe):
                pe.wait_ge(loaded, 64)
                for t in range(NT):
                    if t >= 3:
                        pe.wait_ge(ft_moved, t - 2)
                    for c in range(KD):
                        last = pe.matmul(k.bank(2 * (t % 3) + c // 3)[0:T, (c % 3) * P:(c % 3 + 1) * P],
                                         k.XTF[:, c, cols(t)], Wbd[:, 0, :], start=True, stop=True)
                    last.then_inc(product_done, 1)
                pe_part(pe)

            @block.scalar
            def _(act):
                for t in range(NT):
                    act.wait_ge(product_done, t + 1)
                    out = FTX[:, t, 0:H, 0:HD].rearrange("p (b h) e -> p b h e", b=2)
                    pv = k.slot(t % 3)[0:T].rearrange("p (b n) -> p b n", b=2)[:, :, 0:384]
                    for b in range(2):
                        ins = act.activation(out[:, b], pv[:, b].rearrange("p (h e) -> p h e", e=HD), ACT.Copy)
                    ins.then_inc(ft_moved, 1)

            @block.vector
            def _(dve):
                own = Own(dve, own_dve)
                dve.wait_ge(attn_loaded, 32)
                for t in range(NT):
                    dve.wait_ge(ft_moved, t + 1)
                    own.link(weigh(dve, t, 0))
                    for n in range(2):
                        if n == 1:
                            dve.wait_ge(weighed, t + 1)
                        dve.tensor_reduce(A12[:, t, n * H:(n + 1) * H],
                                          prod[t % 2][:, n, :].rearrange("p (h e) -> p h e", e=HD), AX.X,
                                          ALU.add).then_inc(scored, 1)
                dve_part(dve)

        gat_max(k, H, A12, a1_dram, r_dram, B1, B8)

        R = 3
        with ExitStack() as tmp, k.stage("own_dve agg_done agg_free res_done res_used" + GatWeights.SEMS + Norm.SEMS
                                         ) as s, nc.Block() as block:
            norm = Norm(k, tmp, s, **norm_args)
            gat = GatWeights(k, tmp, s, r_dram, H, B1, B8, R)
            den = k.sb(tmp, "den", [T, NT, 1])
            W2 = 2 * (HD + 1)

            def sums(b):
                return k.slot(b)[0:T, 512 - 3 * W2:512 + 2 * W2].rearrange("p (t e) -> p t e", e=W2)

            agg = k.XN

            @block.sync
            def _(sp):
                for b in range(R):
                    gat.load(sp, b, b, wait=False)
                with sp.Fori(1, H // R) as i:
                    for b in range(R):
                        gat.load(sp, i * R + b, b)

            @block.scalar
            def _(act):
                with act.Fori(0, H // R) as i:
                    for b in range(R):
                        gat.exps(act, i * R + b, b)
                norm.tail_act(act)

            @block.gpsimd
            def _(pool):
                with pool.Fori(0, H // R) as i:
                    for b in range(R):
                        gat.counts_pool(pool, i * R + b, b)

            @block.vector
            def _(dve):
                own = Own(dve, s["own_dve"])
                dve.sem_inc(s["agg_free"], R)

                def normalise(h, b):
                    dve.wait_ge(s["agg_done"], h + 1)
                    o = sums(b)
                    own.link(dve.tensor_scalar(den[:], o[:, :, HD:HD + 1], 1e-16, None, ALU.max))
                    own.link(dve.reciprocal(den[:], den[:]))
                    own.link(dve.tensor_tensor(agg[:, :, bass.ds(h * HD, HD)], o[:, :, 0:HD],
                                               den[:].to_broadcast([T, NT, HD]), ALU.mult))
                    dve.sem_inc(s["agg_free"], 1)

                gat.maxima(dve, 0, 0, 1)
                gat.maxima(dve, 1, 1, 1)
                gat.counts_dve(dve, 0, 0)
                with own.loop(H // R - 1, R * 3) as i:
                    for j in range(1, R + 1):
                        gat.maxima(dve, i * R + (j + 1), (j + 1) % R, i + 1 + (j + 1) // R)
                        gat.counts_dve(dve, i * R + j, j % R)
                        normalise(i * R + (j - 1), j - 1)
                gat.maxima(dve, H - 1, (H - 1) % R, H // R)
                gat.counts_dve(dve, H - 2, (H - 2) % R)
                normalise(H - 3, (H - 3) % R)
                gat.counts_dve(dve, H - 1, (H - 1) % R)
                normalise(H - 2, (H - 2) % R)
                normalise(H - 1, (H - 1) % R)

                def tile(t):
                    dve.wait_ge(s["res_done"], t + 1)
                    r = k.slot(1 + t % 3)[0:T].rearrange("p (b n) -> p b n", b=2)[:, :, 0:384]
                    a = agg[:, t, :].rearrange("p (b n) -> p b n", b=2)
                    own.link(dve.tensor_tensor(a, a, r, ALU.add))
                    dve.sem_inc(s["res_used"], 1)
                    own.link(dve.scalar_tensor_tensor(k.X[:, t, :], agg[:, t, :], 0.0, k.X[:, t, :], ALU.max, ALU.add))

                norm.tail_dve(dve, own, tile)

            @block.tensor
            def _(pe):
                with pe.Fori(0, H // R) as i:
                    for b in range(R):
                        gat.ready(pe, i * R + b)
                        pe.wait_ge(s["agg_free"], i * R + (b + 1))
                        for d in range(NT):
                            for c in range(NT):
                                last = pe.matmul(sums(b)[:, d, :],
                                                 gat.PB[b][:, c, cols(d)], FTX[:, c, bass.ds(i * R + b, 2), :].rearrange("p a e -> p (a e)"),
                                                 start=(c == 0), stop=(c == NT - 1))
                        last.then_inc(s["agg_done"], 1)

                def tile(t):
                    if t == 0:
                        pe.wait_ge(s["agg_free"], H + R)
                    if t >= 3:
                        pe.wait_ge(s["res_used"], t - 2)
                    for c in range(KD):
                        last = pe.matmul(k.bank(2 + 2 * (t % 3) + c // 3)[0:T, (c % 3) * P:(c % 3 + 1) * P],
                                         k.XTF[:, c, cols(t)], Wbd[:, 1, :], start=True, stop=True)
                    last.then_inc(s["res_done"], 1)

                norm.tail_pe(pe, tile)


def product(pe, out, pairs):
    for n, (lhsT, rhs) in enumerate(pairs):
        last = pe.matmul(out, lhsT, rhs, start=(n == 0), stop=(n == len(pairs) - 1), skip_group_check=True)
    return last


def wide(pe, slot, parts, pairs):
    for a, n in HALVES:
        last = product(pe, slot[0:parts, MM + a:MM + a + n], pairs(a, n))
    return last


def halves(ap):
    return ap.rearrange("p (b n) -> p b n", b=2)[:, :, 0:384]


def split(ap):
    return ap.rearrange("p (b n) -> p b n", b=2)


def split_counts(k, pool, own, C):
    own.link(pool.tensor_copy(C.hi[:, :, N:NP], k.zero[0:T, 0:NT, :]))
    own.link(pool.tensor_copy(C.lo[:, :, N:NP], k.zero[0:T, 0:NT, :]))
    for c in range(NT):
        own.link(pool.tensor_copy(C.hi[:, c, 0:N], k.C[:, c, :]))
        own.link(pool.tensor_tensor(C.lo[:, c, 0:N], k.C[:, c, :], C.hi[:, c, 0:N].bitcast(F32), ALU.subtract))


def split_rows_hi(k, act, h, done, h_hi, base=0):
    for n in range(2 * NT):
        act.wait_ge(done, base + n + 1)
        act.activation(h.hi[:, n % NT, n // NT * 384:(n // NT + 1) * 384], row_bank(k, n // NT, n % NT), ACT.Copy,
                       scale=k.dinv[:, n % NT:n % NT + 1]).then_inc(h_hi, 1)


def split_rows_lo(k, dve, h, h_hi, h_ready, base=0):
    for n in range(2 * NT):
        dve.wait_ge(h_hi, base + n + 1)
        o = slice(n // NT * 384, (n // NT + 1) * 384)
        dve.scalar_tensor_tensor(h.lo[:, n % NT, o], row_bank(k, n // NT, n % NT), k.dinv[:, n % NT:n % NT + 1],
                                 h.hi[:, n % NT, o].bitcast(F32), ALU.mult, ALU.subtract).then_inc(h_ready, 1)


def gcn_tile(pe, slot, C, h, d):
    for b in range(2):
        last = product(pe, slot[0:T, b * 512:b * 512 + 384],
                       [p for c in range(NT) for p in passes(C.at(slice(None), c, cols(d)),
                                                             h.at(slice(None), c, slice(b * 384, (b + 1) * 384)))])
    return last


def row_bank(k, b, t):
    return k.bank((5 * b + t) % 8)[0:T, 0:384]


def rows_product(pe, st, units, X, moved, done, base=0):

    def before(b, t):
        if b == 1 and t >= 3:
            pe.wait_ge(moved, base + t - 2)

    def tiles(tile):
        for t in range(NT):
            tile(t)

    node_major(pe, st, units, 2, tiles, lambda b, t: row_bank(st.k, b, t), lambda c, t: X.at(slice(None), c, cols(t)),
               before, done, base=base)


def l1_gnn(k, W, bias, norm_args):
    nc = k.nc
    with ExitStack() as mem, k.stage(
            "bias_loaded product_done h_ready agg_done used own_dve biased own_pool h_hi counts_split" + Stream.SEMS + Norm.SEMS) as s, \
            nc.Block() as block:
        norm = Norm(k, mem, s, **norm_args)
        st = Stream(k, mem, s, node_units(W, 384, 2))
        row = k.sb(mem, "bias_row", [T, D])
        h = Split(k, mem, "h", [T, NT, D])
        C = Split(k, mem, "counts", [T, NT, NP])

        @block.sync
        def _(sp):
            st.load(sp, 0, RING)
            sp.dma_start(row[:], row_of(bias, T)).then_inc(s["bias_loaded"], 16)
            norm.sp(sp)
            st.load(sp, RING)

        @block.tensor
        def _(pe):
            rows_product(pe, st, range(len(st.units)), k.XT, s["h_ready"], s["product_done"])
            pe.wait_ge(s["h_ready"], 2 * NT)
            pe.wait_ge(s["counts_split"], 1)

            def tile(d):
                if d >= 3:
                    pe.wait_ge(s["used"], d - 2)
                gcn_tile(pe, k.slot(d % 3), C, h, d).then_inc(s["agg_done"], 1)

            norm.tail_pe(pe, tile)

        @block.gpsimd
        def _(pool):
            split_counts(k, pool, Own(pool, s["own_pool"]), C)
            pool.sem_inc(s["counts_split"], 1)
            pool.wait_ge(s["bias_loaded"], 16)
            for t in range(NT):
                pool.tensor_tensor(k.X[:, t, :], k.X[:, t, :], row[:], ALU.add).then_inc(s["biased"], 1)
            for t in range(NT):
                norm.pool_lo(pool, t)

        @block.scalar
        def _(act):
            for n in range(len(st.units)):
                st.hi(act, n)
            split_rows_hi(k, act, h, s["product_done"], s["h_hi"])
            norm.tail_act(act)

        @block.vector
        def _(dve):
            own = Own(dve, s["own_dve"])
            for n in range(len(st.units)):
                st.lo(dve, n)
            split_rows_lo(k, dve, h, s["h_hi"], s["h_ready"])

            def tile(d):
                dve.wait_ge(s["agg_done"], d + 1)
                dve.wait_ge(s["biased"], d + 1)
                x = split(k.X[:, d, :])
                own.link(dve.scalar_tensor_tensor(x, halves(k.slot(d % 3)[0:T]), k.dinv[:, d:d + 1], x, ALU.mult,
                                                  ALU.add))
                dve.sem_inc(s["used"], 1)

            norm.tail_dve(dve, own, tile)


def l2_gnn(k, W1, b1, W2, b2, norm_args):
    nc = k.nc
    dinv_dram = k.dram("dinv_row", [1, N])
    with ExitStack() as mem, k.stage(
            "bias_loaded product_done h_ready agg_done agg_used used own_dve biased turned moved "
            "stored row_loaded activated relu_done z_lo own_pool h_hi counts_split" + Stream.SEMS + Norm.SEMS) as s, nc.Block() as block:
        norm = Norm(k, mem, s, **norm_args)
        st = Stream(k, mem, s, node_units(W1, 384, 2) + node_units(W2, 384, 2))
        UC = len(st.units) // 2
        b1c = k.sb(mem, "b1_column", [P, KD])
        row = k.sb(mem, "bias_row", [T, D])
        h = Split(k, mem, "h", [T, NT, D])
        C = Split(k, mem, "counts", [T, NT, NP])
        dr = k.sb(mem, "dinv_row", [P, N])
        z = [k.sb(mem, "z", [P, N]) for _ in range(2)]
        zT = k.XT

        @block.sync
        def _(sp):
            st.load(sp, 0, RING)
            sp.dma_start(row[:], row_of(b2, T)).then_inc(s["bias_loaded"], 16)
            sp.dma_start(b1c[:], b1).then_inc(s["bias_loaded"], 16)
            sp.wait_ge(s["moved"], 1)
            sp.dma_start(dinv_dram, k.rows[0:1, :]).then_inc(s["stored"], 16)
            sp.wait_ge(s["stored"], 16)
            sp.dma_start(dr[:], dinv_dram.to_broadcast([P, N])).then_inc(s["row_loaded"], 16)
            st.load(sp, RING)

        @block.gpsimd
        def _(pool):
            split_counts(k, pool, Own(pool, s["own_pool"]), C)
            pool.sem_inc(s["counts_split"], 1)
            pool.wait_ge(s["bias_loaded"], 32)
            for t in range(NT):
                pool.tensor_tensor(k.X[:, t, :], k.X[:, t, :], row[:], ALU.add).then_inc(s["biased"], 1)

        @block.tensor
        def _(pe):
            for t in range(NT):
                last = pe.transpose(k.slot(3)[0:1, TR + t * T:TR + (t + 1) * T], k.dinv[:, t:t + 1],
                                    k.ident[0:T, 0:T])
            last.then_inc(s["turned"], 1)
            for conv in range(2):
                if conv:
                    pe.wait_ge(s["z_lo"], KD)
                rows_product(pe, st, range(conv * UC, (conv + 1) * UC), k.XT, s["h_ready"], s["product_done"],
                             conv * 2 * NT)
                pe.wait_ge(s["h_ready"], (conv + 1) * 2 * NT)
                if conv == 0:
                    pe.wait_ge(s["counts_split"], 1)
                    for c in range(KD):
                        if c >= 3:
                            pe.wait_ge(s["agg_used"], c - 2)
                        wide3(pe, k.slot(c % 3), P, lambda cc: [
                            (h.at(slice(None), u, slice(c * P, (c + 1) * P)), C.at(slice(None), u, cc))
                            for u in range(NT)]).then_inc(s["agg_done"], 1)
                else:
                    def tile(d):
                        if d >= 3:
                            pe.wait_ge(s["used"], d - 2)
                        gcn_tile(pe, k.slot(d % 3), C, h, d).then_inc(s["agg_done"], 1)

                    norm.tail_pe(pe, tile)

        @block.scalar
        def _(act):
            for conv in range(2):
                for n in range(conv * UC + (RING if conv else 0), (conv + 1) * UC):
                    st.hi(act, n)
                if conv:
                    act.wait_ge(s["agg_done"], KD)
                split_rows_hi(k, act, h, s["product_done"], s["h_hi"], conv * 2 * NT)
                if conv == 0:
                    for n in range(UC, UC + RING):
                        st.hi(act, n)
                    act.wait_ge(s["bias_loaded"], 32)
                    for c in range(KD):
                        act.wait_ge(s["agg_used"], c + 1)
                        act.activation(z[c % 2][:], z[c % 2][:], ACT.Relu, bias=b1c[:, c:c + 1]).then_inc(s["relu_done"], 1)
                        act.wait_ge(s["relu_done"], c + 1)
                        act.activation(zT.hi[:, c, 0:N], z[c % 2][:], ACT.Copy).then_inc(s["activated"], 1)
            norm.tail_act(act)

        @block.vector
        def _(dve):
            for n in range(RING):
                st.lo(dve, n)
            dve.wait_ge(s["turned"], 1)
            dve.tensor_copy(k.rows[0:1, :], k.slot(3)[0:1, TR:TR + N]).then_inc(s["moved"], 1)
            dve.wait_ge(s["row_loaded"], 16)
            for n in range(RING, UC):
                st.lo(dve, n)
            split_rows_lo(k, dve, h, s["h_hi"], s["h_ready"])
            for n in range(UC, UC + RING):
                st.lo(dve, n)

            def z_low(c):
                dve.wait_ge(s["activated"], c + 1)
                low_part(dve, zT.lo[:, c, 0:N], z[c % 2][:], zT.hi[:, c, 0:N]).then_inc(s["z_lo"], 1)

            for c in range(KD):
                dve.wait_ge(s["agg_done"], c + 1)
                if c >= 2:
                    dve.wait_ge(s["z_lo"], c - 1)
                dve.tensor_tensor(z[c % 2][:], k.slot(c % 3)[:, MM:MM + N], dr[:], ALU.mult).then_inc(s["agg_used"], 1)
                if c >= 1:
                    z_low(c - 1)
            z_low(KD - 1)
            for n in range(UC + RING, 2 * UC):
                st.lo(dve, n)
            split_rows_lo(k, dve, h, s["h_hi"], s["h_ready"], 2 * NT)
            own = Own(dve, s["own_dve"])

            def tile(d):
                dve.wait_ge(s["agg_done"], KD + d + 1)
                dve.wait_ge(s["biased"], d + 1)
                x = split(k.X[:, d, :])
                own.link(dve.scalar_tensor_tensor(x, halves(k.slot(d % 3)[0:T]), k.dinv[:, d:d + 1], x, ALU.mult,
                                                  ALU.add))
                dve.sem_inc(s["used"], 1)

            norm.tail_dve(dve, own, tile)


MOE_E, MOE_F = 8, 192
MOE_C = MOE_E * MOE_F // P


def moe_units(w1, w2):
    up = w1.rearrange("e (k p) f -> p k e f", p=P)
    units = []
    for c in range(MOE_C):
        pieces, a = [], c * P
        while a < (c + 1) * P:
            e = a // MOE_F
            b = min((e + 1) * MOE_F, (c + 1) * P)
            pieces.append((a - c * P, b - c * P, up[:, :, e, a - e * MOE_F:b - e * MOE_F]))
            a = b
        units.append((pieces, (KD, P)))
    return units + node_units(w2.rearrange("e f d -> (e f) d"), 384, 2)


def node_major(pe, st, units, blocks, tiles_last, bank_of, operand, before, done, extra=None, chunk_ready=None,
               base=0, by_tile=True):
    per = len(units) // blocks
    for b in range(blocks):
        mine = list(units[b * per:(b + 1) * per])
        keep = min(RING, per) if b == blocks - 1 and by_tile else 0
        head, tail = mine[:per - keep], mine[per - keep:]
        chunk = 0

        def run(t, n, a, chunk, stop):
            w = st.part(n, a, slice(None))
            for i, (lhsT, rhs) in enumerate(passes(operand(chunk, t), w)):
                last = pe.matmul(bank_of(b, t), lhsT, rhs, start=(chunk == 0 and i == 0), stop=(stop and i == 2),
                                 skip_group_check=True)
            return last

        for n in head:
            st.ready(pe, n)
            for a in range(st.units[n][1][0]):
                if chunk_ready is not None:
                    chunk_ready(b, chunk)
                for t in range(NT):
                    if chunk == 0:
                        before(b, t)
                    end = n == head[-1] and not tail and a == st.units[n][1][0] - 1
                    last = run(t, n, a, chunk, end and extra is None)
                    if end:
                        if extra is not None:
                            last = extra(b, t)
                        last.then_inc(done, 1)
                chunk += 1
            if n == head[-1] and not tail:
                pe.wait_ge(done, base + NT * (b + 1))
                pe.sem_inc(st.used, 1)
            else:
                last.then_inc(st.used, 1)
        if not tail:
            continue

        def tile(t):
            c = chunk
            if c == 0:
                before(b, t)
            for n in tail:
                if t == 0:
                    st.ready(pe, n)
                for a in range(st.units[n][1][0]):
                    stop = n == tail[-1] and a == st.units[n][1][0] - 1
                    last = run(t, n, a, c, stop and extra is None)
                    c += 1
            if extra is not None:
                last = extra(b, t)
            last.then_inc(done, 1)

        tiles_last(tile)
        if units[-1] + 1 < len(st.units):
            pe.wait_ge(done, base + NT * blocks)
            pe.sem_inc(st.used, len(tail))


def moe(k, router, w1, w2, acted, gating, norm_args, b1=None, b2=None, out=None):
    nc = k.nc
    NE, F, NC = MOE_E, MOE_F, MOE_C
    K2 = 32 + NE
    up_units, down_units = range(NC), range(NC, 2 * NC)
    with ExitStack() as mem, k.stage(
            "r_loaded r_hi r_lo logits_done logits_moved logits_turned exps_in exps_out own_dve gates_ready turned "
            "gates_hi gates_lo b_loaded b_hi b_lo up_moved gate_done scaled h_hi h_lo down_done down_used zeroed "
            "sel_ready own_pool x_done stored" + Stream.SEMS + Norm.SEMS) as s, nc.Block() as block:
        norm = Norm(k, mem, s, **norm_args) if norm_args else NoNorm()
        st = Stream(k, mem, s, moe_units(w1, w2))
        zeros = k.XN[0:K2, 3:5, :].rearrange("p t d -> p (t d)")
        rw = k.sb(mem, "router", [P, KD, NE])
        rs = Split(k, mem, "router", [P, KD, NE])
        HT = Split(k, mem, "hidden", [P, NC, NP])
        act_out = [k.sb(mem, "acted", [P, N]) for _ in range(2)]
        lgT = k.sb(mem, "logits_rows", [NE, N])
        gT = k.sb(mem, "gates_rows", [K2, NP], F32R)
        sel = k.sb(mem, "selector", [K2, NC, P], F32R)
        b1c = k.sb(mem, "b1_columns", [P, NC])
        lg = k.sb(mem, "logits", [T, NT, NE])
        pr = k.sb(mem, "probs", [T, NT, NE])
        top = k.sb(mem, "top", [T, NT, 8])
        idx = k.sb(mem, "index", [T, NT, 8], U32)
        idf = k.sb(mem, "index_float", [T, NT, 8])
        sm = k.sb(mem, "sums", [T, NT, 1])
        wt = k.sb(mem, "top_weights", [T, NT, 2])
        gs = k.sb(mem, "gates", [T, 2, NT, NE])
        if b1 is not None:
            b2s = k.XN[0:K2, 0, :]
            b2h = k.sb(mem, "b2_hi", [K2, D], F32R)
            b2l = k.sb(mem, "b2_lo", [NE, D], F32R)

        @block.gpsimd
        def _(pool):
            own = Own(pool, s["own_pool"])
            seln = k.XN[0:NE, 1:3, :].rearrange("p t d -> p (t d)")
            own.link(pool.memset(seln, 1.0))
            own.link(pool.affine_select(out=seln, in_=seln, compare_op=ALU.is_ge, fill=0.0, base=0,
                                        pattern=[[1, NC * P]], channel_multiplier=-F))
            own.link(pool.affine_select(out=seln, in_=seln, compare_op=ALU.is_ge, fill=0.0, base=F - 1,
                                        pattern=[[-1, NC * P]], channel_multiplier=F))
            own.link(pool.memset(zeros, 0.0))
            own.link(pool.tensor_copy(gT[:], zeros[:, 0:NP]))
            if b1 is not None:
                own.link(pool.tensor_copy(b2h[:], zeros[:, 0:D]))
            pool.sem_inc(s["zeroed"], 1)
            own.link(pool.tensor_copy(sel[:].rearrange("e c p -> e (c p)"), zeros))
            for p0 in (0, 32):
                own.link(pool.tensor_copy(sel[p0:p0 + NE, :, :].rearrange("e c p -> e (c p)"), seln))
            pool.sem_inc(s["sel_ready"], 1)

        @block.sync
        def _(sp):
            sp.dma_start(rw[:], router.rearrange("(k p) e -> p k e", p=P)).then_inc(s["r_loaded"], 16)
            norm.sp(sp)
            if b1 is not None:
                sp.dma_start(b1c[:], b1).then_inc(s["b_loaded"], 16)
                sp.dma_start(b2s[0:NE, :], b2).then_inc(s["b_loaded"], 16)
                sp.dma_start(b2s[32:32 + NE, :], b2).then_inc(s["b_loaded"], 16)
            st.load(sp)
            if out is not None:
                for t in range(NT):
                    sp.wait_ge(s["x_done"], t + 1)
                    sp.dma_start(out[cols(t), :], k.X[:, t, :]).then_inc(s["stored"], 16)
                sp.wait_ge(s["stored"], 16 * NT)

        @block.tensor
        def _(pe):
            pe.wait_ge(s["r_lo"], 1)
            wide3(pe, k.slot(3), NE, lambda c: [(rs.at(slice(None), kk), k.XT.at(slice(None), kk, c))
                                                for kk in range(KD)]).then_inc(s["logits_done"], 1)

            def turn_logits():
                pe.wait_ge(s["logits_moved"], 1)
                for t in range(NT):
                    last = pe.transpose(k.bank(6)[0:T, t * NE:(t + 1) * NE], lgT[:, cols(t)], k.ident[0:NE, 0:NE])
                last.then_inc(s["logits_turned"], 1)

            def turn_gates():
                pe.wait_ge(s["gates_ready"], 1)
                for t in range(NT):
                    last = pe.transpose(k.slot(3)[0:NE, TR + t * T:TR + (t + 1) * T], gs[:, 0, t, :],
                                        k.ident[0:T, 0:T])
                last.then_inc(s["turned"], 1)
                pe.wait_ge(s["gates_lo"], 1)
                pe.wait_ge(s["sel_ready"], 1)

            def up(c):
                n = up_units[c]
                st.ready(pe, n)
                if c >= 3:
                    pe.wait_ge(s["up_moved"], c - 2)
                wide3(pe, k.slot(c % 3), P, lambda cc: [(st.part(n, kk, slice(None)), k.XT.at(slice(None), kk, cc))
                                                        for kk in range(KD)]).then_inc(st.used, 1)

            def spread(c):
                if c >= 1:
                    pe.wait_ge(s["scaled"], c)
                for a, n in RHALVES:
                    last = product(pe, k.slot(3)[:, MM + a:MM + a + n], [(sel[:, c, :], gT[:, a:a + n])])
                last.then_inc(s["gate_done"], 1)

            LAG = 2
            for c in range(NC + LAG):
                if c < NC:
                    up(c)
                if c == 0:
                    turn_logits()
                if c == LAG:
                    turn_gates()
                if c >= LAG:
                    spread(c - LAG)

            def bank_of(b, t):
                return k.bank((5 * b + t) % 8)[0:T, 0:384]

            def before(b, t):
                if b == 0:
                    pe.wait_ge(s["up_moved"], NC if t == 4 else NC - 1)
                elif t >= 3:
                    pe.wait_ge(s["down_used"], t - 2)

            def hidden_ready(b, c):
                if b == 0:
                    pe.wait_ge(s["h_lo"], c + 1)

            extra = None
            if b1 is not None:
                def extra(b, t):
                    if b == 0 and t == 0:
                        pe.wait_ge(s["b_lo"], 1)
                    o = slice(b * 384, (b + 1) * 384)
                    pe.matmul(bank_of(b, t), gT[:, cols(t)], b2h[:, o], start=False, stop=False, skip_group_check=True)
                    return pe.matmul(bank_of(b, t), gT[0:NE, cols(t)], b2l[:, o], start=False, stop=True,
                                     skip_group_check=True)

            node_major(pe, st, down_units, 2, lambda tile: norm.tail_pe(pe, tile), bank_of,
                              lambda c, t: HT.at(slice(None), c, cols(t)), before, s["down_done"], extra, hidden_ready)

        def hidden_hi(act, c):
            act.wait_ge(s["scaled"], c + 1)
            act.activation(HT.hi[:, c, 0:N], act_out[c % 2][:], ACT.Copy).then_inc(s["h_hi"], 1)

        @block.scalar
        def _(act):
            act.wait_ge(s["r_loaded"], 16)
            act.activation(rs.hi[:], rw[:], ACT.Copy).then_inc(s["r_hi"], 1)
            st.hi(act, 0)
            if b1 is not None:
                act.wait_ge(s["b_loaded"], 48)
                act.wait_ge(s["zeroed"], 1)
                for p0 in (0, 32):
                    act.activation(b2h[p0:p0 + NE, :], b2s[p0:p0 + NE, :], ACT.Copy).then_inc(s["b_hi"], 1)
            for n in range(1, RING):
                st.hi(act, n)
            act.wait_ge(s["exps_in"], 1)
            if gating == "logits":
                act.activation(wt[:], wt[:], ACT.Exp).then_inc(s["exps_out"], 1)
            else:
                act.activation(pr[:], lg[:], ACT.Exp).then_inc(s["exps_out"], 1)
            for c in range(NC):
                act.wait_ge(st.used, c + 1)
                if c >= 2:
                    act.wait_ge(s["h_lo"], c - 1)
                bias = b1c[:, c:c + 1] if b1 is not None else 0.0
                act.activation(act_out[c % 2][:], k.slot(c % 3)[:, MM:MM + N], acted, bias=bias).then_inc(s["up_moved"], 1)
                st.hi(act, c + RING)
                if c >= 1:
                    hidden_hi(act, c - 1)
            hidden_hi(act, NC - 1)
            for n in down_units[RING:]:
                st.hi(act, n)
            norm.tail_act(act)

        @block.vector
        def _(dve):
            own = Own(dve, s["own_dve"])
            dve.wait_ge(s["r_hi"], 1)
            low_part(dve, rs.lo[:], rw[:], rs.hi[:]).then_inc(s["r_lo"], 1)
            st.lo(dve, 0)
            if b1 is not None:
                dve.wait_ge(s["b_hi"], 2)
                low_part(dve, b2l[:], b2s[0:NE, :], b2h[0:NE, :]).then_inc(s["b_lo"], 1)
            dve.wait_ge(s["logits_done"], 1)
            dve.tensor_copy(lgT[:], k.slot(3)[0:NE, MM:MM + N]).then_inc(s["logits_moved"], 1)
            dve.wait_ge(s["logits_turned"], 1)
            own.link(dve.tensor_copy(lg[:], k.bank(6)[0:T, 0:NT * NE].rearrange("p (t e) -> p t e", e=NE)))
            st.lo(dve, 1)
            from_ = lg
            if gating != "logits":
                own.link(dve.tensor_reduce(sm[:], lg[:], AX.X, ALU.max))
                own.link(dve.tensor_tensor(lg[:], lg[:], sm[:].to_broadcast([T, NT, NE]), ALU.subtract))
                dve.sem_inc(s["exps_in"], 1)
                dve.wait_ge(s["exps_out"], 1)
                own.link(dve.tensor_reduce(sm[:], pr[:], AX.X, ALU.add))
                own.link(dve.reciprocal(sm[:], sm[:]))
                own.link(dve.tensor_tensor(pr[:], pr[:], sm[:].to_broadcast([T, NT, NE]), ALU.mult))
                from_ = pr
            for t in range(NT):
                own.sign(dve.max(top[:, t, :], from_[:, t, :]))
            own.wait()
            for t in range(NT):
                own.sign(dve.max_index(idx[:, t, :], top[:, t, :], from_[:, t, :]))
            own.wait()
            own.sign(dve.tensor_copy(idf[:], idx[:]))
            if gating == "logits":
                own.link(dve.tensor_tensor(wt[:], top[:, :, 0:2], top[:, :, 0:1].to_broadcast([T, NT, 2]), ALU.subtract))
                dve.sem_inc(s["exps_in"], 1)
                dve.wait_ge(s["exps_out"], 1)
            else:
                own.link(dve.tensor_copy(wt[:], top[:, :, 0:2]))
            if gating != "probs":
                own.link(dve.tensor_reduce(sm[:], wt[:], AX.X, ALU.add))
                own.link(dve.reciprocal(sm[:], sm[:]))
                own.link(dve.tensor_tensor(wt[:], wt[:], sm[:].to_broadcast([T, NT, 2]), ALU.mult))
            for n in range(2):
                own.sign(dve.tensor_tensor(gs[:, n, :, :], k.iota8[0:T, :].rearrange("p (a e) -> p a e", a=1)
                                           .to_broadcast([T, NT, NE]), idf[:, :, n:n + 1].to_broadcast([T, NT, NE]),
                                           ALU.is_equal))
            own.wait()
            for n in range(2):
                own.sign(dve.tensor_tensor(gs[:, n, :, :], gs[:, n, :, :], wt[:, :, n:n + 1].to_broadcast([T, NT, NE]),
                                           ALU.mult))
            own.wait()
            dve.tensor_tensor(gs[:, 0, :, :], gs[:, 0, :, :], gs[:, 1, :, :], ALU.add).then_inc(s["gates_ready"], 1)
            for n in range(2, RING):
                st.lo(dve, n)
            dve.wait_ge(s["turned"], 1)
            dve.wait_ge(s["zeroed"], 1)
            g = k.slot(3)[0:NE, TR:TR + N]
            dve.tensor_copy(gT[0:NE, 0:N], g).then_inc(s["gates_hi"], 1)
            dve.wait_ge(s["gates_hi"], 1)
            low_part(dve, gT[32:32 + NE, 0:N], g, gT[0:NE, 0:N]).then_inc(s["gates_lo"], 1)
            for c in range(NC):
                st.lo(dve, c + RING)
                dve.wait_ge(s["up_moved"], c + 1)
                dve.wait_ge(s["gate_done"], c + 1)
                dve.tensor_tensor(act_out[c % 2][:], act_out[c % 2][:], k.slot(3)[:, MM:MM + N], ALU.mult
                                  ).then_inc(s["scaled"], 1)
                dve.wait_ge(s["h_hi"], c + 1)
                low_part(dve, HT.lo[:, c, 0:N], act_out[c % 2][:], HT.hi[:, c, 0:N]).then_inc(s["h_lo"], 1)
            first = len(down_units) // 2
            for i, n in enumerate(down_units):
                if i >= RING:
                    st.lo(dve, n)
                if i >= first + 1 and i - first - 1 < NT:
                    t = i - first - 1
                    dve.wait_ge(s["down_done"], t + 1)
                    x = k.X[:, t, 0:384]
                    dve.tensor_tensor(x, x, k.bank(t)[0:T, 0:384], ALU.add).then_inc(s["down_used"], 1)

            def tile(t):
                dve.wait_ge(s["down_done"], NT + t + 1)
                x = k.X[:, t, 384:768]
                own.link(dve.tensor_tensor(x, x, k.bank((5 + t) % 8)[0:T, 0:384], ALU.add))
                dve.sem_inc(s["x_done"], 1)

            norm.tail_dve(dve, own, tile)


def at(sem_wait, sem, base, const):
    if isinstance(base, int):
        if base + const > 0:
            sem_wait(sem, base + const)
    else:
        assert const > 0
        sem_wait(sem, base + const)


def qkv_units(w):
    return feature_units(w, 0, 2 * KD) + node_units(w[:, 2 * D:3 * D], 384, 2)


def attention(k, x, qkv_w, qkv_b, qkv_columns, proj_w, proj_b, norm_args):
    nc, H, HD = k.nc, 12, 64
    SCALE = HD ** -0.5
    with ExitStack() as kept:
        O = k.sb(kept, "o", [T, NT, D])
        with ExitStack() as mem:
            QK = k.sb(mem, "qk", [P, 2 * KD, N])
            V = k.sb(mem, "v", [T, NT, D])
            with ExitStack() as tmp, k.stage("b_loaded qk_moved v_done v_moved" + Stream.SEMS) as s, nc.Block() as block:
                st = Stream(k, tmp, s, qkv_units(qkv_w))
                v_units = range(2 * KD, len(st.units))
                bc = k.sb(tmp, "qkv_bias", [P, 3 * KD])
                vrow = k.sb(tmp, "v_bias", [T, D])

                def v_bank(b, t):
                    return k.bank((5 * b + t) % 8)[0:T, 0:384]

                @block.sync
                def _(sp):
                    sp.dma_start(bc[:], qkv_columns).then_inc(s["b_loaded"], 16)
                    sp.dma_start(vrow[:], row_of(qkv_b[2 * D:3 * D], T)).then_inc(s["b_loaded"], 16)
                    st.load(sp)

                @block.tensor
                def _(pe):
                    for c in range(2 * KD):
                        st.ready(pe, c)
                        if c >= 3:
                            pe.wait_ge(s["qk_moved"], c - 2)
                        wide3(pe, k.slot(c % 3), P, lambda cc: [(st.part(c, kk, slice(None)), k.XT.at(slice(None), kk, cc))
                                                                for kk in range(KD)]).then_inc(st.used, 1)

                    def before(b, t):
                        if b == 0 and t == 0:
                            pe.wait_ge(s["qk_moved"], 2 * KD)
                        elif b == 1 and t >= 3:
                            pe.wait_ge(s["v_moved"], t - 2)

                    def tiles(tile):
                        for t in range(NT):
                            tile(t)

                    node_major(pe, st, v_units, 2, tiles, v_bank, lambda c, t: k.XT.at(slice(None), c, cols(t)), before,
                               s["v_done"])

                @block.scalar
                def _(act):
                    for n in range(RING):
                        st.hi(act, n)
                    act.wait_ge(s["b_loaded"], 32)
                    for c in range(2 * KD):
                        act.wait_ge(st.used, c + 1)
                        act.activation(QK[:, c, :], k.slot(c % 3)[:, MM:MM + N], ACT.Identity, bias=bc[:, c:c + 1]
                                       ).then_inc(s["qk_moved"], 1)
                        st.hi(act, c + RING)
                    for n in v_units[RING:]:
                        st.hi(act, n)

                @block.vector
                def _(dve):
                    for n in range(len(st.units)):
                        st.lo(dve, n)
                    dve.wait_ge(s["b_loaded"], 32)
                    for b in range(2):
                        o = slice(b * 384, (b + 1) * 384)
                        for t in range(NT):
                            dve.wait_ge(s["v_done"], b * NT + t + 1)
                            dve.tensor_tensor(V[:, t, o], v_bank(b, t), vrow[:, o], ALU.add).then_inc(s["v_moved"], 1)

            with ExitStack() as tmp, k.sems(
                    "pair_ready s_done maxed e_done t_done moved_dve moved_act av_done normed own_dve own_pool "
                    "first_ready first_hi") as (
                    pair_ready, s_done, maxed, e_done, t_done, moved_dve, moved_act, av_done, normed, own_dve, own_pool,
                    first_ready, first_hi), \
                    nc.Block() as block:
                QS = [Split(k, tmp, "pair", [P, 3, NP]) for _ in range(2)]
                PR = [k.sb(tmp, "probs", [T, N]) for _ in range(2)]
                PT = [k.sb(tmp, "probs_turned", [T, NT, T]) for _ in range(2)]
                mx = k.sb(tmp, "max", [T, 2])
                nb = k.sb(tmp, "minus_max", [T, 2])
                sums = k.sb(tmp, "sums", [T, 4])
                inv = k.sb(tmp, "inverse", [T, 2])
                PU = 2 * NT
                BODY, U = 2 * PU, H * NT
                PEEL, LOOPS = 3, 2

                def s_ap(u):
                    return k.slot(u % 2)[0:T, MM:MM + N]

                def t_ap():
                    return k.slot(2)[0:T, TR:TR + N].rearrange("p (t n) -> p t n", n=T)

                def av_ap(u):
                    return k.bank(6 + u % 2)[0:T, 0:2 * HD]

                def steps(eng, before, step, after):
                    before()
                    for u in range(PEEL):
                        step(0, u)
                    with eng.Fori(0, LOOPS) as i:
                        for j in range(PEEL, PEEL + BODY):
                            step(i * BODY, j)
                    for u in range(PEEL + LOOPS * BODY, U):
                        step(0, u)
                    after()

                def head(base, j):
                    return base // NT + j // NT

                def own_after_max(base, j):
                    return base * 2, j + 1 + max(j - 3, 0) if isinstance(base, int) else 2 * j - 2

                def own_after_norm(base, j):
                    return base * 2, min(j + 4, U) + j + 1 if isinstance(base, int) else 2 * j + 5

                def pieces(pair):
                    return (slice(0, HD), 0, pair), (slice(HD, P), 1, pair), (slice(0, P), 2, KD + pair)

                @block.gpsimd
                def _(pool):
                    own = Own(pool, own_pool)
                    for number, buf in enumerate(QS):
                        for b in range(2):
                            other = slice((1 - b) * HD, (2 - b) * HD)
                            for part in (buf.hi, buf.lo):
                                own.link(pool.tensor_copy(part[other, b, 0:N], k.zero[other, 0, :].to_broadcast([HD, N])))
                        own.link(pool.tensor_copy(buf.hi[:, 2, N:NP], k.zero[:, 0, :]))
                        own.link(pool.tensor_copy(buf.lo[:, 2, N:NP], k.zero[:, 0, :]))
                        if number == 0:
                            pool.sem_inc(first_ready, 1)
                    for pair in range(1, KD):
                        if pair >= 2:
                            pool.wait_ge(s_done, (pair - 1) * PU)
                        buf = QS[pair % 2]
                        for rows, n, src in pieces(pair):
                            own.link(pool.tensor_copy(buf.hi[rows, n, 0:N], QK[rows, src, :]))
                            own.link(pool.tensor_tensor(buf.lo[rows, n, 0:N], QK[rows, src, :],
                                                        buf.hi[rows, n, 0:N].bitcast(F32), ALU.subtract))
                        pool.sem_inc(pair_ready, 1)

                @block.tensor
                def _(pe):
                    def scores(base, j):
                        if isinstance(base, int) and base + j >= U:
                            return
                        pair, b, t = j // PU, (j // NT) % 2, j % NT
                        if j % PU == 0:
                            if isinstance(base, int) and pair == 0:
                                pe.wait_ge(first_ready, 4)
                            else:
                                at(pe.wait_ge, pair_ready, base // PU, pair)
                        at(pe.wait_ge, e_done, base, j - 1)
                        buf = QS[pair % 2]
                        for a, n in RHALVES:
                            last = product(pe, k.slot(j % 2)[0:T, MM + a:MM + a + n],
                                           passes(buf.at(slice(None), b, cols(t)), buf.at(slice(None), 2, slice(a, a + n))))
                        last.then_inc(s_done, 1)

                    def turn(base, j):
                        at(pe.wait_ge, e_done, base, j + 1)
                        at(pe.wait_ge, moved_dve, base, j)
                        at(pe.wait_ge, moved_act, base, j)
                        for c in range(NT):
                            last = pe.transpose(t_ap()[:, c, :], PR[j % 2][:, cols(c)], k.ident[0:T, 0:T])
                        last.then_inc(t_done, 1)

                    def mix(base, j):
                        at(pe.wait_ge, moved_dve, base, j + 1)
                        at(pe.wait_ge, moved_act, base, j + 1)
                        at(pe.wait_ge, normed, base, j - 1)
                        pair = base // PU + j // PU
                        product(pe, av_ap(j), [(PT[j % 2][:, c, :], V[:, c, bass.ds(pair * 2 * HD, 2 * HD)]) for c in range(NT)]
                                ).then_inc(av_done, 1)

                    def step(base, j):
                        turn(base, j)
                        scores(base, j + 2)
                        if not (isinstance(base, int) and base + j == 0):
                            mix(base, j - 1)

                    def before():
                        scores(0, 0)
                        scores(0, 1)

                    steps(pe, before, step, lambda: mix(0, U - 1))

                @block.scalar
                def _(act):
                    def exps(base, j):
                        if isinstance(base, int) and base + j >= U:
                            return
                        at(act.wait_ge, maxed, base, j + 1)
                        at(act.wait_ge, t_done, base, j - 1)
                        act.activation(PR[j % 2][:], s_ap(j), ACT.Exp, bias=nb[:, j % 2:j % 2 + 1], scale=SCALE,
                                       accum_out=sums[:, j % 4:j % 4 + 1]).then_inc(e_done, 1)

                    def move(base, j):
                        at(act.wait_ge, t_done, base, j + 1)
                        at(act.wait_ge, av_done, base, j - 1)
                        act.activation(PT[j % 2][:, 3:NT, :], t_ap()[:, 3:NT, :], ACT.Copy).then_inc(moved_act, 1)

                    def step(base, j):
                        exps(base, j + 1)
                        move(base, j)

                    for rows, n, src in pieces(0):
                        act.activation(QS[0].hi[rows, n, 0:N], QK[rows, src, :], ACT.Copy).then_inc(first_hi, 1)
                    steps(act, lambda: exps(0, 0), step, lambda: None)

                @block.vector
                def _(dve):
                    def maxima(base, j):
                        if isinstance(base, int) and base + j >= U:
                            return
                        at(dve.wait_ge, s_done, base, j + 1)
                        at(dve.wait_ge, e_done, base, j - 1)
                        dve.tensor_reduce(mx[:, j % 2:j % 2 + 1], s_ap(j), AX.X, ALU.max).then_inc(own_dve, 1)
                        at(dve.wait_ge, own_dve, *own_after_max(base, j))
                        dve.tensor_scalar(nb[:, j % 2:j % 2 + 1], mx[:, j % 2:j % 2 + 1], -SCALE, None, ALU.mult
                                          ).then_inc(maxed, 1)

                    def move(base, j):
                        at(dve.wait_ge, t_done, base, j + 1)
                        at(dve.wait_ge, av_done, base, j - 1)
                        dve.tensor_copy(PT[j % 2][:, 0:3, :], t_ap()[:, 0:3, :]).then_inc(moved_dve, 1)

                    def norm(base, j):
                        at(dve.wait_ge, av_done, base, j + 1)
                        dve.reciprocal(inv[:, j % 2:j % 2 + 1], sums[:, j % 4:j % 4 + 1]).then_inc(own_dve, 1)
                        at(dve.wait_ge, own_dve, *own_after_norm(base, j))
                        h, b = head(base, j), (j // NT) % 2
                        dve.tensor_scalar(O[:, j % NT, bass.ds(h * HD, HD)], av_ap(j)[:, b * HD:(b + 1) * HD], inv[:, j % 2:j % 2 + 1], None,
                                          ALU.mult).then_inc(normed, 1)

                    def step(base, j):
                        move(base, j)
                        maxima(base, j + 2)
                        if not (isinstance(base, int) and base + j == 0):
                            norm(base, j - 1)

                    def before():
                        for number, (rows, n, src) in enumerate(pieces(0)):
                            dve.wait_ge(first_hi, number + 1)
                            low_part(dve, QS[0].lo[rows, n, 0:N], QK[rows, src, :], QS[0].hi[rows, n, 0:N]
                                     ).then_inc(first_ready, 1)
                        maxima(0, 0)
                        maxima(0, 1)

                    steps(dve, before, step, lambda: norm(0, U - 1))

        with ExitStack() as tmp, k.stage(
                "b_loaded turned ot_hi ot_lo biased done used own_dve y_done" + Stream.SEMS + Norm.SEMS) as s, \
                  nc.Block() as block:
            st = Stream(k, tmp, s, node_units(proj_w, 384, 2))
            norm = Norm(k, tmp, s, **norm_args)
            OT = Split(k, tmp, "o_features", [P, KD, NP])
            row = k.sb(tmp, "proj_bias", [T, D])

            def bank_of(b, t):
                return k.bank((5 * b + t) % 8)[0:T, 0:384]

            @block.sync
            def _(sp):
                sp.dma_start(row[:], row_of(proj_b, T)).then_inc(s["b_loaded"], 16)
                norm.sp(sp)
                st.load(sp)

            @block.gpsimd
            def _(pool):
                pool.wait_ge(s["b_loaded"], 16)
                for t in range(NT):
                    pool.tensor_tensor(x[:, t, :], x[:, t, :], row[:], ALU.add).then_inc(s["biased"], 1)
                for t in range(NT + 2):
                    if t < NT:
                        pool.wait_ge(s["y_done"], t + 1)
                        pool.tensor_tensor(k.X[:, t, :], k.X[:, t, :], x[:, t, :], ALU.add)
                    if t >= 2:
                        norm.pool_lo(pool, t - 2)

            @block.scalar
            def _(act):
                for n in range(RING):
                    st.hi(act, n)
                for c in range(KD):
                    act.wait_ge(s["turned"], c + 1)
                    act.activation(OT.hi[:, c, 0:N], k.slot(c % 4)[:, TR:TR + N], ACT.Copy).then_inc(s["ot_hi"], 1)
                for n in range(RING, len(st.units)):
                    st.hi(act, n)
                norm.tail_act(act)

            @block.tensor
            def _(pe):
                for c in range(KD):
                    if c >= 4:
                        pe.wait_ge(s["ot_lo"], c - 3)
                    for t in range(NT):
                        last = pe.transpose(k.slot(c % 4)[:, TR + t * T:TR + (t + 1) * T], O[:, t, c * P:(c + 1) * P],
                                            k.ident[0:T, 0:T])
                    last.then_inc(s["turned"], 1)

                def before(b, t):
                    if b == 0 and t == 0:
                        pe.wait_ge(s["ot_lo"], KD)
                    elif b == 1 and t >= 3:
                        pe.wait_ge(s["used"], t - 2)

                node_major(pe, st, range(len(st.units)), 2, lambda tile: norm.tail_pe(pe, tile), bank_of,
                           lambda c, t: OT.at(slice(None), c, cols(t)), before, s["done"])

            @block.vector
            def _(dve):
                own = Own(dve, s["own_dve"])
                for n in range(RING):
                    st.lo(dve, n)
                for c in range(KD):
                    dve.wait_ge(s["ot_hi"], c + 1)
                    low_part(dve, OT.lo[:, c, 0:N], k.slot(c % 4)[:, TR:TR + N], OT.hi[:, c, 0:N]).then_inc(s["ot_lo"], 1)
                for n in range(RING, len(st.units)):
                    st.lo(dve, n)
                dve.wait_ge(s["biased"], NT)
                for t in range(NT):
                    dve.wait_ge(s["done"], t + 1)
                    dve.tensor_tensor(x[:, t, 0:384], x[:, t, 0:384], bank_of(0, t), ALU.add).then_inc(s["used"], 1)

                def tile(t):
                    dve.wait_ge(s["done"], NT + t + 1)
                    own.link(dve.tensor_tensor(x[:, t, 384:D], x[:, t, 384:D], bank_of(1, t), ALU.add))
                    dve.sem_inc(s["y_done"], 1)

                dve.wait_ge(s["used"], NT)
                norm.tail_dve(dve, own, tile)


def l1_ffn(k, w, norm_args):
    attention(k, k.XN, w["qkv_w"], w["qkv_b"], w["qkv_b_columns"], w["proj_w"], w["proj_b"],
              dict(src=k.XN, out=None, slot=1, split=True, scale=w["norm2_w_columns"], shift=w["norm2_b_columns"]))
    moe(k, w["w_gate"], w["W1"], w["W2"], ACT.Gelu, "logits", norm_args, w["b1_columns"], w["b2"])


def l2_ffn(k, phi, w1, b1, w2, b2, norm_args):
    nc = k.nc
    NE, S, F = 4, 1024, 192
    NS = NE * S // P
    ES = S // P
    F2 = F - P
    G = 2
    with ExitStack() as mem:
        XW = k.XN
        graph_dram = k.dram("graph", [2, T, NT * N])
        cuts = [(0, n * N, (n + 1) * N) for n in range(3)] + [(0, 3 * N, 3 * N + D)]
        cuts += [(1, n * D, (n + 1) * D) for n in range(2)] + [(1, 2 * D + n * NT * P, 2 * D + (n + 1) * NT * P) for n in range(2)]
        M, *DT, row, ph0, ph1, DN0, DN1 = [k.graph[g][:, u:v] for g, u, v in cuts]
        row = row.rearrange("p (e f) -> p e f", f=F)
        ph = [ap.rearrange("p (k n) -> p k n", n=P) for ap in (ph0, ph1)]
        DN = [ap[0:T].rearrange("p (t n) -> p t n", n=P) for ap in (DN0, DN1)]
        GT = [ap.rearrange("p (e n) -> p e n", n=N)
              for ap in (k.graph[0][:, 0:NE * N], k.XN[:].rearrange("p t d -> p (t d)")[:, 0:NE * N])]
        HS = k.sb(mem, "hidden", [P, NS, F + 1])
        with ExitStack() as tmp, k.stage("saved first_loaded done moved" + Stream.SEMS) as s, nc.Block() as block:
            w1v = w1.rearrange("e (k p) f -> p k e f", p=P)
            st = Stream(k, tmp, s, [([(n * F, (n + 1) * F, w1v[:, c:c + 2, 2 * b + n, :]) for n in range(2)], (2, 2 * F))
                                    for b in range(2) for c in range(0, KD, 2)])

            @block.sync
            def _(sp):
                st.load(sp, 0, RING)
                for g in range(2):
                    sp.dma_start(graph_dram[g], k.graph[g][0:T, :]).then_inc(s["saved"], 16)
                st.load(sp, RING)
                sp.wait_ge(s["saved"], 32)
                phv = phi.rearrange("(k p) s -> p k s", p=P)
                for n in range(2):
                    sp.dma_start(ph[n], phv[:, :, n * P:(n + 1) * P]).then_inc(s["first_loaded"], 16)
                sp.dma_start(row.rearrange("p e f -> p (e f)"), row_of(b1.rearrange("e f -> (e f)"), P)
                             ).then_inc(s["first_loaded"], 16)
                sp.wait_ge(s["first_loaded"], 48)

            @block.tensor
            def _(pe):
                rows_product(pe, st, range(len(st.units)), k.XT, s["moved"], s["done"])

            @block.scalar
            def _(act):
                for n in range(len(st.units)):
                    st.hi(act, n)
                for n in range(2 * NT):
                    act.wait_ge(s["done"], n + 1)
                    act.activation(XW[:, n % NT, n // NT * 384:(n // NT + 1) * 384], row_bank(k, n // NT, n % NT),
                                   ACT.Copy).then_inc(s["moved"], 1)

            @block.vector
            def _(dve):
                for n in range(len(st.units)):
                    st.lo(dve, n)
                dve.wait_ge(s["saved"], 32)
                dve.memset(M[:], -3e38)

            @block.gpsimd
            def _(pool):
                pool.memset(HS[:, :, F:F + 1], 1.0)

        with ExitStack() as lmem:
            L = k.sb(lmem, "logits", [P, NS, N])
            with ExitStack() as tmp, k.sems(
                    "phi_loaded0 phi_loaded1 p_hi p_lo b_loaded l_done maxed copied e_done t_done t_moved "
                    "h_done h_moved own_dve") as (
                    phi_loaded0, phi_loaded1, p_hi, p_lo, b_loaded, l_done, maxed, copied, e_done, t_done, t_moved,
                    h_done, h_moved, own_dve), nc.Block() as block:
                phi_loaded = [phi_loaded0, phi_loaded1]
                PH = [Split(k, tmp, "phi", [P, KD, P]) for _ in range(2)]
                nm = k.sb(tmp, "minus_max", [P, 2])
                cs = k.sb(tmp, "sums", [P, 2])
                rc = k.sb(tmp, "inverse", [P, 2])
                phv = phi.rearrange("(k p) s -> p k s", p=P)

                def l_ap(j):
                    return k.slot(j % 2)[:, MM:MM + N]

                def t_ap():
                    return k.slot(2)[0:T, 0:NT * P].rearrange("p (t n) -> p t n", n=P)

                def h_ap(j):
                    return k.bank(6 + j % 2)[:, 0:F]

                @block.sync
                def _(sp):
                    def load(chunk, b):
                        sp.dma_start(ph[b][:], phv[:, :, bass.ts(chunk, P)]).then_inc(phi_loaded[b], 16)

                    for sem in (*phi_loaded, b_loaded):
                        sp.sem_inc(sem, 16)
                    with sp.Fori(1, NS // G) as i:
                        for b in range(G):
                            sp.wait_ge(p_lo, i * G + (b - 1))
                            load(i * G + b, b)

                @block.tensor
                def _(pe):
                    def logits(base, b):
                        at(pe.wait_ge, p_lo, base, b + 1)
                        at(pe.wait_ge, copied, base, b - 1)
                        at(pe.wait_ge, e_done, base, b - 1)
                        wide3(pe, k.slot(b), P, lambda cc: [
                            (PH[b].at(slice(None), c), k.XT.at(slice(None), c, cc)) for c in range(KD)]
                              ).then_inc(l_done, 1)

                    def turn(base, b):
                        at(pe.wait_ge, e_done, base, b + 1)
                        at(pe.wait_ge, t_moved, base, b)
                        for t in range(NT):
                            last = pe.transpose(t_ap()[:, t, :], DT[b][:, cols(t)], k.ident[:])
                        last.then_inc(t_done, 1)

                    def hidden(base, b):
                        at(pe.wait_ge, t_moved, base, b + 1)
                        at(pe.wait_ge, h_moved, base, b - 1)
                        e = base // ES
                        product(pe, h_ap(b), [(DN[b][:, t, :], XW[:, t, bass.ds(e * F, F)]) for t in range(NT)]
                                ).then_inc(h_done, 1)

                    def pair(base, next_):
                        turn(base, 0)
                        logits_at(next_, 0)
                        hidden(base, 0)
                        turn(base, 1)
                        logits_at(next_, 1)
                        hidden(base, 1)

                    def logits_at(base, b):
                        if base is not None:
                            if isinstance(base, int):
                                logits(base, b)
                            else:
                                pe.wait_ge(p_lo, base + (b + 1))
                                pe.wait_ge(copied, base + (b - 1))
                                pe.wait_ge(e_done, base + (b - 1))
                                wide3(pe, k.slot(b), P, lambda cc: [
                                    (PH[b].at(slice(None), c), k.XT.at(slice(None), c, cc)) for c in range(KD)]
                                      ).then_inc(l_done, 1)

                    logits(0, 0)
                    logits(0, 1)
                    pair(0, G)
                    with pe.Fori(1, NS // G - 1) as i:
                        for b in range(G):
                            pe.wait_ge(e_done, i * G + (b + 1))
                            pe.wait_ge(t_moved, i * G + b)
                            for t in range(NT):
                                last = pe.transpose(t_ap()[:, t, :], DT[b][:, cols(t)], k.ident[:])
                            last.then_inc(t_done, 1)
                            logits_at(i * G + G, b)
                            pe.wait_ge(t_moved, i * G + (b + 1))
                            pe.wait_ge(h_moved, i * G + (b - 1))
                            product(pe, h_ap(b), [(DN[b][:, t, :], XW[:, t, bass.ds(((i * G) // ES) * F, F)])
                                                  for t in range(NT)]).then_inc(h_done, 1)
                    pair(NS - G, None)

                @block.vector
                def _(dve):
                    own = Own(dve, own_dve)

                    def phi_lo(base, b):
                        at(dve.wait_ge, p_hi, base, b + 1)
                        low_part(dve, PH[b % G].lo[:], ph[b % G], PH[b % G].hi[:]).then_inc(p_lo, 1)

                    def chunk_max(base, b):
                        at(dve.wait_ge, l_done, base, b + 1)
                        own.link(dve.tensor_reduce(nm[:, b:b + 1], l_ap(b), AX.X, ALU.max, negate=True))
                        own.link(dve.tensor_tensor(M[:], M[:], l_ap(b), ALU.max))
                        dve.sem_inc(maxed, 1)

                    def finish(base, b):
                        at(dve.wait_ge, t_done, base, b + 1)
                        at(dve.wait_ge, h_done, base, b - 1)
                        own.link(dve.tensor_copy(DN[b][:], t_ap()))
                        dve.sem_inc(t_moved, 1)
                        own.link(dve.reciprocal(rc[:, b:b + 1], cs[:, b:b + 1]))
                        at(dve.wait_ge, h_done, base, b + 1)
                        own.link(dve.scalar_tensor_tensor(
                            HS[:, bass.ds(base + b, 1), 0:F].rearrange("p a n -> p (a n)"), h_ap(b), rc[:, b:b + 1],
                            row[:, base // ES, :], ALU.mult, ALU.add))
                        dve.sem_inc(h_moved, 1)

                    dve.wait_ge(b_loaded, 16)
                    phi_lo(0, 0)
                    phi_lo(0, 1)
                    chunk_max(0, 0)
                    phi_lo(0, 2)
                    chunk_max(0, 1)
                    phi_lo(0, 3)
                    finish(0, 0)
                    chunk_max(G, 0)
                    phi_lo(G, 2)
                    finish(0, 1)
                    chunk_max(G, 1)
                    phi_lo(G, 3)

                    def round_(i, more):
                        for b in range(G):
                            dve.wait_ge(t_done, i * G + (b + 1))
                            dve.wait_ge(h_done, i * G + (b - 1))
                            own.link(dve.tensor_copy(DN[b][:], t_ap()))
                            dve.sem_inc(t_moved, 1)
                            own.link(dve.reciprocal(rc[:, b:b + 1], cs[:, b:b + 1]))
                            dve.wait_ge(l_done, i * G + (G + b + 1))
                            dve.wait_ge(e_done, i * G + (b + 1))
                            own.link(dve.tensor_reduce(nm[:, b:b + 1], l_ap(b), AX.X, ALU.max, negate=True))
                            own.link(dve.tensor_tensor(M[:], M[:], l_ap(b), ALU.max))
                            dve.sem_inc(maxed, 1)
                            if more:
                                phi_lo(i * G + G, b + 2)
                            dve.wait_ge(h_done, i * G + (b + 1))
                            own.link(dve.scalar_tensor_tensor(
                                HS[:, bass.ds(i * G + b, 1), 0:F].rearrange("p a n -> p (a n)"), h_ap(b),
                                rc[:, b:b + 1], row[:, bass.ds((i * G) // ES, 1), :].rearrange("p a n -> p (a n)"),
                                ALU.mult, ALU.add))
                            dve.sem_inc(h_moved, 1)

                    with own.loop(NS // G - 3, 2 * 5) as i0:
                        round_(i0 + 1, True)
                    round_(NS // G - 2, False)
                    finish(NS - G, 0)
                    finish(NS - G, 1)

                @block.scalar
                def _(act):
                    def exps(base, b):
                        at(act.wait_ge, maxed, base, b + 1)
                        at(act.wait_ge, t_done, base, b - 1)
                        at(act.wait_ge, h_moved, base, b - 1)
                        act.activation(DT[b][:], l_ap(b), ACT.Exp, bias=nm[:, b:b + 1], accum_out=cs[:, b:b + 1]
                                       ).then_inc(e_done, 1)
                        act.activation(L[:, bass.ds(base + b, 1), :].rearrange("p a n -> p (a n)"), l_ap(b), ACT.Copy
                                       ).then_inc(copied, 1)

                    def phi_hi(base, b):
                        if isinstance(base, int):
                            act.wait_ge(phi_loaded[b % G], (base + b) // G * 16 + 16)
                        else:
                            act.wait_ge(phi_loaded[b % G], (base // G) * 16 + (b // G * 16 + 16))
                        at(act.wait_ge, l_done, base, b - 1)
                        act.activation(PH[b % G].hi[:], ph[b % G], ACT.Copy).then_inc(p_hi, 1)

                    for b in range(G):
                        phi_hi(0, b)
                    for b in range(G):
                        phi_hi(0, G + b)
                        exps(0, b)

                    def round_(i, more):
                        for b in range(G):
                            if more:
                                phi_hi(i * G, G + b)
                            act.wait_ge(maxed, i * G + (b + 1))
                            act.wait_ge(t_done, i * G + (b - 1))
                            act.wait_ge(h_moved, i * G + (b - 1))
                            act.activation(DT[b][:], l_ap(b), ACT.Exp, bias=nm[:, b:b + 1], accum_out=cs[:, b:b + 1]
                                           ).then_inc(e_done, 1)
                            act.activation(L[:, bass.ds(i * G + b, 1), :].rearrange("p a n -> p (a n)"), l_ap(b),
                                           ACT.Copy).then_inc(copied, 1)

                    with act.Fori(1, NS // G - 1) as i:
                        round_(i, True)
                    round_(NS // G - 1, False)

            with ExitStack() as tmp, k.sems(
                    "turned reduced spread row_ready own_dve gelu_done diff_done e_done staged g_moved "
                    "g_used restored") as (turned, reduced, spread, row_ready, own_dve, gelu_done, diff_done, e_done, staged,
                          g_moved, g_used, restored), nc.Block() as block:
                top = k.sb(tmp, "top", [T, NT])
                diag = k.sb(tmp, "top_diagonal", [T, NT, T])
                trow = k.sb(tmp, "top_row", [P, N])
                CT = [k.sb(tmp, "combine", [P, N]) for _ in range(2)]
                HB = [k.sb(tmp, "hidden_chunk", [P, F + 1]) for _ in range(2)]

                def chunk_of(ap, n):
                    return ap[:, bass.ds(n, 1), :].rearrange("p a n -> p (a n)")

                @block.scalar
                def _(act):
                    for q in range(4):
                        n = NS // 4
                        act.activation(HS[:, q * n:(q + 1) * n, 0:F], HS[:, q * n:(q + 1) * n, 0:F],
                                       ACT.Gelu_apprx_tanh).then_inc(gelu_done, 1)

                    def move(e, q):
                        act.wait_ge(g_used, e * ES + (ES + 2))
                        act.activation(GT[1][0:F2 + 1, bass.ds(e, 1), :].rearrange("p a n -> p (a n)"),
                                       k.slot(2 * q + 1)[0:F2 + 1, MM:MM + N], ACT.Copy).then_inc(g_moved, 1)

                    def exps(e, chunks):
                        for j in chunks:
                            act.wait_ge(diff_done, e * ES + (j + 1))
                            act.activation(CT[j % 2][:], CT[j % 2][:], ACT.Exp).then_inc(e_done, 1)

                    exps(0, range(ES))
                    exps(1, range(2))
                    move(0, 0)
                    exps(1, range(2, ES))
                    with act.Fori(1, NE // 2) as i:
                        for q in range(2):
                            exps(i * 2 + q, range(2))
                            move(i * 2 + (q - 1), 1 - q)
                            exps(i * 2 + q, range(2, ES))
                    move(NE - 1, 1)

                @block.gpsimd
                def _(pool):
                    pool.wait_ge(gelu_done, 4)
                    pool.tensor_copy(HB[0][:], HS[:, 0, :]).then_inc(staged, 1)
                    pool.tensor_copy(HB[1][:], HS[:, 1, :]).then_inc(staged, 1)
                    with pool.Fori(1, NS // G) as i:
                        for b in range(G):
                            pool.wait_ge(g_used, i * G + (b + 1))
                            pool.tensor_copy(HB[b][:], chunk_of(HS, i * G + b)).then_inc(staged, 1)

                @block.sync
                def _(sp):
                    sp.dma_start(k.graph[1][0:T, :], graph_dram[1]).then_inc(restored, 16)
                    sp.wait_ge(restored, 16)

                @block.tensor
                def _(pe):
                    for t in range(NT):
                        last = pe.transpose(k.slot(2)[0:T, t * P:(t + 1) * P], M[:, cols(t)], k.ident[:])
                    last.then_inc(turned, 1)
                    for t in range(NT):
                        pe.wait_ge(reduced, t + 1)
                        last = pe.matmul(k.slot(3)[:, TR + t * T:TR + (t + 1) * T], k.ones[0:T, :], diag[:, t, :],
                                         start=True, stop=True)
                    last.then_inc(spread, 1)
                    pe.sem_inc(g_moved, 4)
                    pe.sem_inc(g_used, 2)
                    with pe.Fori(0, NE // 2) as i:
                        for q in range(2):
                            e = i * 2 + q
                            pe.wait_ge(g_moved, e * 2 + 2)
                            for j in range(ES):
                                pe.wait_ge(staged, e * ES + (j + 1))
                                pe.wait_ge(e_done, e * ES + (j + 1))
                                for c, (f0, fn) in enumerate(((0, P), (P, F2 + 1))):
                                    for a, n in HALVES:
                                        last = pe.matmul(k.slot(2 * q + c)[0:fn, MM + a:MM + a + n],
                                                         HB[j % 2][:, f0:f0 + fn], CT[j % 2][:, a:a + n],
                                                         start=(j == 0), stop=(j == ES - 1))
                                last.then_inc(g_used, 1)

                @block.vector
                def _(dve):
                    dve.wait_ge(turned, 1)
                    own = Own(dve, own_dve)
                    own.link(dve.tensor_reduce(top[:], k.slot(2)[0:T, 0:NT * P].rearrange("p (t n) -> p t n", n=P),
                                               AX.X, ALU.max))
                    for t in range(NT):
                        dve.tensor_scalar(diag[:, t, :], k.ident[0:T, 0:T], top[:, t:t + 1], None, ALU.mult
                                          ).then_inc(reduced, 1)
                    dve.wait_ge(spread, 1)
                    dve.tensor_copy(trow[:], k.slot(3)[:, TR:TR + N]).then_inc(row_ready, 1)
                    dve.wait_ge(row_ready, 1)

                    def move(e, q):
                        dve.wait_ge(g_used, e * ES + (ES + 2))
                        dve.tensor_copy(GT[0][:, bass.ds(e, 1), :].rearrange("p a n -> p (a n)"),
                                        k.slot(2 * q)[:, MM:MM + N]).then_inc(g_moved, 1)

                    def diffs(e, chunks):
                        for j in chunks:
                            dve.wait_ge(g_used, e * ES + (j + 1))
                            dve.tensor_tensor(CT[j % 2][:], chunk_of(L, e * ES + j), trow[:], ALU.subtract
                                              ).then_inc(diff_done, 1)

                    diffs(0, range(ES))
                    diffs(1, range(2))
                    move(0, 0)
                    diffs(1, range(2, ES))
                    with dve.Fori(1, NE // 2) as i:
                        for q in range(2):
                            diffs(i * 2 + q, range(2))
                            move(i * 2 + (q - 1), 1 - q)
                            diffs(i * 2 + q, range(2, ES))
                    move(NE - 1, 1)

        with ExitStack() as tmp, k.stage("w_loaded0 w_loaded1 w_loaded2 w_loaded3 ones_done done inverted used own_dve restored" + Norm.SEMS) as s, \
                nc.Block() as block:
            norm = Norm(k, tmp, s, **norm_args)
            w_loaded = [s["w_loaded0"], s["w_loaded1"], s["w_loaded2"], s["w_loaded3"]]
            w2b = k.sb(tmp, "w2", [P, NE, 2, D + 1])
            inv = k.sb(tmp, "inverse", [T, NT])

            @block.gpsimd
            def _(pool):
                pool.memset(w2b[:, :, :, D:D + 1], 0.0).then_inc(s["ones_done"], 1)
                pool.wait_ge(s["ones_done"], 1)
                pool.memset(w2b[F2:F2 + 1, :, 1, D:D + 1], 1.0).then_inc(s["ones_done"], 1)

            @block.sync
            def _(sp):
                for e in range(NE):
                    sp.dma_start(w2b[:, e, 0, 0:D], w2[e, 0:P, :]).then_inc(w_loaded[e], 16)
                    sp.dma_start(w2b[0:F2, e, 1, 0:D], w2[e, P:F, :]).then_inc(w_loaded[e], 16)
                    sp.dma_start(w2b[F2:F2 + 1, e, 1, 0:D], b2[e:e + 1, :]).then_inc(w_loaded[e], 16)
                sp.wait_ge(s["done"], NT)
                sp.dma_start(k.graph[0][0:T, :], graph_dram[0]).then_inc(s["restored"], 16)
                sp.wait_ge(s["restored"], 16)

            @block.tensor
            def _(pe):
                pe.wait_ge(s["ones_done"], 2)

                def tile(t):
                    if t >= 3:
                        pe.wait_ge(s["used"], t - 2)
                    for b in range(2):
                        n = 384 + b
                        for e in range(NE):
                            if t == 0 and b == 0:
                                pe.wait_ge(w_loaded[e], 48)
                            for c, p in ((0, P), (1, F2 + 1)):
                                last = pe.matmul(k.slot(t % 3)[0:T, b * 512:b * 512 + n], GT[c][0:p, e, cols(t)],
                                                 w2b[0:p, e, c, b * 384:b * 384 + n], start=(e == 0 and c == 0),
                                                 stop=(e == NE - 1 and c == 1), skip_group_check=True)
                    last.then_inc(s["done"], 1)

                norm.tail_pe(pe, tile)

            @block.scalar
            def _(act):
                norm.tail_act(act)

            @block.vector
            def _(dve):
                own = Own(dve, s["own_dve"])

                def tile(t):
                    dve.wait_ge(s["done"], t + 1)
                    dve.reciprocal(inv[:, t:t + 1], k.slot(t % 3)[0:T, 512 + 384:512 + 385]).then_inc(s["inverted"], 1)
                    dve.wait_ge(s["inverted"], t + 1)
                    x = split(k.X[:, t, :])
                    own.link(dve.scalar_tensor_tensor(x, halves(k.slot(t % 3)[0:T]), inv[:, t:t + 1], x, ALU.mult,
                                                      ALU.add))
                    dve.sem_inc(s["used"], 1)

                norm.tail_dve(dve, own, tile)


def l3_gnn(k, W1, s1, d1, b1, W2, s2, d2, b2, norm_args):
    nc, H, HD = k.nc, 4, 512
    K2 = H * HD // P
    a_dram, r_dram = k.dram("l3_a", [2 * H, N]), k.dram("l3_r", [2 * H, N])
    a_dram2, r_dram2 = k.dram("l3_a2", [2, N]), k.dram("l3_r2", [2, N])
    with ExitStack() as mem:
        ZT = k.sb(mem, "z_features", [P, K2, N])
        with ExitStack() as hmem:
            H1 = k.sb(hmem, "h1", [T, NT, H * HD])
            A12 = k.sb(hmem, "a12", [T, NT, 2 * H])
            B1 = k.sb(hmem, "a1_times_slope", [T, NT, H])
            B8 = k.sb(hmem, "a1_rest", [T, NT, H])
            with ExitStack() as tmp, k.stage(
                    "a_loaded done moved scored turned moved_rows stored" + Stream.SEMS) as s, nc.Block() as block:
                wv = W1.rearrange("(k p) n -> p k n", p=P)
                st = Stream(k, tmp, s, [(wv[:, c:c + 1, h * HD:(h + 1) * HD], (1, HD)) for h in range(H)
                                        for c in range(KD)], HD)
                flat = k.XN[:].rearrange("p t d -> p (t d)")
                ar = [flat[:, 0:H * HD], k.sb(tmp, "attn", [T, H * HD])]
                junk = [flat[:, (H + n) * HD:(H + n + 1) * HD] for n in range(2)]
                pe_part, dve_part, sp_part = rows_out(k, block, A12, 2 * H, a_dram, s["scored"], s["turned"], s["moved_rows"],
                                                      s["stored"], need=2 * NT * H)

                @block.sync
                def _(sp):
                    st.load(sp, 0, RING)
                    sp.dma_start(ar[0], row_of(s1, T)).then_inc(s["a_loaded"], 16)
                    sp.dma_start(ar[1][:], row_of(d1, T)).then_inc(s["a_loaded"], 16)
                    st.load(sp, RING)
                    sp_part(sp)

                def h_bank(h, t):
                    return k.bank((h * NT + t) % 8)[0:T, :]

                @block.tensor
                def _(pe):
                    def before(h, t):
                        if h * NT + t >= 8:
                            pe.wait_ge(s["moved"], h * NT + t - 7)

                    def tiles(tile):
                        for t in range(NT):
                            tile(t)

                    node_major(pe, st, range(len(st.units)), H, tiles, h_bank,
                               lambda c, t: k.XT.at(slice(None), c, cols(t)), before, s["done"])
                    pe_part(pe)

                @block.scalar
                def _(act):
                    for n in range(RING):
                        st.hi(act, n)
                    for h in range(H):
                        for n in range(h * KD + RING, min((h + 1) * KD + RING, len(st.units))):
                            st.hi(act, n)
                        for t in range(NT):
                            act.wait_ge(s["done"], h * NT + t + 1)
                            act.activation(H1[:, t, h * HD:(h + 1) * HD], h_bank(h, t), ACT.Copy).then_inc(s["moved"], 1)

                @block.vector
                def _(dve):
                    for n in range(RING):
                        st.lo(dve, n)
                    for h in range(H):
                        for n in range(h * KD + RING, min((h + 1) * KD + RING, len(st.units))):
                            st.lo(dve, n)
                        if h == 0:
                            dve.wait_ge(s["a_loaded"], 32)
                        for t in range(NT):
                            n = h * NT + t
                            dve.wait_ge(s["moved"], n + 1)
                            for side in range(2):
                                if n >= 1:
                                    dve.wait_ge(s["scored"], 2 * n - 1 + side)
                                dve.tensor_tensor_reduce(
                                    junk[side], H1[:, t, h * HD:(h + 1) * HD], ar[side][:, h * HD:(h + 1) * HD],
                                    1.0, 0.0, ALU.mult, ALU.add, A12[:, t, side * H + h:side * H + h + 1]
                                    ).then_inc(s["scored"], 1)
                    dve_part(dve)

            gat_max(k, H, A12, a_dram, r_dram, B1, B8)

            R = 2
            with ExitStack() as tmp, k.stage(
                    "b_loaded own_dve own_pool summed den_done inverted agg_done clipped elu_used exp_done" + GatWeights.SEMS
                    ) as s, nc.Block() as block:
                gat = GatWeights(k, tmp, s, r_dram, H, B1, B8, R, 1, on_dve=2)
                PB = gat.PB
                total = k.sb(tmp, "weights_sum", [T, N])
                rec = k.sb(tmp, "inverse", [P, N])
                low = [k.sb(tmp, "low", [P, N]) for _ in range(2)]
                bc = k.sb(tmp, "b1_columns", [P, K2])
                FC = HD // P

                @block.sync
                def _(sp):
                    sp.dma_start(bc[:], b1).then_inc(s["b_loaded"], 16)
                    for h in range(H):
                        gat.load(sp, h, 0, wait=h >= 1)

                def elu_exps(act, h):
                    for f in range(h * FC, (h + 1) * FC):
                        act.wait_ge(s["clipped"], f + 1)
                        act.activation(low[f % 2][:], low[f % 2][:], ACT.Exp).then_inc(s["exp_done"], 1)

                @block.scalar
                def _(act):
                    act.wait_ge(s["b_loaded"], 16)
                    for h in range(H):
                        gat.exps(act, h, h % R)
                        if h >= 1:
                            elu_exps(act, h - 1)
                    elu_exps(act, H - 1)

                @block.vector
                def _(dve):
                    own = Own(dve, s["own_dve"])
                    dve.wait_ge(s["b_loaded"], 16)

                    def elu(h):
                        dve.wait_ge(s["den_done"], h + 1)
                        own.link(dve.tensor_scalar(rec[:], k.slot(3)[:, MM:MM + N], 1e-16, None, ALU.add))
                        own.link(dve.reciprocal(rec[:], rec[:]))
                        dve.sem_inc(s["inverted"], 1)

                        def last_part(f):
                            z = ZT[:, f, :]
                            dve.wait_ge(s["exp_done"], f + 1)
                            own.link(dve.tensor_scalar(z, z, bc[:, f:f + 1], 0.0, ALU.add, ALU.max))
                            own.link(dve.scalar_tensor_tensor(z, low[f % 2][:], -1.0, z, ALU.add, ALU.add))

                        for f in range(h * FC, (h + 1) * FC):
                            z = ZT[:, f, :]
                            dve.wait_ge(s["agg_done"], f + 1)
                            own.link(dve.tensor_tensor(z, k.slot(f % 3)[:, MM:MM + N], rec[:], ALU.mult))
                            dve.sem_inc(s["elu_used"], 1)
                            own.link(dve.tensor_scalar(low[f % 2][:], z, bc[:, f:f + 1], 0.0, ALU.add, ALU.min))
                            dve.sem_inc(s["clipped"], 1)
                            if f > h * FC:
                                last_part(f - 1)
                        last_part((h + 1) * FC - 1)

                    for h in range(H):
                        gat.maxima(dve, h, h % R, h + 1, 0)
                        gat.counts_dve(dve, h, h % R)
                        if h >= 1:
                            elu(h - 1)
                    elu(H - 1)

                @block.gpsimd
                def _(pool):
                    own = Own(pool, s["own_pool"])
                    for h in range(H):
                        gat.counts_pool(pool, h, h % R)
                        pool.wait_ge(s["p_pool"], (h + 1) * (NT - gat.on_dve))
                        if h >= 1:
                            pool.wait_ge(s["den_done"], h)
                        w = gat.PB[h % R]
                        own.link(pool.tensor_tensor(total[:], w[:, 2, :], w[:, 3, :], ALU.add))
                        own.link(pool.tensor_tensor(total[:], total[:], w[:, 4, :], ALU.add))
                        pool.wait_ge(s["p_dve"], (h + 1) * gat.on_dve)
                        own.link(pool.tensor_tensor(total[:], total[:], w[:, 0, :], ALU.add))
                        own.link(pool.tensor_tensor(total[:], total[:], w[:, 1, :], ALU.add))
                        pool.sem_inc(s["summed"], 1)

                @block.tensor
                def _(pe):
                    for h in range(H):
                        gat.ready(pe, h)
                        for f in range(h * FC, (h + 1) * FC):
                            if f >= 3:
                                pe.wait_ge(s["elu_used"], f - 2)
                            wide(pe, k.slot(f % 3), P, lambda a, n: [
                                (H1[:, u, f * P:(f + 1) * P], PB[h % R][:, u, a:a + n]) for u in range(NT)]
                                ).then_inc(s["agg_done"], 1)
                            if f == h * FC:
                                pe.wait_ge(s["summed"], h + 1)
                                if h >= 1:
                                    pe.wait_ge(s["inverted"], h)
                                wide(pe, k.slot(3), P, lambda a, n: [(k.ones[0:T, :], total[:, a:a + n])]
                                     ).then_inc(s["den_done"], 1)

        H2 = k.sb(mem, "h2", [T, NT, D + 1])
        A12 = k.sb(mem, "a12", [T, NT, 2])
        B1 = k.sb(mem, "a1_times_slope", [T, NT, 1])
        B8 = k.sb(mem, "a1_rest", [T, NT, 1])
        with ExitStack() as tmp, k.stage(
                "a_loaded done moved scored turned moved_rows stored z_hi z_lo" + Stream.SEMS) as s, \
                nc.Block() as block:
            st = Stream(k, tmp, s, node_units(W2, 384, 2))
            UC = len(st.units)
            ZR = 4
            ZS = [Split(k, tmp, "z_chunk", [P, NP]) for _ in range(ZR)]
            ar, junk = [k.XN[:].rearrange("p t d -> p (t d)")[:, n * D:(n + 2) * D].rearrange("p (a d) -> p a d", d=D)
                        for n in (0, 2)]
            pe_part, dve_part, sp_part = rows_out(k, block, A12, 2, a_dram2, s["scored"], s["turned"], s["moved_rows"], s["stored"],
                                                  need=2 * NT)

            def move(act, n):
                act.wait_ge(s["done"], n + 1)
                act.activation(H2[:, n % NT, n // NT * 384:(n // NT + 1) * 384], row_bank(k, n // NT, n % NT), ACT.Copy
                               ).then_inc(s["moved"], 1)

            @block.gpsimd
            def _(pool):
                pool.memset(H2[:, :, D:D + 1], 1.0)

            @block.sync
            def _(sp):
                st.load(sp, 0, RING)
                sp.dma_start(ar[:, 0, :], row_of(s2, T)).then_inc(s["a_loaded"], 16)
                sp.dma_start(ar[:, 1, :], row_of(d2, T)).then_inc(s["a_loaded"], 16)
                st.load(sp, RING)
                sp_part(sp)

            @block.tensor
            def _(pe):
                def before(b, t):
                    if b == 1 and t >= 3:
                        pe.wait_ge(s["moved"], t - 2)

                node_major(pe, st, range(UC), 2, None, lambda b, t: row_bank(k, b, t),
                           lambda c, t: ZS[c % ZR].at(slice(None), cols(t)), before, s["done"],
                           chunk_ready=lambda b, c: pe.wait_ge(s["z_lo"], b * K2 + c + 1), by_tile=False)
                pe_part(pe)

            @block.scalar
            def _(act):
                for n in range(UC):
                    st.hi(act, n)
                    if n >= 2:
                        act.wait_ge(st.used, n - 1)
                    for c in range(2 * n, 2 * n + 2):
                        act.activation(ZS[c % ZR].hi[:, 0:N], ZT[:, c % K2, :], ACT.Copy).then_inc(s["z_hi"], 1)
                    if n == UC // 2:
                        move(act, 0)
                        move(act, 1)
                    if n == UC // 2 + 1:
                        for m in range(2, NT):
                            move(act, m)
                for m in range(NT, 2 * NT):
                    move(act, m)

            @block.vector
            def _(dve):
                for n in range(UC):
                    st.lo(dve, n)
                    for c in range(2 * n, 2 * n + 2):
                        dve.wait_ge(s["z_hi"], c + 1)
                        low_part(dve, ZS[c % ZR].lo[:, 0:N], ZT[:, c % K2, :], ZS[c % ZR].hi[:, 0:N]).then_inc(s["z_lo"], 1)
                dve.wait_ge(s["a_loaded"], 32)
                for t in range(NT):
                    dve.wait_ge(s["moved"], NT + t + 1)
                    for side in range(2):
                        if t >= 1:
                            dve.wait_ge(s["scored"], 2 * t - 1 + side)
                        dve.tensor_tensor_reduce(junk[:, side, :], H2[:, t, 0:D], ar[:, side, :], 1.0, 0.0, ALU.mult,
                                                 ALU.add, A12[:, t, side:side + 1]).then_inc(s["scored"], 1)
                dve_part(dve)

        gat_max(k, 1, A12, a_dram2, r_dram2, B1, B8)

        with ExitStack() as tmp, k.stage(
                "b_loaded own_dve agg_done used biased" + GatWeights.SEMS + Norm.SEMS
                ) as s, nc.Block() as block:
            norm = Norm(k, tmp, s, **norm_args)
            gat = GatWeights(k, tmp, s, r_dram2, 1, B1, B8, 1, on_dve=3)
            den = k.sb(tmp, "den", [T, NT])
            row = k.sb(tmp, "bias_row", [T, D])

            @block.sync
            def _(sp):
                gat.load(sp, 0, 0, wait=False)
                sp.dma_start(row[:], row_of(b2, T)).then_inc(s["b_loaded"], 16)

            @block.gpsimd
            def _(pool):
                gat.counts_pool(pool, 0, 0)
                pool.wait_ge(s["b_loaded"], 16)
                for t in range(NT):
                    pool.tensor_tensor(k.X[:, t, :], k.X[:, t, :], row[:], ALU.add).then_inc(s["biased"], 1)

            @block.scalar
            def _(act):
                gat.exps(act, 0, 0)
                norm.tail_act(act)

            @block.tensor
            def _(pe):

                def tile(d):
                    if d >= 3:
                        pe.wait_ge(s["used"], d - 2)
                    for b in range(2):
                        n = 384 + b
                        for c in range(NT):
                            if d == 0 and b == 0:
                                gat.ready_tile(pe, c)
                            last = pe.matmul(k.slot(d % 3)[0:T, b * 512:b * 512 + n], gat.PB[0][:, c, cols(d)],
                                             H2[:, c, b * 384:b * 384 + n], start=(c == 0), stop=(c == NT - 1),
                                             skip_group_check=True)
                    last.then_inc(s["agg_done"], 1)

                norm.tail_pe(pe, tile)

            @block.vector
            def _(dve):
                own = Own(dve, s["own_dve"])
                gat.maxima(dve, 0, 0, 1)
                gat.counts_dve(dve, 0, 0)

                def tile(d):
                    dve.wait_ge(s["agg_done"], d + 1)
                    own.link(dve.tensor_scalar(den[:, d:d + 1], k.slot(d % 3)[0:T, 512 + 384:512 + 385], 1e-16, None,
                                               ALU.add))
                    own.link(dve.reciprocal(den[:, d:d + 1], den[:, d:d + 1]))
                    dve.wait_ge(s["biased"], d + 1)
                    x = split(k.X[:, d, :])
                    own.link(dve.scalar_tensor_tensor(x, halves(k.slot(d % 3)[0:T]), den[:, d:d + 1], x, ALU.mult,
                                                      ALU.add))
                    dve.sem_inc(s["used"], 1)

                norm.tail_dve(dve, own, tile)


def build(nc, a, out):
    ctx = ExitStack()
    with ctx:
        k = Kit(nc, ctx)

        def dram(name, shape):
            k.stage_no += 1
            return nc.dram_tensor(f"{name}_{k.stage_no}", shape, F32).ap()

        k.dram = dram
        k.ring = None
        k.X = k.sb(ctx, "X", [T, NT, D])
        k.XN = k.sb(ctx, "XN", [T, NT, D])
        k.XT = Split(k, ctx, "XT", [P, KD, NP])
        k.graph = [k.sb(ctx, name, [P, NT * N]) for name in ("counts", "mask")]
        k.C, k.MASK = [ap[0:T, :].rearrange("p (t n) -> p t n", n=N) for ap in k.graph]
        k.dinv = k.sb(ctx, "dinv", [T, NT])
        k.ident = k.sb(ctx, "ident", [P, P])
        k.ones = k.sb(ctx, "ones", [P, P])
        k.eps = k.sb(ctx, "eps", [P, 1])
        k.zero = k.sb(ctx, "zero", [P, KD, 1])
        k.iota8 = k.sb(ctx, "iota8", [P, 8])
        k.rows = k.sb(ctx, "rows", [24, N])
        k.ps = ctx.enter_context(nc.psum_tensor("ps", [P, 4 * SLOT], F32))
        whole = dict(src=k.X, out=k.XN, slot=3)
        parts = dict(whole, split=True)
        block1 = {n[7:]: v for n, v in a.items() if n.startswith("L1_ffn_")}
        twice = dict(parts, again=True, scale=block1["norm1_w_columns"], shift=block1["norm1_b_columns"])
        with ExitStack() as first:
            k.XTF = k.sb(first, "XT_whole", [P, KD, N])
            setup(k, a["x"], a["src"], a["dst"], whole)
            l0_gnn(k, a["L0_gnn_W"], a["L0_gnn_attn_l"], a["L0_gnn_attn_r"], a["L0_gnn_W_res"], dict(parts, slot=0))
        plan = [
            moe_units(a["L0_ffn_w1"], a["L0_ffn_w2"]),
            node_units(a["L1_gnn_W"], 384, 2),
            qkv_units(block1["qkv_w"]),
            node_units(block1["proj_w"], 384, 2),
            moe_units(block1["W1"], block1["W2"]),
            node_units(a["L2_gnn_W1"], 384, 2) + node_units(a["L2_gnn_W2"], 384, 2),
        ]
        with ExitStack() as mem, k.sems("ring_loaded0 ring_loaded1 ring_loaded2 ring_loaded3") as loaded:
            k.ring = Ring(k, mem, loaded, plan)
            add_loops(k)
            moe(k, a["L0_ffn_router_w"], a["L0_ffn_w1"], a["L0_ffn_w2"], ACT.Gelu_apprx_tanh, "probs", dict(parts, slot=1))
            l1_gnn(k, a["L1_gnn_W"], a["L1_gnn_b"], twice)
            l1_ffn(k, block1, dict(parts, slot=1))
            l2_gnn(k, a["L2_gnn_W1"], a["L2_gnn_b1_columns"], a["L2_gnn_W2"], a["L2_gnn_b2"], parts)
            k.ring = None
        l2_ffn(k, a["L2_ffn_phi"], a["L2_ffn_w1"], a["L2_ffn_b1"], a["L2_ffn_w2"], a["L2_ffn_b2"],
               dict(parts, out=None))
        l3_gnn(k, a["L3_gnn_W1"], a["L3_gnn_a1_src"], a["L3_gnn_a1_dst"], a["L3_gnn_b1_columns"], a["L3_gnn_W2"],
               a["L3_gnn_a2_src"], a["L3_gnn_a2_dst"], a["L3_gnn_b2"], parts)
        moe(k, a["L3_ffn_router_w"], a["L3_ffn_up_w"], a["L3_ffn_down_w"], ACT.Gelu, "renormalised", None, out=out)


def layout(inputs):
    import numpy as np
    turned = {"L0_gnn_W", "L0_gnn_W_res", "L0_ffn_router_w", "L1_ffn_qkv_w", "L1_ffn_proj_w", "L3_ffn_router_w"}
    flat = {"L0_gnn_attn_l", "L0_gnn_attn_r", "L3_gnn_a1_src", "L3_gnn_a1_dst", "L3_gnn_a2_src", "L3_gnn_a2_dst"}
    columns = {"L1_ffn_norm1_w", "L1_ffn_norm1_b", "L1_ffn_norm2_w", "L1_ffn_norm2_b", "L1_ffn_qkv_b", "L1_ffn_b1",
               "L2_gnn_b1", "L3_gnn_b1"}
    arrays = {}
    for name, v in inputs.items():
        v = np.asarray(v)
        if name in turned:
            v = v.T
        if name in flat:
            v = v.reshape(-1)
        if name in columns:
            arrays[name + "_columns"] = np.ascontiguousarray(v.reshape(-1, P).T)
        if name == "L2_ffn_phi":
            v = v.reshape(-1, v.shape[-1]).T
        arrays[name] = np.ascontiguousarray(v)
    return arrays


def kernel(**inputs):
    import concourse.bacc as bacc
    from concourse.bass_utils import run_bass_kernel_spmd
    nc = bacc.Bacc("TRN2", target_bir_lowering=False, num_devices=1)
    arrays = layout(inputs)
    aps = {n: nc.dram_tensor("in_" + n, v.shape, mybir.dt.from_np(v.dtype), kind="ExternalInput").ap()
           for n, v in arrays.items()}
    out = nc.dram_tensor("out", (N, D), F32, kind="ExternalOutput").ap()
    build(nc, aps, out)
    r = run_bass_kernel_spmd(nc, [{"in_" + n: v for n, v in arrays.items()}], core_ids=[0])
    return r.results[0]["out"]
```
